# Optimizing a Trainium2 kernel written in Bass

```python
import numpy as np
import jax
import jax.numpy as jnp

def _softmax(x, axis=-1):
    return jax.nn.softmax(x, axis=axis)

def _gelu(x):
    return jax.nn.gelu(x, approximate=True)

def _silu(x):
    return jax.nn.silu(x)

def _sigmoid(x):
    return jax.nn.sigmoid(x)

def _layernorm(x, axis=-1, eps=1e-05):
    m = jnp.mean(x, axis=axis, keepdims=True)
    v = jnp.var(x, axis=axis, keepdims=True)
    return (x - m) / jnp.sqrt(v + eps)

def _scatter_add(tgt, idx, src, axis=0):
    return tgt.at[idx].add(src)

def _segment_sum(src, seg, n):
    return jax.ops.segment_sum(src, seg, n)
kernel_name = 'mk_lm_tower_d2_tok_ids256_r4_5b8ea6'

def setup_inputs(seed: int=0):
    np.random.seed(seed)
    _w = jnp.asarray

    def _rec_inputs():
        import jax
        import jax.numpy as jnp
        _rk = jax.random.key(seed)
        x = jax.random.randint(jax.random.fold_in(_rk, 1), (8, 256), 0, 7, jnp.int32)
        itok_BS_0_23 = jax.random.randint(jax.random.fold_in(_rk, 21), (8, 256), 0, 24, jnp.int32)
        itok_BS_0_11 = jax.random.randint(jax.random.fold_in(_rk, 22), (8, 256), 0, 12, jnp.int32)
        itok_BS_0_30 = jax.random.randint(jax.random.fold_in(_rk, 23), (8, 256), 0, 31, jnp.int32)
        return (x, itok_BS_0_23, itok_BS_0_11, itok_BS_0_30)
    x, itok_BS_0_23, itok_BS_0_11, itok_BS_0_30 = _rec_inputs()

    def _L0_tok_setup():
        import jax, jax.numpy as jnp
        import numpy as np
        import math
        B, S = (64, 512)
        HARM = 3
        N_PERIODS = 4
        FD = N_PERIODS * 2 * HARM
        TD = 64
        PERIODS = np.array([7.0, 24.0, 12.0, 1.0], dtype=np.float32)
        LN_EPS = 1e-05

        def _fourier_concat(dayofweek, hour, month, dayofmonth, hw, ph):
            t = jnp.stack([dayofweek, hour, month, dayofmonth]).astype(jnp.float32)
            periods = jnp.asarray(PERIODS)
            norm = 2.0 * math.pi * t / periods[:, None, None]
            h = jnp.arange(1, HARM + 1, dtype=jnp.float32)
            ang = norm[..., None] * h + ph[:, None, None, :]
            w = hw[:, None, None, :]
            f = jnp.stack([w * jnp.sin(ang), w * jnp.cos(ang)], axis=-1)
            return jnp.moveaxis(f, 0, 2).reshape(t.shape[1], t.shape[2], FD)
        key = jax.random.key(seed)
        ks = jax.random.split(key, 12)
        maxv = [7, 24, 12, 31]
        times = {n: jax.random.randint(ks[i], (B, S), 0, maxv[i], dtype=jnp.int32) for i, n in enumerate(['dayofweek', 'hour', 'month', 'dayofmonth'])}
        inp = dict(times)
        inp['hw'] = jax.random.uniform(ks[4], (N_PERIODS, HARM), dtype=jnp.float32) + 0.5
        inp['ph'] = jax.random.normal(ks[5], (N_PERIODS, HARM), dtype=jnp.float32) * 0.1
        inp['W1'] = jax.random.normal(ks[6], (FD, 2 * TD), dtype=jnp.float32) / math.sqrt(FD)
        inp['b1'] = jax.random.normal(ks[7], (2 * TD,), dtype=jnp.float32) * 0.01
        inp['W2'] = jax.random.normal(ks[8], (2 * TD, TD), dtype=jnp.float32) / math.sqrt(2 * TD)
        inp['b2'] = jax.random.normal(ks[9], (TD,), dtype=jnp.float32) * 0.01
        inp['gamma'] = jnp.ones((TD,), dtype=jnp.float32)
        inp['beta'] = jnp.zeros((TD,), dtype=jnp.float32)
        inp['Wres'] = jax.random.normal(ks[10], (FD, TD), dtype=jnp.float32) / math.sqrt(FD)
        inp['bres'] = jax.random.normal(ks[11], (TD,), dtype=jnp.float32) * 0.01
        return inp
    _L0_tok_all = _L0_tok_setup()
    _L0_tok_in = {k: v for k, v in _L0_tok_all.items() if k in ('hw', 'ph', 'W1', 'b1', 'W2', 'b2', 'gamma', 'beta', 'Wres', 'bres')}
    del _L0_tok_all

    def _L0_attn_setup():
        import jax, jax.numpy as jnp
        import numpy as np
        from jax import lax
        D_MODEL = 64
        D_FF = 256
        D_STATE = 16
        D_CONV = 4
        EXPAND = 2
        D_INNER = EXPAND * D_MODEL
        DT_RANK = (D_MODEL + 15) // 16
        BATCH, SEQ = (4, 512)
        EPS = 1e-05

        def _silu(x):
            return x * jax.nn.sigmoid(x)

        def _mamba(x, in_w, conv_w, conv_b, xproj_w, dt_w, dt_b, Alog, Dskip, out_w):
            B, L, _ = x.shape
            xz = jnp.einsum('bld,ed->ble', x, in_w)
            xi, z = jnp.split(xz, 2, axis=-1)
            xc = lax.conv_general_dilated(xi.transpose(0, 2, 1), conv_w[:, None, :], (1,), [(D_CONV - 1, 0)], dimension_numbers=('NCH', 'OIH', 'NCH'), feature_group_count=D_INNER)
            xi = _silu((xc + conv_b[None, :, None]).transpose(0, 2, 1))
            dbc = jnp.einsum('bld,ed->ble', xi, xproj_w)
            dt, Bm, Cm = jnp.split(dbc, [DT_RANK, DT_RANK + D_STATE], axis=-1)
            delta = jax.nn.softplus(jnp.einsum('blr,dr->bld', dt, dt_w) + dt_b)
            A = -jnp.exp(Alog)

            def step(h, inp):
                u_t, d_t, b_t, c_t = inp
                dA = jnp.exp(d_t[:, :, None] * A)
                h = dA * h + (d_t * u_t)[:, :, None] * b_t[:, None, :]
                y = jnp.einsum('bdn,bn->bd', h, c_t)
                return (h, y)
            h0 = jnp.zeros((B, D_INNER, D_STATE), x.dtype)
            xs = (xi.transpose(1, 0, 2), delta.transpose(1, 0, 2), Bm.transpose(1, 0, 2), Cm.transpose(1, 0, 2))
            _, ys = lax.scan(step, h0, xs)
            y = ys.transpose(1, 0, 2) + xi * Dskip
            y = y * _silu(z)
            return jnp.einsum('bld,ed->ble', y, out_w)

        def _bn(x, g, b, m, v):
            return (x - m) * lax.rsqrt(v + EPS) * g + b

        def _ln(x, g, b):
            mu = jnp.mean(x, -1, keepdims=True)
            var = jnp.var(x, -1, keepdims=True)
            return (x - mu) * lax.rsqrt(var + EPS) * g + b

        def _forward(x, mamba_in_w, mamba_conv_w, mamba_conv_b, mamba_xproj_w, mamba_dt_w, mamba_dt_b, mamba_Alog, mamba_D, mamba_out_w, bn_gamma, bn_beta, bn_mean, bn_var, ln_gamma, ln_beta, ff_w1, ff_b1, ff_w2, ff_b2):
            mp = (mamba_in_w, mamba_conv_w, mamba_conv_b, mamba_xproj_w, mamba_dt_w, mamba_dt_b, mamba_Alog, mamba_D, mamba_out_w)
            f = _mamba(x, *(p[0] for p in mp))
            f = _bn(f, bn_gamma[0], bn_beta[0], bn_mean[0], bn_var[0])
            bwd = _mamba(x[:, ::-1], *(p[1] for p in mp))
            bwd = _bn(bwd, bn_gamma[1], bn_beta[1], bn_mean[1], bn_var[1])[:, ::-1]
            f = _ln(x + f, ln_gamma[0], ln_beta[0])
            bwd = _ln(x + bwd, ln_gamma[1], ln_beta[1])
            out = f + bwd
            out = jnp.maximum(out @ ff_w1.T + ff_b1, 0.0) @ ff_w2.T + ff_b2
            out = _bn(out, bn_gamma[2], bn_beta[2], bn_mean[2], bn_var[2])
            return out + x
        key = jax.random.key(seed)
        ks = jax.random.split(key, 16)
        r = lambda k, s, sc=0.02: sc * jax.random.normal(k, s, dtype=jnp.float32)
        inp = {}
        inp['x'] = jax.random.normal(ks[0], (BATCH, SEQ, D_MODEL), dtype=jnp.float32)
        inp['mamba_in_w'] = r(ks[1], (2, 2 * D_INNER, D_MODEL))
        inp['mamba_conv_w'] = r(ks[2], (2, D_INNER, D_CONV), 0.1)
        inp['mamba_conv_b'] = r(ks[3], (2, D_INNER))
        inp['mamba_xproj_w'] = r(ks[4], (2, DT_RANK + 2 * D_STATE, D_INNER))
        inp['mamba_dt_w'] = r(ks[5], (2, D_INNER, DT_RANK), 0.1)
        inp['mamba_dt_b'] = r(ks[6], (2, D_INNER))
        inp['mamba_Alog'] = jnp.broadcast_to(jnp.log(jnp.arange(1, D_STATE + 1, dtype=jnp.float32)), (2, D_INNER, D_STATE))
        inp['mamba_D'] = jnp.ones((2, D_INNER), jnp.float32)
        inp['mamba_out_w'] = r(ks[7], (2, D_MODEL, D_INNER))
        inp['bn_gamma'] = 1.0 + r(ks[8], (3, D_MODEL), 0.05)
        inp['bn_beta'] = r(ks[9], (3, D_MODEL), 0.05)
        inp['bn_mean'] = jnp.zeros((3, D_MODEL), jnp.float32)
        inp['bn_var'] = jnp.ones((3, D_MODEL), jnp.float32)
        inp['ln_gamma'] = jnp.ones((3, D_MODEL), jnp.float32)
        inp['ln_beta'] = jnp.zeros((3, D_MODEL), jnp.float32)
        inp['ff_w1'] = r(ks[10], (D_FF, D_MODEL))
        inp['ff_b1'] = r(ks[11], (D_FF,))
        inp['ff_w2'] = r(ks[12], (D_MODEL, D_FF))
        inp['ff_b2'] = r(ks[13], (D_MODEL,))
        return inp
    _L0_attn_all = _L0_attn_setup()
    _L0_attn_in = {k: v for k, v in _L0_attn_all.items() if k in ('mamba_in_w', 'mamba_conv_w', 'mamba_conv_b', 'mamba_xproj_w', 'mamba_dt_w', 'mamba_dt_b', 'mamba_Alog', 'mamba_D', 'mamba_out_w', 'bn_gamma', 'bn_beta', 'bn_mean', 'bn_var', 'ln_gamma', 'ln_beta', 'ff_w1', 'ff_b1', 'ff_w2', 'ff_b2')}
    del _L0_attn_all

    def _L0_ffn_setup():
        import jax, jax.numpy as jnp
        import numpy as np
        TOP_K = 2
        LN_EPS = 1e-05
        key = jax.random.key(seed)
        ks = jax.random.split(key, 8)
        B, S, D, E, H = (16, 256, 64, 8, 256)
        x = jax.random.normal(ks[0], (B, S, D), dtype=jnp.float32)
        Wr = jax.random.normal(ks[1], (D, E), dtype=jnp.float32) * 0.1
        br = jnp.zeros((E,), dtype=jnp.float32)
        ln_g = jnp.ones((E, D), dtype=jnp.float32)
        ln_b = jnp.zeros((E, D), dtype=jnp.float32)
        W1 = jax.random.normal(ks[2], (E, D, H), dtype=jnp.float32) * (1.0 / np.sqrt(D))
        b1 = jnp.zeros((E, H), dtype=jnp.float32)
        W2 = jax.random.normal(ks[3], (E, H, D), dtype=jnp.float32) * (1.0 / np.sqrt(H))
        b2 = jnp.zeros((E, D), dtype=jnp.float32)
        return {'x': x, 'Wr': Wr, 'br': br, 'ln_g': ln_g, 'ln_b': ln_b, 'W1': W1, 'b1': b1, 'W2': W2, 'b2': b2}
    _L0_ffn_all = _L0_ffn_setup()
    _L0_ffn_in = {k: v for k, v in _L0_ffn_all.items() if k in ('Wr', 'br', 'ln_g', 'ln_b', 'W1', 'b1', 'W2', 'b2')}
    del _L0_ffn_all

    def _L1_attn_setup():
        import math
        import jax, jax.numpy as jnp
        import numpy as np
        D_MODEL = 64
        N_HEADS = 4
        HEAD_DIM = D_MODEL // N_HEADS
        MAX_REL = 30

        def _rel_pos_encodings(t, d_model):
            n = 2 * MAX_REL + 1
            positions = jnp.arange(n, dtype=jnp.float32)[:, None]
            div_term = jnp.exp(jnp.arange(0, d_model, 2, dtype=jnp.float32) * (-math.log(10000.0) / d_model))
            ang = positions * div_term
            enc = jnp.stack([jnp.sin(ang), jnp.cos(ang)], axis=-1).reshape(n, d_model)
            rng = jnp.arange(t)
            final_mat = jnp.clip(rng[None, :] - rng[:, None], -MAX_REL, MAX_REL) + MAX_REL
            return enc[final_mat]
        key = jax.random.key(seed)
        ks = jax.random.split(key, 12)
        d = D_MODEL
        s = 1.0 / math.sqrt(d)
        inp = {'inputs': jax.random.normal(ks[0], (16, 128, d), dtype=jnp.float32), 'ln_gamma': jnp.ones((d,), jnp.float32), 'ln_beta': jnp.zeros((d,), jnp.float32), 'Wq': jax.random.normal(ks[1], (d, d), jnp.float32) * s, 'bq': jnp.zeros((d,), jnp.float32), 'Wk': jax.random.normal(ks[2], (d, d), jnp.float32) * s, 'bk': jnp.zeros((d,), jnp.float32), 'Wv': jax.random.normal(ks[3], (d, d), jnp.float32) * s, 'bv': jnp.zeros((d,), jnp.float32), 'Wpos': jax.random.normal(ks[4], (d, d), jnp.float32) * s, 'bpos': jnp.zeros((d,), jnp.float32), 'Wo': jax.random.normal(ks[5], (d, d), jnp.float32) * s, 'bo': jnp.zeros((d,), jnp.float32), 'u_bias': jax.random.normal(ks[6], (1, N_HEADS, 1, HEAD_DIM), jnp.float32) * 0.02, 'v_bias': jax.random.normal(ks[7], (1, N_HEADS, 1, HEAD_DIM), jnp.float32) * 0.02}
        return inp
    _L1_attn_all = _L1_attn_setup()
    _L1_attn_in = {k: v for k, v in _L1_attn_all.items() if k in ('ln_gamma', 'ln_beta', 'Wq', 'bq', 'Wk', 'bk', 'Wv', 'bv', 'Wpos', 'bpos', 'Wo', 'bo', 'u_bias', 'v_bias')}
    del _L1_attn_all

    def _L1_ffn_setup():
        import jax, jax.numpy as jnp
        import numpy as np
        B, S, D, E, H, K = (4, 1024, 64, 8, 128, 2)
        key = jax.random.key(seed)
        ks = jax.random.split(key, 6)
        x = jax.random.normal(ks[0], (B, S, D), jnp.float32)
        Wg = jax.random.normal(ks[1], (D, E), jnp.float32) * 0.02
        bg = jnp.zeros((E,), jnp.float32)
        W1 = jax.random.normal(ks[2], (E, D, H), jnp.float32) * 0.02
        b1 = jnp.zeros((E, H), jnp.float32)
        W2 = jax.random.normal(ks[3], (E, H, D), jnp.float32) * 0.02
        b2 = jnp.zeros((E, D), jnp.float32)
        return {'x': x, 'Wg': Wg, 'bg': bg, 'W1': W1, 'b1': b1, 'W2': W2, 'b2': b2}
    _L1_ffn_all = _L1_ffn_setup()
    _L1_ffn_in = {k: v for k, v in _L1_ffn_all.items() if k in ('Wg', 'bg', 'W1', 'b1', 'W2', 'b2')}
    del _L1_ffn_all
    return {'x': x, 'itok_BS_0_23': itok_BS_0_23, 'itok_BS_0_11': itok_BS_0_11, 'itok_BS_0_30': itok_BS_0_30, 'L0_tok_hw': _L0_tok_in['hw'], 'L0_tok_ph': _L0_tok_in['ph'], 'L0_tok_W1': _L0_tok_in['W1'], 'L0_tok_b1': _L0_tok_in['b1'], 'L0_tok_W2': _L0_tok_in['W2'], 'L0_tok_b2': _L0_tok_in['b2'], 'L0_tok_gamma': _L0_tok_in['gamma'], 'L0_tok_beta': _L0_tok_in['beta'], 'L0_tok_Wres': _L0_tok_in['Wres'], 'L0_tok_bres': _L0_tok_in['bres'], 'L0_attn_mamba_in_w': _L0_attn_in['mamba_in_w'], 'L0_attn_mamba_conv_w': _L0_attn_in['mamba_conv_w'], 'L0_attn_mamba_conv_b': _L0_attn_in['mamba_conv_b'], 'L0_attn_mamba_xproj_w': _L0_attn_in['mamba_xproj_w'], 'L0_attn_mamba_dt_w': _L0_attn_in['mamba_dt_w'], 'L0_attn_mamba_dt_b': _L0_attn_in['mamba_dt_b'], 'L0_attn_mamba_Alog': _L0_attn_in['mamba_Alog'], 'L0_attn_mamba_D': _L0_attn_in['mamba_D'], 'L0_attn_mamba_out_w': _L0_attn_in['mamba_out_w'], 'L0_attn_bn_gamma': _L0_attn_in['bn_gamma'], 'L0_attn_bn_beta': _L0_attn_in['bn_beta'], 'L0_attn_bn_mean': _L0_attn_in['bn_mean'], 'L0_attn_bn_var': _L0_attn_in['bn_var'], 'L0_attn_ln_gamma': _L0_attn_in['ln_gamma'], 'L0_attn_ln_beta': _L0_attn_in['ln_beta'], 'L0_attn_ff_w1': _L0_attn_in['ff_w1'], 'L0_attn_ff_b1': _L0_attn_in['ff_b1'], 'L0_attn_ff_w2': _L0_attn_in['ff_w2'], 'L0_attn_ff_b2': _L0_attn_in['ff_b2'], 'L0_ffn_Wr': _L0_ffn_in['Wr'], 'L0_ffn_br': _L0_ffn_in['br'], 'L0_ffn_ln_g': _L0_ffn_in['ln_g'], 'L0_ffn_ln_b': _L0_ffn_in['ln_b'], 'L0_ffn_W1': _L0_ffn_in['W1'], 'L0_ffn_b1': _L0_ffn_in['b1'], 'L0_ffn_W2': _L0_ffn_in['W2'], 'L0_ffn_b2': _L0_ffn_in['b2'], 'L1_attn_ln_gamma': _L1_attn_in['ln_gamma'], 'L1_attn_ln_beta': _L1_attn_in['ln_beta'], 'L1_attn_Wq': _L1_attn_in['Wq'], 'L1_attn_bq': _L1_attn_in['bq'], 'L1_attn_Wk': _L1_attn_in['Wk'], 'L1_attn_bk': _L1_attn_in['bk'], 'L1_attn_Wv': _L1_attn_in['Wv'], 'L1_attn_bv': _L1_attn_in['bv'], 'L1_attn_Wpos': _L1_attn_in['Wpos'], 'L1_attn_bpos': _L1_attn_in['bpos'], 'L1_attn_Wo': _L1_attn_in['Wo'], 'L1_attn_bo': _L1_attn_in['bo'], 'L1_attn_u_bias': _L1_attn_in['u_bias'], 'L1_attn_v_bias': _L1_attn_in['v_bias'], 'L1_ffn_Wg': _L1_ffn_in['Wg'], 'L1_ffn_bg': _L1_ffn_in['bg'], 'L1_ffn_W1': _L1_ffn_in['W1'], 'L1_ffn_b1': _L1_ffn_in['b1'], 'L1_ffn_W2': _L1_ffn_in['W2'], 'L1_ffn_b2': _L1_ffn_in['b2']}

def reference(x, itok_BS_0_23, itok_BS_0_11, itok_BS_0_30, L0_tok_hw, L0_tok_ph, L0_tok_W1, L0_tok_b1, L0_tok_W2, L0_tok_b2, L0_tok_gamma, L0_tok_beta, L0_tok_Wres, L0_tok_bres, L0_attn_mamba_in_w, L0_attn_mamba_conv_w, L0_attn_mamba_conv_b, L0_attn_mamba_xproj_w, L0_attn_mamba_dt_w, L0_attn_mamba_dt_b, L0_attn_mamba_Alog, L0_attn_mamba_D, L0_attn_mamba_out_w, L0_attn_bn_gamma, L0_attn_bn_beta, L0_attn_bn_mean, L0_attn_bn_var, L0_attn_ln_gamma, L0_attn_ln_beta, L0_attn_ff_w1, L0_attn_ff_b1, L0_attn_ff_w2, L0_attn_ff_b2, L0_ffn_Wr, L0_ffn_br, L0_ffn_ln_g, L0_ffn_ln_b, L0_ffn_W1, L0_ffn_b1, L0_ffn_W2, L0_ffn_b2, L1_attn_ln_gamma, L1_attn_ln_beta, L1_attn_Wq, L1_attn_bq, L1_attn_Wk, L1_attn_bk, L1_attn_Wv, L1_attn_bv, L1_attn_Wpos, L1_attn_bpos, L1_attn_Wo, L1_attn_bo, L1_attn_u_bias, L1_attn_v_bias, L1_ffn_Wg, L1_ffn_bg, L1_ffn_W1, L1_ffn_b1, L1_ffn_W2, L1_ffn_b2):
    import jax
    import jax.numpy as jnp

    def _L0_tok_ref(dayofweek, hour, month, dayofmonth, hw, ph, W1, b1, W2, b2, gamma, beta, Wres, bres):
        import jax, jax.numpy as jnp
        import numpy as np
        import math
        B, S = (64, 512)
        HARM = 3
        N_PERIODS = 4
        FD = N_PERIODS * 2 * HARM
        TD = 64
        PERIODS = np.array([7.0, 24.0, 12.0, 1.0], dtype=np.float32)
        LN_EPS = 1e-05

        def _fourier_concat(dayofweek, hour, month, dayofmonth, hw, ph):
            t = jnp.stack([dayofweek, hour, month, dayofmonth]).astype(jnp.float32)
            periods = jnp.asarray(PERIODS)
            norm = 2.0 * math.pi * t / periods[:, None, None]
            h = jnp.arange(1, HARM + 1, dtype=jnp.float32)
            ang = norm[..., None] * h + ph[:, None, None, :]
            w = hw[:, None, None, :]
            f = jnp.stack([w * jnp.sin(ang), w * jnp.cos(ang)], axis=-1)
            return jnp.moveaxis(f, 0, 2).reshape(t.shape[1], t.shape[2], FD)
        x = _fourier_concat(dayofweek, hour, month, dayofmonth, hw, ph)
        h1 = jax.nn.relu(jnp.einsum('bsf,fd->bsd', x, W1) + b1)
        h2 = jnp.einsum('bsd,dt->bst', h1, W2) + b2
        mu = jnp.mean(h2, axis=-1, keepdims=True)
        var = jnp.mean(jnp.square(h2 - mu), axis=-1, keepdims=True)
        ln = (h2 - mu) * jax.lax.rsqrt(var + LN_EPS) * gamma + beta
        residual = jnp.einsum('bsf,ft->bst', x, Wres) + bres
        return ln + 0.1 * residual

    def _L0_attn_ref(x, mamba_in_w, mamba_conv_w, mamba_conv_b, mamba_xproj_w, mamba_dt_w, mamba_dt_b, mamba_Alog, mamba_D, mamba_out_w, bn_gamma, bn_beta, bn_mean, bn_var, ln_gamma, ln_beta, ff_w1, ff_b1, ff_w2, ff_b2):
        import jax, jax.numpy as jnp
        import numpy as np
        from jax import lax
        D_MODEL = 64
        D_FF = 256
        D_STATE = 16
        D_CONV = 4
        EXPAND = 2
        D_INNER = EXPAND * D_MODEL
        DT_RANK = (D_MODEL + 15) // 16
        BATCH, SEQ = (4, 512)
        EPS = 1e-05

        def _silu(x):
            return x * jax.nn.sigmoid(x)

        def _mamba(x, in_w, conv_w, conv_b, xproj_w, dt_w, dt_b, Alog, Dskip, out_w):
            B, L, _ = x.shape
            xz = jnp.einsum('bld,ed->ble', x, in_w)
            xi, z = jnp.split(xz, 2, axis=-1)
            xc = lax.conv_general_dilated(xi.transpose(0, 2, 1), conv_w[:, None, :], (1,), [(D_CONV - 1, 0)], dimension_numbers=('NCH', 'OIH', 'NCH'), feature_group_count=D_INNER)
            xi = _silu((xc + conv_b[None, :, None]).transpose(0, 2, 1))
            dbc = jnp.einsum('bld,ed->ble', xi, xproj_w)
            dt, Bm, Cm = jnp.split(dbc, [DT_RANK, DT_RANK + D_STATE], axis=-1)
            delta = jax.nn.softplus(jnp.einsum('blr,dr->bld', dt, dt_w) + dt_b)
            A = -jnp.exp(Alog)

            def step(h, inp):
                u_t, d_t, b_t, c_t = inp
                dA = jnp.exp(d_t[:, :, None] * A)
                h = dA * h + (d_t * u_t)[:, :, None] * b_t[:, None, :]
                y = jnp.einsum('bdn,bn->bd', h, c_t)
                return (h, y)
            h0 = jnp.zeros((B, D_INNER, D_STATE), x.dtype)
            xs = (xi.transpose(1, 0, 2), delta.transpose(1, 0, 2), Bm.transpose(1, 0, 2), Cm.transpose(1, 0, 2))
            _, ys = lax.scan(step, h0, xs)
            y = ys.transpose(1, 0, 2) + xi * Dskip
            y = y * _silu(z)
            return jnp.einsum('bld,ed->ble', y, out_w)

        def _bn(x, g, b, m, v):
            return (x - m) * lax.rsqrt(v + EPS) * g + b

        def _ln(x, g, b):
            mu = jnp.mean(x, -1, keepdims=True)
            var = jnp.var(x, -1, keepdims=True)
            return (x - mu) * lax.rsqrt(var + EPS) * g + b

        def _forward(x, mamba_in_w, mamba_conv_w, mamba_conv_b, mamba_xproj_w, mamba_dt_w, mamba_dt_b, mamba_Alog, mamba_D, mamba_out_w, bn_gamma, bn_beta, bn_mean, bn_var, ln_gamma, ln_beta, ff_w1, ff_b1, ff_w2, ff_b2):
            mp = (mamba_in_w, mamba_conv_w, mamba_conv_b, mamba_xproj_w, mamba_dt_w, mamba_dt_b, mamba_Alog, mamba_D, mamba_out_w)
            f = _mamba(x, *(p[0] for p in mp))
            f = _bn(f, bn_gamma[0], bn_beta[0], bn_mean[0], bn_var[0])
            bwd = _mamba(x[:, ::-1], *(p[1] for p in mp))
            bwd = _bn(bwd, bn_gamma[1], bn_beta[1], bn_mean[1], bn_var[1])[:, ::-1]
            f = _ln(x + f, ln_gamma[0], ln_beta[0])
            bwd = _ln(x + bwd, ln_gamma[1], ln_beta[1])
            out = f + bwd
            out = jnp.maximum(out @ ff_w1.T + ff_b1, 0.0) @ ff_w2.T + ff_b2
            out = _bn(out, bn_gamma[2], bn_beta[2], bn_mean[2], bn_var[2])
            return out + x
        return _forward(x, mamba_in_w, mamba_conv_w, mamba_conv_b, mamba_xproj_w, mamba_dt_w, mamba_dt_b, mamba_Alog, mamba_D, mamba_out_w, bn_gamma, bn_beta, bn_mean, bn_var, ln_gamma, ln_beta, ff_w1, ff_b1, ff_w2, ff_b2)

    def _L0_ffn_ref(x, Wr, br, ln_g, ln_b, W1, b1, W2, b2):
        import jax, jax.numpy as jnp
        import numpy as np
        TOP_K = 2
        LN_EPS = 1e-05
        B, S, D = x.shape
        N = B * S
        xt = x.reshape(N, D)
        logits = xt @ Wr + br
        probs = jax.nn.softmax(logits, axis=-1)
        top_p, top_idx = jax.lax.top_k(probs, TOP_K)
        weights = top_p / top_p.sum(axis=-1, keepdims=True)
        mu = xt.mean(axis=-1, keepdims=True)
        var = ((xt - mu) ** 2).mean(axis=-1, keepdims=True)
        xn = (xt - mu) * jax.lax.rsqrt(var + LN_EPS)
        xe = xn[None, :, :] * ln_g[:, None, :] + ln_b[:, None, :]
        h = jax.nn.gelu(jnp.einsum('end,edh->enh', xe, W1) + b1[:, None, :], approximate=False)
        y = jnp.einsum('enh,ehd->end', h, W2) + b2[:, None, :]
        y_tok = jnp.transpose(y, (1, 0, 2))
        sel = jnp.take_along_axis(y_tok, top_idx[:, :, None], axis=1)
        out = (weights[:, :, None] * sel).sum(axis=1)
        return out.reshape(B, S, D)

    def _L1_attn_ref(inputs, ln_gamma, ln_beta, Wq, bq, Wk, bk, Wv, bv, Wpos, bpos, Wo, bo, u_bias, v_bias):
        import math
        import jax, jax.numpy as jnp
        import numpy as np
        D_MODEL = 64
        N_HEADS = 4
        HEAD_DIM = D_MODEL // N_HEADS
        MAX_REL = 30

        def _rel_pos_encodings(t, d_model):
            n = 2 * MAX_REL + 1
            positions = jnp.arange(n, dtype=jnp.float32)[:, None]
            div_term = jnp.exp(jnp.arange(0, d_model, 2, dtype=jnp.float32) * (-math.log(10000.0) / d_model))
            ang = positions * div_term
            enc = jnp.stack([jnp.sin(ang), jnp.cos(ang)], axis=-1).reshape(n, d_model)
            rng = jnp.arange(t)
            final_mat = jnp.clip(rng[None, :] - rng[:, None], -MAX_REL, MAX_REL) + MAX_REL
            return enc[final_mat]
        b, t, d = inputs.shape
        h, hd = (N_HEADS, HEAD_DIM)
        mu = jnp.mean(inputs, axis=-1, keepdims=True)
        var = jnp.mean(jnp.square(inputs - mu), axis=-1, keepdims=True)
        x = (inputs - mu) * jax.lax.rsqrt(var + 1e-05) * ln_gamma + ln_beta

        def split_heads(y):
            return y.reshape(b, t, h, hd).transpose(0, 2, 1, 3)
        q = split_heads(x @ Wq.T + bq)
        k = split_heads(x @ Wk.T + bk)
        v = split_heads(x @ Wv.T + bv)
        rel = jax.lax.stop_gradient(_rel_pos_encodings(t, d))
        pos = (rel @ Wpos.T + bpos).reshape(t, t, h, hd)
        qk_score = jnp.einsum('bhtd,bhsd->bhts', q + u_bias, k)
        pos_score = jnp.einsum('bhtd,tshd->bhts', q + v_bias, pos)
        scores = (qk_score + pos_score) / math.sqrt(hd)
        attn = jax.nn.softmax(scores, axis=-1)
        ctx = jnp.einsum('bhts,bhsd->bhtd', attn, v)
        ctx = ctx.transpose(0, 2, 1, 3).reshape(b, t, d)
        return ctx @ Wo.T + bo

    def _L1_ffn_ref(x, Wg, bg, W1, b1, W2, b2):
        import jax, jax.numpy as jnp
        import numpy as np
        B, S, D, E, H, K = (4, 1024, 64, 8, 128, 2)
        Bv, Sv, Dv = x.shape
        gate_scores = x @ Wg + bg
        _, idx = jax.lax.top_k(gate_scores, K)
        mask = jax.nn.one_hot(idx, E, dtype=x.dtype).sum(axis=-2)
        xf = x.reshape(-1, Dv)
        mf = mask.reshape(-1, E)
        h = jax.nn.gelu(jnp.einsum('td,edh->teh', xf, W1) + b1[None], approximate=False)
        y = jnp.einsum('teh,ehd->ted', h, W2) + b2[None]
        out = jnp.einsum('ted,te->td', y, mf)
        return out.reshape(Bv, Sv, Dv)
    h = _L0_tok_ref(x, itok_BS_0_23, itok_BS_0_11, itok_BS_0_30, L0_tok_hw, L0_tok_ph, L0_tok_W1, L0_tok_b1, L0_tok_W2, L0_tok_b2, L0_tok_gamma, L0_tok_beta, L0_tok_Wres, L0_tok_bres)
    h = h + _L0_attn_ref(_layernorm(h, axis=-1), L0_attn_mamba_in_w, L0_attn_mamba_conv_w, L0_attn_mamba_conv_b, L0_attn_mamba_xproj_w, L0_attn_mamba_dt_w, L0_attn_mamba_dt_b, L0_attn_mamba_Alog, L0_attn_mamba_D, L0_attn_mamba_out_w, L0_attn_bn_gamma, L0_attn_bn_beta, L0_attn_bn_mean, L0_attn_bn_var, L0_attn_ln_gamma, L0_attn_ln_beta, L0_attn_ff_w1, L0_attn_ff_b1, L0_attn_ff_w2, L0_attn_ff_b2)
    h = h + _L0_ffn_ref(_layernorm(h, axis=-1), L0_ffn_Wr, L0_ffn_br, L0_ffn_ln_g, L0_ffn_ln_b, L0_ffn_W1, L0_ffn_b1, L0_ffn_W2, L0_ffn_b2)
    h = h + _L1_attn_ref(_layernorm(h, axis=-1), L1_attn_ln_gamma, L1_attn_ln_beta, L1_attn_Wq, L1_attn_bq, L1_attn_Wk, L1_attn_bk, L1_attn_Wv, L1_attn_bv, L1_attn_Wpos, L1_attn_bpos, L1_attn_Wo, L1_attn_bo, L1_attn_u_bias, L1_attn_v_bias)
    h = h + _L1_ffn_ref(_layernorm(h, axis=-1), L1_ffn_Wg, L1_ffn_bg, L1_ffn_W1, L1_ffn_b1, L1_ffn_W2, L1_ffn_b2)
    return h

_drawn_inputs = setup_inputs


def setup_inputs(seed=0):
    import zlib

    import numpy as np

    out = dict(_drawn_inputs(seed))
    spreads = {'L0_tok_gamma': (1.0, 0.2),
     'L0_tok_beta': (0.0, 0.1),
     'L0_attn_mamba_D': (1.0, 0.6),
     'L0_attn_bn_mean': (0.0, 0.1),
     'L0_attn_bn_var': (1.0, 0.6),
     'L0_attn_ln_gamma': (1.0, 0.6),
     'L0_attn_ln_beta': (0.0, 0.717),
     'L0_ffn_br': (0.0, 0.1),
     'L0_ffn_ln_g': (1.0, 0.2),
     'L0_ffn_ln_b': (0.0, 0.334),
     'L0_ffn_b1': (0.0, 0.353),
     'L0_ffn_b2': (0.0, 0.1),
     'L1_attn_ln_gamma': (1.0, 0.2),
     'L1_attn_ln_beta': (0.0, 0.1),
     'L1_attn_bq': (0.0, 0.8),
     'L1_attn_bk': (0.0, 0.8),
     'L1_attn_bv': (0.0, 0.1),
     'L1_attn_bpos': (0.0, 0.8),
     'L1_attn_bo': (0.0, 0.1),
     'L1_ffn_bg': (0.0, 0.1),
     'L1_ffn_b1': (0.0, 0.8),
     'L1_ffn_b2': (0.0, 0.1)}
    factors = {'L0_tok_bres': 8.0,
     'L0_attn_mamba_in_w': 8.0,
     'L0_attn_mamba_conv_w': 8.0,
     'L0_attn_mamba_conv_b': 8.0,
     'L0_attn_mamba_xproj_w': 8.0,
     'L0_attn_mamba_dt_w': 8.0,
     'L0_attn_mamba_dt_b': 8.0,
     'L0_attn_mamba_Alog': 8.0,
     'L0_attn_mamba_out_w': 8.0,
     'L0_attn_bn_gamma': 8.0,
     'L0_attn_ff_b1': 5.579,
     'L1_attn_Wpos': 4.951,
     'L1_attn_u_bias': 8.0,
     'L1_attn_v_bias': 8.0,
     'L1_ffn_W1': 5.147,
     'L1_ffn_W2': 4.467}
    for name, (base, spread) in spreads.items():
        noise = np.random.default_rng([zlib.crc32(name.encode()), seed]).standard_normal(out[name].shape)
        drawn = base * np.exp(spread * noise) if base else spread * noise
        out[name] = jnp.asarray(drawn.astype(out[name].dtype))
    for name, factor in factors.items():
        out[name] = (out[name] * factor).astype(out[name].dtype)
    return out
```

```python
import math
from contextlib import ExitStack

import numpy as np
import concourse.bass as bass
from concourse import mybir

F32 = mybir.dt.float32
BF16 = mybir.dt.bfloat16
I32 = mybir.dt.int32
ALU = mybir.AluOpType
ACT = mybir.ActivationFunctionType
AX = mybir.AxisListType

D, S, NSEQ = 64, 256, 8
GSEQ = 2
T = GSEQ * S
NG = NSEQ // GSEQ
P = 128
TILES = T // P
HARM, PERIODS = 3, (7.0, 24.0, 12.0, 1.0)
FD = len(PERIODS) * 2 * HARM
TAPS, NSTATE, RANK = 4, 16, 4
PADW = S + 2 * (TAPS - 1)
NE, CH0 = 8, 2
NH, HD, MAXREL = 4, 16, 30
SKEW = P + S - 1
EPS = 1e-5
TWO_PI = 2.0 * math.pi
TURN = (6.28125, 0.0019350051879882812, 3.0199159819574e-07)
ROUND = 12582912.0
PI_LO = 3.1415925
RING = 4

PACKED = [
    [("invp", 1), ("harm", 1), ("phase", 1), ("quarter", 1), ("halfpi", 1), ("amp", 1), ("tok_b1", 1),
     ("tok_b2", 1), ("tok_g", 1), ("tok_b", 1), ("tok_bres", 1), ("tok_w1", P), ("tok_w2", P), ("tok_wres", P),
     ("center", P), ("mean", P)],
    [("ident", P), ("mean2", P), ("center2", P), ("centerd", P), ("centers", D),
     ("inx", 2 * D), ("conv_w", 2 * TAPS), ("conv_b", 2), ("inz", 2 * P), ("bc_w", 2 * P), ("xp_dt", 2 * P),
     ("dt_w", 2 * P), ("dt_b", 2), ("alog", 2 * NSTATE), ("dskip", 2), ("out_w", P), ("bn_g", 1), ("bn_b", 1),
     ("bn_m", 1), ("bn_v", 1), ("bn2_g", 1), ("bn2_b", 1), ("bn2_m", 1), ("bn2_v", 1), ("ln_g", 1), ("ln_b", 1),
     ("ff_w1", 2 * P), ("ff_b1", 2), ("ff_w2", 2 * P), ("ff_b2", 1)],
    [("tri", NE * NE), ("e0_w1", NE * P), ("e0_g", NE), ("e0_lb", NE), ("e0_b1", NE * CH0),
     ("e0_w2", NE * CH0 * D), ("e0_b2", P), ("e0_wr", NE), ("e0_br", NE),
     ("at_g", 1), ("at_b", 1), ("at_wq", P), ("at_wk", P), ("at_wp", P), ("at_bq", 1), ("at_bk", 1), ("at_bp", 1),
     ("at_u", 1), ("at_v", 1), ("at_wv", D), ("at_wo", P), ("at_bv", 1), ("at_bo", 1), ("enc", 2 * S - 1),
     ("e1_w1", NE // 2 * P), ("e1_b1", NE), ("e1_w2", NE * D), ("e1_b2", D), ("e1_wg", NE), ("e1_bg", NE)],
]
WIDTHS = [sum(n for _, n in part) for part in PACKED]


def places():
    out = {}
    for k, part in enumerate(PACKED):
        at = 0
        for name, n in part:
            out[name] = (k, at, n)
            at += n
    return out


class Signal:

    def __init__(self, sem, steps):
        self.sem, self.steps = sem, steps

    def __call__(self, i, step):
        n = step if isinstance(step, int) else self.steps.index(step) + 1
        return self.sem, i * len(self.steps) + n

    def before(self, i):
        return self.sem, i * len(self.steps)


def tower(nc, idx, w0, w1, w2, sel_in, out):
    where = places()
    ctx = ExitStack()
    with ctx:
        def sb(name, shape, dt=F32):
            return ctx.enter_context(nc.sbuf_tensor(name, shape, dt))

        def signal(name, steps):
            return Signal(ctx.enter_context(nc.semaphore(name)), steps)

        bank = [ctx.enter_context(nc.psum_tensor(f"bank{b}", [P, T], F32)) for b in range(8)]
        packed = [sb(f"packed{k}", [P, n]) for k, n in enumerate(WIDTHS)]

        def W(name, rows=slice(0, P)):
            k, at, n = where[name]
            return packed[k][rows, at:at + n]

        h_all = sb("h_all", [P, NG * T])
        sel = sb("sel", [P, 2 * NSTATE], BF16)

        conv_w = sb("conv_w", [P, 4, P])
        eps_c = sb("eps_c", [P, 2])
        tok_bias = sb("tok_bias", [P, 1])
        bn2_d = sb("bn2_d", [P, 1])
        eps1, eps2 = eps_c[:, 0:1], eps_c[:, 1:2]
        delta_w = sb("delta_w", [P, 2, P])
        skip_w = sb("skip_w", [P, 2, P])
        a_neg = sb("a_neg", [P, 2 * NSTATE])
        bn_s, bn_t, bn2_s, bn2_t = (sb(n, [P, 1]) for n in ("bn_s", "bn_t", "bn2_s", "bn2_t"))
        out_s = sb("out_s", [P, P])
        out_w = sb("out_w", [P, 2, D])
        cen_t = sb("cen_t", [P, 1])
        ff_w1 = sb("ff_w1", [P, 2 * P])
        ff_b1 = sb("ff_b1", [P, 2])
        e0_w1 = W("e0_w1").rearrange("p (e n) -> p e n", e=NE)
        e0_b1 = sb("e0_b1", [P, NE * CH0])
        pos = sb("pos", [P, 2 * S - 1])
        bq_u, bq_v, bo_v = sb("bq_u", [P, 1]), sb("bq_v", [P, 1]), sb("bo_v", [P, 1])

        h0 = sb("h0", [P, T])
        sq, rs, rs2 = sb("sq", [P, T]), sb("rs", [P, T]), sb("rs2", [P, T])
        conv_s = sq[:, :].rearrange("p (q n) -> p q n", q=4)
        xf = sb("xf", [P, T])
        xpad = sb("xpad", [P, GSEQ, PADW])
        hx = sb("hx", [P, T])
        u = [sb(f"u{d}", [P, T]) for d in range(2)]
        z = [sb(f"z{d}", [P, T]) for d in range(2)]
        bc = [sb(f"bc{d}", [P, T], BF16) for d in range(2)]
        rest = sb("rest", [P, T])
        ab, soft = sb("ab", [P, T]), sb("soft", [P, T])
        delta = [sb(f"delta{d}", [P, T]) for d in range(2)]
        du = [sb(f"du{d}", [P, T]) for d in range(2)]
        decay = [[sb(f"decay{d}_{r}", [P, T]) for r in range(RING)] for d in range(2)]
        drive = [sb(f"drive{r}", [P, T]) for r in range(2)]
        state = [sb(f"state{r}", [P, T]) for r in range(RING)]
        c_sb = [sb(f"c_sb{r}", [P, T]) for r in range(RING)]
        hc = [sb(f"hc{r}", [P, T]) for r in range(RING)]
        y = [sb(f"y{d}", [P, T]) for d in range(2)]
        fb = sb("fb", [P, T])
        idx_i = fb[:, :].bitcast(I32)
        f1 = sb("f1", [P, 2, T])
        h1, h2, h3 = sb("h1", [P, T]), sb("h2", [P, T]), sb("h3", [P, T])
        angle, turns, feat = h1, h2, h3

        xa, xb = sb("xa", [P, T]), sb("xb", [P, T])
        lg, ls, ex, wt, gate = (sb(n, [P, TILES, NE]) for n in ("lg", "ls", "ex", "wt", "gate"))
        gt, eq = sb("gt", [P, TILES, NE, NE]), sb("eq", [P, TILES, NE, NE])
        rank = sb("rank", [P, TILES, NE])
        mx, sw, rw = (sb(n, [P, TILES]) for n in ("mx", "sw", "rw"))
        gate_t = sb("gate_t", [NE, T])
        yg = sb("yg", [P, NE, TILES * D])
        acc2 = sb("acc2", [P, TILES, P])
        acc = acc2[:, 0:2, :].rearrange("p a n -> p (a n)")
        held = sb("held", [P, TILES * NH])
        fin = sb("fin", [P, TILES, D])

        qu, qv, kk = xa, xb, sb("kk", [P, T])
        xg = sb("xg", [P, T])
        vv = sb("vv", [P, TILES, D])
        es = [sb(f"es{r}", [P, NH, SKEW]) for r in range(2)]
        hid = [es[r // 2][:, :, :].rearrange("p h n -> p (h n)")[:, r % 2 * T:(r % 2 + 1) * T] for r in range(RING)]
        ps = sb("ps", [P, TILES, NH, S])
        early = ps[:, :, :, :].rearrange("p b h s -> p (b h s)").rearrange("p (a c t) -> p a c t", a=2, c=NG)
        tok_h, tok_sq = early[:, 0], early[:, 1]
        tok_rs = yg[:, :, :].rearrange("p e n -> p (e n)").rearrange("p (c t) -> p c t", c=NG)
        ss = [xg[:, 0:S], xg[:, S:T], *(r[:, :, :, :].rearrange("p b e f -> p (b e f)") for r in (gt, eq))]
        smax, nmax, ssum, rsum = (sb(n, [P, TILES * NH]) for n in ("smax", "nmax", "ssum", "rsum"))
        pb = yg
        ptc = [sb(f"ptc{r}", [P, 2, S]) for r in range(2)]
        cn = sb("cn", [P, TILES * D])
        ct = kk[0:D, :]
        skew = nc.dram_tensor("skew", [TILES, P, NH, SKEW], F32, kind="Internal").ap()

        loaded = [signal(f"loaded{k}", ["done"]) for k in range(5)]
        tokv = signal("tok_vector", ["eps", "bias", "t", "norm", "angle", "k", "kr", "r1", "r2", "r3", "r4", "r5", "feat",
                                     *(f"xn{c}" for c in range(NG)), *(f"h{c}" for c in range(NG))])
        toks = signal("tok_scalar", ["sin", *(f"{s}{c}" for s in ("relu", "h2_", "sq", "ln", "rs", "aff")
                                              for c in range(NG))])
        tokp = signal("tok_tensor", [f"{s}{c}" for s in ("w1_", "w2_", "cen", "var", "res") for c in range(NG)])
        setg = signal("setup_pool", ["pad", "zero"])
        setv = signal("setup_vector", ["taps", "aneg", "bns", "bnt0", "bnt", "bn2d", "bn2s", "bn2t0", "bn2t", "outs", "skip",
                                       "sums", "ffw", "convw", "deltaw", "outw", "cent", "ffb", "e0b", "e0w",
                                       "pos", "bo"])
        sets = signal("setup_scalar", ["alog", "ln", "rsq", "ln2", "rsq2"])
        setp = signal("setup_tensor", ["conv", "delta", "outw", "cent", "ffb", "e0b", "pos", "bo"])

        x_t = signal("x_tensor", ["center", "var"])
        x_s = signal("x_scalar", ["h0", "sq", "ln", "rs", "low"])
        x_v = signal("x_vector", ["x", "high", "hx"])
        prep_t = signal("prep_tensor", ["conv0", "z0", "conv1", "z1", "bc0", "dt0", "bc1", "dt1"])
        prep_s = signal("prep_scalar", ["u0", "z0", "u1", "z1",
                                     *(f"{s}{d}" for d in range(2) for s in ("part", "abs", "relu", "exp", "ln"))])
        prep_v = signal("prep_vector", [f"{s}{d}" for d in range(2) for s in ("rest", "mid", "low", "delta", "du")])
        NM = 2 * NSTATE
        bc_ready = signal("bc_ready", list(range(NM)))
        decay_ready = signal("decay_ready", list(range(NM)))
        c_ready = signal("c_ready", list(range(NM)))
        drive_ready = signal("drive_ready", list(range(NM)))
        state_ready = signal("state_ready", list(range(NM)))
        hc_ready = signal("hc_ready", list(range(NM)))
        sum_done = signal("sum_done", list(range(NM)))
        y_sum = signal("y_sum", ["y0", "y1"])
        y_ready = signal("y_ready", ["y0", "y1"])
        comb_t = signal("out_tensor", ["center", "var", "f0", "f1", "ff"])
        comb_s = signal("out_scalar", ["sq", "ln", "rs", "g0", "g1"])
        comb_v = signal("out_vector", ["fb", "h1"])

        route = ["logits", "max", "shift", "gt", "eq", "tie", "sum", "rank"]
        mt = [signal("moe0_tensor", ["center", "var", "logits", "gate_t", "sum"]),
              signal("moe1_tensor", ["center", "var", "logits", "gate_t", "sum"])]
        ms = [signal("moe0_scalar", ["sq", "ln", "rs", "ln2", "rs2", "exp"]),
              signal("moe1_scalar", ["sq", "ln", "rs"])]
        mv = [signal("moe0_vector", ["xa", "xb", *route, "masked", "wsum", "wrec", "gate", "gate_t",
                                     "add1", "add2", "add3", "h"]),
              signal("moe1_vector", ["xa", *route, "gate", "gate_t", "add1", "add2", "add3", "h"])]
        NC = [NE * CH0, NE]
        down_done = [signal(f"down_done{m}", list(range(NE))) for m in range(2)]
        hid_ready = [signal(f"hid_ready{m}", list(range(NC[m]))) for m in range(2)]
        gelu_ready = [signal(f"gelu_ready{m}", list(range(NC[m]))) for m in range(2)]
        yg_ready = [signal(f"yg_ready{m}", list(range(NE // 2))) for m in range(2)]
        YB, SB, TB = (7, 4), (5, 4), (6, 3)

        NU = TILES * NH
        att_t = signal("attn_tensor", ["center", "var", "q", "k", "v", "ctx_t", "out"])
        att_s = signal("attn_scalar", ["sq", "ln", "rs", "xg", "qu", "qv", "ctx_t"])
        att_v = signal("attn_vector", ["xn", "k", "v", "rsum", "cn", "h"])
        e_ready = signal("e_ready", list(range(NU)))
        es_ready = signal("es_ready", list(range(NU)))
        s_ready = signal("s_ready", list(range(NU)))
        ss_ready = signal("ss_ready", list(range(NU)))
        nmax_ready = signal("nmax_ready", list(range(TILES)))
        p_ready = signal("p_ready", list(range(NU)))
        pt_ready = signal("pt_ready", list(range(GSEQ * NH)))
        ptc_ready = signal("ptc_ready", list(range(GSEQ * NH)))
        ctx_ready = signal("ctx_ready", list(range(GSEQ * NH)))
        skew_out = [signal(f"skew_out{b}", list(range(16))) for b in range(TILES)]
        skew_in = [signal(f"skew_in{b}", list(range(16))) for b in range(TILES)]
        stored = signal("stored", list(range(16)))

        block = ctx.enter_context(nc.Block())

        @block.sync
        def _(sp):
            for k, (dst, src) in enumerate([(idx_i, idx), (packed[0], w0), (packed[1], w1), (sel, sel_in),
                                            (packed[2], w2)]):
                sp.dma_start(dst[:, :] if k else dst, src).then_inc(loaded[k].sem, 16)

            def skews(i):
                for b in range(TILES):
                    sp.wait_ge(*es_ready(i, NH * (b + 1)))
                    sp.wait_ge(*skew_in[b].before(i))
                    sp.dma_start(skew[b], es[b % 2][:, :, :]).then_inc(skew_out[b].sem, 16)
                    sp.wait_ge(*skew_out[b](i, 16))
                    rows = skew[b]
                    shifted = bass.AP(rows.tensor, rows.offset + P - 1,
                                      [[NH * SKEW - 1, P], [SKEW, NH], [1, S]])
                    sp.dma_start(ps[:, b, :, :], shifted).then_inc(skew_in[b].sem, 16)

            def store(i):
                sp.wait_ge(*mv[1](i, "h"))
                sp.dma_start(out[bass.ds(i, 1)].rearrange("g p b d -> (g p) b d"), fin[:, :, :]).then_inc(stored.sem, 16)

            with sp.Fori(0, NG) as i:
                skews(i)
                store(i)
            sp.wait_ge(*stored.before(NG))

        @block.gpsimd
        def _(pool):
            pool.memset(xpad[:, :, :], 0.0).then_inc(setg.sem, 1)
            for d in range(2):
                edge = 0 if d == 0 else S - 1
                for r in range(RING):
                    v = decay[d][r][:, :].rearrange("p (s t) -> p s t", s=GSEQ)
                    last = pool.memset(v[:, :, edge:edge + 1], 0.0)
            last.then_inc(setg.sem, 1)

            def scan_outputs(i):
                for m in range(NM):
                    pool.wait_ge(*state_ready(i, m + 1))
                    pool.wait_ge(*c_ready(i, m + 1))
                    pool.wait_ge(*sum_done(i, max(m + 1 - RING, 0)))
                    pool.tensor_tensor(hc[m % RING][:, :], state[m % RING][:, :], c_sb[m % RING][:, :],
                                       ALU.mult).then_inc(hc_ready.sem, 1)

            with pool.Fori(0, NG) as i:
                scan_outputs(i)

        @block.scalar
        def _(act):
            def afn(out_, in_, fn, **kw):
                return act.activation(out_, in_, fn, **kw)

            act.wait_ge(*tokv(0, "r5"))
            afn(feat[:, :], angle[:, :], ACT.Sin).then_inc(toks.sem, 1)
            act.wait_ge(loaded[1].sem, 16)
            for c in range(NG):
                act.wait_ge(*tokp(0, f"w1_{c}"))
                afn(tok_h[:, c, :], bank[c][:, :], ACT.Relu, bias=W("tok_b1")).then_inc(toks.sem, 1)
            for c in range(NG):
                act.wait_ge(*tokp(0, f"w2_{c}"))
                afn(tok_h[:, c, :], bank[4 + c][:, :], ACT.Identity, bias=W("tok_b2")).then_inc(toks.sem, 1)
            for c in range(NG):
                act.wait_ge(*tokp(0, f"cen{c}"))
                afn(tok_sq[:, c, :], bank[c][:, :], ACT.Square).then_inc(toks.sem, 1)
            act.preload_act_table_set("natural_log_exp_and_others")
            act.wait_ge(*tokv(0, "bias"))
            for c in range(NG):
                act.wait_ge(*tokp(0, f"var{c}"))
                afn(tok_rs[:, c, :], bank[4 + c][:, :], ACT.Ln, bias=eps1).then_inc(toks.sem, 1)
            for c in range(NG):
                act.wait_ge(*toks(0, f"ln{c}"))
                afn(tok_rs[:, c, :], tok_rs[:, c, :], ACT.Exp, scale=-0.5).then_inc(toks.sem, 1)
            for c in range(NG):
                act.wait_ge(*tokv(0, f"xn{c}"))
                afn(tok_sq[:, c, :], tok_sq[:, c, :], ACT.Identity, scale=W("tok_g"), bias=tok_bias[:, :])\
                    .then_inc(toks.sem, 1)
            act.wait_ge(loaded[2].sem, 16)
            afn(a_neg[:, :], W("alog"), ACT.Exp).then_inc(sets.sem, 1)
            afn(bn_s[:, :], W("bn_v"), ACT.Ln, bias=eps1).then_inc(sets.sem, 1)
            act.wait_ge(*sets(0, "ln"))
            afn(bn_s[:, :], bn_s[:, :], ACT.Exp, scale=-0.5).then_inc(sets.sem, 1)
            afn(bn2_s[:, :], W("bn2_v"), ACT.Ln, bias=eps1).then_inc(sets.sem, 1)
            act.wait_ge(*sets(0, "ln2"))
            afn(bn2_s[:, :], bn2_s[:, :], ACT.Exp, scale=-0.5).then_inc(sets.sem, 1)
            act.wait_ge(*setg(0, "zero"))
            act.wait_ge(*setv(0, "bo"))

            def rsqrt(pe_sig, s_sig, i, b, ln="ln", rs_="rs", dst=rs, bias=None, scale=1.0):
                act.wait_ge(*pe_sig(i, "var"))
                afn(dst[:, :], bank[b][:, :], ACT.Ln, bias=bias, scale=scale).then_inc(s_sig.sem, 1)
                act.wait_ge(*s_sig(i, ln))
                afn(dst[:, :], dst[:, :], ACT.Exp, scale=-0.5).then_inc(s_sig.sem, 1)

            def normalise_x(i):
                act.preload_act_table_set("natural_log_exp_and_others")
                afn(h0[:, :], h_all[:, bass.ds(i * T, T)], ACT.Copy).then_inc(x_s.sem, 1)
                act.wait_ge(*x_t(i, "center"))
                afn(sq[:, :], bank[0][:, :], ACT.Square).then_inc(x_s.sem, 1)
                rsqrt(x_t, x_s, i, 1, bias=eps1)
                act.wait_ge(*x_v(i, "x"))
                afn(xpad[0:D, :, TAPS - 1:TAPS - 1 + S], xf[0:D, :].rearrange("p (s t) -> p s t", s=GSEQ),
                    ACT.Copy).then_inc(x_s.sem, 1)

            def prepare(i):
                act.preload_act_table_set("silu_and_others")
                for d in range(2):
                    act.wait_ge(*prep_t(i, f"conv{d}"))
                    afn(u[d][:, :], bank[d][:, :], ACT.Silu, bias=W("conv_b")[:, d:d + 1]).then_inc(prep_s.sem, 1)
                    act.wait_ge(*prep_t(i, f"z{d}"))
                    afn(z[d][:, :], bank[2 + d][:, :], ACT.Silu).then_inc(prep_s.sem, 1)
                act.preload_act_table_set("natural_log_exp_and_others")
                for d in range(2):
                    dtb = W("dt_b")[:, d:d + 1]
                    act.wait_ge(*prep_t(i, f"bc{d}"))
                    afn(bc[d][:, :], bank[d][:, :], ACT.Copy).then_inc(prep_s.sem, 1)
                    act.wait_ge(*prep_t(i, f"dt{d}"))
                    if d:
                        act.wait_ge(*prep_v(i, "delta0"))
                    afn(ab[:, :], bank[2 + d][:, :], ACT.Abs, bias=dtb).then_inc(prep_s.sem, 1)
                    afn(soft[:, :], bank[2 + d][:, :], ACT.Relu, bias=dtb).then_inc(prep_s.sem, 1)
                    act.wait_ge(*prep_s(i, f"abs{d}"))
                    afn(ab[:, :], ab[:, :], ACT.Exp, scale=-1.0).then_inc(prep_s.sem, 1)
                    act.wait_ge(*prep_s(i, f"exp{d}"))
                    afn(ab[:, :], ab[:, :], ACT.Ln, bias=1.0).then_inc(prep_s.sem, 1)

            def scan_inputs(i):
                for m in range(NM):
                    d, n = divmod(m, NSTATE)
                    cut = slice(1, S) if d == 0 else slice(0, S - 1)
                    if n == 0:
                        act.wait_ge(*prep_v(i, f"delta{d}"))
                    act.wait_ge(*state_ready(i, max(m + 1 - RING, 0)))
                    afn(decay[d][m % RING][:, :].rearrange("p (s t) -> p s t", s=GSEQ)[:, :, cut],
                        delta[d][:, :].rearrange("p (s t) -> p s t", s=GSEQ)[:, :, cut], ACT.Exp,
                        scale=a_neg[:, m:m + 1]).then_inc(decay_ready.sem, 1)
                    act.wait_ge(*bc_ready(i, m + 1))
                    act.wait_ge(*hc_ready(i, max(m + 1 - RING, 0)))
                    afn(c_sb[m % RING][:, :], bank[2 + m % 2][:, :], ACT.Copy).then_inc(c_ready.sem, 1)

            def combine(i):
                act.wait_ge(*comb_t(i, "center"))
                afn(sq[:, :], bank[0][:, :], ACT.Square, bias=cen_t[:, :]).then_inc(comb_s.sem, 1)
                rsqrt(comb_t, comb_s, i, 1, bias=eps1)
                for c in range(2):
                    act.wait_ge(*comb_t(i, f"f{c}"))
                    afn(f1[:, c, :], bank[2 + c][:, :], ACT.Relu, bias=ff_b1[:, c:c + 1]).then_inc(comb_s.sem, 1)

            def experts(i, m):
                t, s = mt[m], ms[m]
                act.wait_ge(*t(i, "center"))
                afn(sq[:, :], bank[5][:, :], ACT.Square).then_inc(s.sem, 1)
                rsqrt(t, s, i, 6, bias=eps1)
                if m == 0:
                    rsqrt(t, s, i, 6, "ln2", "rs2", rs2, bias=eps2, scale=1.0 + EPS)
                    act.wait_ge(*mv[0](i, "shift"))
                    afn(ex[:, :, :], ls[:, :, :], ACT.Exp).then_inc(s.sem, 1)
                act.preload_act_table_set("gelu_and_others")
                bias = (e0_b1[:, :], W("e1_b1"))[m]
                ch = NC[m] // NE
                for c in range(NC[m]):
                    act.wait_ge(*hid_ready[m](i, c + 1))
                    if c >= RING:
                        act.wait_ge(*down_done[m](i, (c - RING) // ch + 1))
                    afn(hid[c % RING], bank[5 + c % 2][:, :], ACT.Gelu, bias=bias[:, c:c + 1])\
                        .then_inc(gelu_ready[m].sem, 1)

            def attention(i):
                act.preload_act_table_set("natural_log_exp_and_others")
                act.wait_ge(*att_t(i, "center"))
                afn(sq[:, :], bank[5][:, :], ACT.Square).then_inc(att_s.sem, 1)
                rsqrt(att_t, att_s, i, 6, bias=eps2, scale=1.0 + EPS)
                act.wait_ge(*att_v(i, "xn"))
                afn(xg[0:D, :], xg[0:D, :], ACT.Identity, scale=W("at_g", slice(0, D)),
                    bias=W("at_b", slice(0, D))).then_inc(att_s.sem, 1)
                act.wait_ge(*att_t(i, "q"))
                afn(qu[:, :], bank[5][:, :], ACT.Identity, bias=bq_u[:, :]).then_inc(att_s.sem, 1)
                afn(qv[:, :], bank[5][:, :], ACT.Identity, bias=bq_v[:, :]).then_inc(att_s.sem, 1)
                for j in range(NU):
                    b, h = divmod(j, NH)
                    act.wait_ge(*e_ready(i, j + 1))
                    if h == 0:
                        act.wait_ge(*(skew_out[b - 2](i, 16) if b >= 2 else skew_out[b + 2].before(i)))
                    afn(es[b % 2][:, h, :], bank[5 + j % 3][:, 0:SKEW], ACT.Copy).then_inc(es_ready.sem, 1)
                for b in range(TILES):
                    act.wait_ge(*nmax_ready(i, b + 1))
                    if b == 2:
                        act.wait_ge(*pt_ready(i, NH))
                    for h in range(NH):
                        j = b * NH + h
                        afn(pb[:, (b % 2) * NH + h, :], ss[h], ACT.Exp, scale=HD ** -0.5,
                            bias=nmax[:, j:j + 1], accum_out=ssum[:, j:j + 1]).then_inc(p_ready.sem, 1)
                act.wait_ge(*att_t(i, "ctx_t"))
                afn(ct, bank[5][0:D, :], ACT.Copy).then_inc(att_s.sem, 1)

            with act.Fori(0, NG) as i:
                normalise_x(i)
                prepare(i)
                scan_inputs(i)
                combine(i)
                experts(i, 0)
                attention(i)
                act.preload_act_table_set("natural_log_exp_and_others")
                experts(i, 1)

        @block.vector
        def _(dve):
            dve.memset(eps_c[:, 0:1], EPS)
            dve.memset(eps_c[:, 1:2], EPS * EPS).then_inc(tokv.sem, 1)
            dve.wait_ge(loaded[0].sem, 16)
            dve.wait_ge(loaded[1].sem, 16)
            dve.tensor_scalar(tok_bias[:, :], W("tok_bres"), 0.1, W("tok_b"), ALU.mult, ALU.add).then_inc(tokv.sem, 1)
            dve.tensor_copy(angle[:, :], idx_i).then_inc(tokv.sem, 1)
            dve.wait_ge(*tokv(0, "t"))
            dve.tensor_scalar(angle[:, :], angle[:, :], TWO_PI, W("invp"), ALU.mult, ALU.mult).then_inc(tokv.sem, 1)
            dve.wait_ge(*tokv(0, "norm"))
            dve.tensor_scalar(angle[:, :], angle[:, :], W("harm"), W("phase"), ALU.mult, ALU.add)\
                .then_inc(tokv.sem, 1)
            dve.wait_ge(*tokv(0, "angle"))
            dve.tensor_scalar(turns[:, :], angle[:, :], 1.0 / TWO_PI, W("quarter"), ALU.mult, ALU.add)\
                .then_inc(tokv.sem, 1)
            dve.wait_ge(*tokv(0, "k"))
            dve.tensor_scalar(turns[:, :], turns[:, :], ROUND, ROUND, ALU.add, ALU.subtract).then_inc(tokv.sem, 1)
            for n, part in enumerate(TURN):
                dve.wait_ge(*tokv(0, ("kr", "r1", "r2")[n]))
                dve.scalar_tensor_tensor(out=angle[:, :], in0=turns[:, :], scalar=-part, in1=angle[:, :],
                                         op0=ALU.mult, op1=ALU.add).then_inc(tokv.sem, 1)
            dve.wait_ge(*tokv(0, "r3"))
            dve.tensor_scalar(angle[:, :], angle[:, :], W("halfpi"), PI_LO, ALU.add, ALU.min).then_inc(tokv.sem, 1)
            dve.wait_ge(*tokv(0, "r4"))
            dve.tensor_scalar(angle[:, :], angle[:, :], -PI_LO, None, ALU.max).then_inc(tokv.sem, 1)
            dve.wait_ge(*toks(0, "sin"))
            dve.tensor_scalar(feat[:, :], feat[:, :], W("amp"), None, ALU.mult).then_inc(tokv.sem, 1)
            for c in range(NG):
                dve.wait_ge(*toks(0, f"rs{c}"))
                dve.tensor_tensor(tok_sq[:, c, :], bank[c][:, :], tok_rs[:, c, :], ALU.mult).then_inc(tokv.sem, 1)
            for c in range(NG):
                dve.wait_ge(*toks(0, f"aff{c}"))
                dve.wait_ge(*tokp(0, f"res{c}"))
                dve.scalar_tensor_tensor(out=h_all[:, c * T:(c + 1) * T], in0=bank[4 + c][:, :], scalar=0.1,
                                         in1=tok_sq[:, c, :], op0=ALU.mult, op1=ALU.add).then_inc(tokv.sem, 1)

            dve.wait_ge(loaded[2].sem, 16)
            for d in range(2):
                for k in range(TAPS):
                    pair, half = divmod(k if d == 0 else TAPS - 1 - k, 2)
                    last = dve.tensor_scalar(conv_s[:, 2 * d + pair, half * D:(half + 1) * D],
                                             W("inx")[:, d * D:(d + 1) * D],
                                             W("conv_w")[:, d * TAPS + k:d * TAPS + k + 1], None, ALU.mult)
            last.then_inc(setv.sem, 1)
            dve.wait_ge(*sets(0, "rsq2"))
            dve.tensor_scalar(a_neg[:, :], a_neg[:, :], -1.0, None, ALU.mult).then_inc(setv.sem, 1)
            dve.tensor_scalar(bn_s[:, :], bn_s[:, :], W("bn_g"), None, ALU.mult).then_inc(setv.sem, 1)
            dve.wait_ge(*setv(0, "bns"))
            dve.tensor_scalar(bn_t[:, :], W("bn_m"), bn_s[:, :], -1.0, ALU.mult, ALU.mult).then_inc(setv.sem, 1)
            dve.wait_ge(*setv(0, "bnt0"))
            dve.tensor_scalar(bn_t[:, :], bn_t[:, :], W("bn_b"), None, ALU.add).then_inc(setv.sem, 1)
            dve.tensor_tensor(bn2_d[:, :], W("bn2_m"), W("ff_b2"), ALU.subtract).then_inc(setv.sem, 1)
            dve.tensor_scalar(bn2_s[:, :], bn2_s[:, :], W("bn2_g"), None, ALU.mult).then_inc(setv.sem, 1)
            dve.wait_ge(*setv(0, "bn2s"))
            dve.tensor_scalar(bn2_t[:, :], bn2_d[:, :], bn2_s[:, :], -1.0, ALU.mult, ALU.mult).then_inc(setv.sem, 1)
            dve.wait_ge(*setv(0, "bn2t0"))
            dve.tensor_scalar(bn2_t[:, :], bn2_t[:, :], W("bn2_b"), None, ALU.add).then_inc(setv.sem, 1)
            dve.tensor_scalar(out_s[:, :], W("out_w"), bn_s[:, :], None, ALU.mult).then_inc(setv.sem, 1)
            for d in range(2):
                last = dve.tensor_scalar(skip_w[:, d, :], W("ident"), W("dskip")[:, d:d + 1], None, ALU.mult)
            last.then_inc(setv.sem, 1)
            dve.wait_ge(loaded[4].sem, 16)
            dve.tensor_tensor(bq_u[:, :], W("at_bq"), W("at_u"), ALU.add)
            dve.tensor_tensor(bq_v[:, :], W("at_bq"), W("at_v"), ALU.add).then_inc(setv.sem, 1)
            dve.tensor_scalar(ff_w1[:, :], W("ff_w1"), W("ln_g"), None, ALU.mult).then_inc(setv.sem, 1)
            dve.wait_ge(*setp(0, "conv"))
            dve.tensor_copy(conv_w[:, :, :], bank[0][:, :].rearrange("p (q n) -> p q n", q=4)).then_inc(setv.sem, 1)
            dve.wait_ge(*setp(0, "delta"))
            dve.tensor_copy(delta_w[:, :, :], bank[1][:, 0:2 * P].rearrange("p (d n) -> p d n", d=2))\
                .then_inc(setv.sem, 1)
            dve.wait_ge(*setp(0, "outw"))
            for d in range(2):
                last = dve.tensor_copy(out_w[:, d, :], bank[2 + d][:, 0:D])
            last.then_inc(setv.sem, 1)
            dve.wait_ge(*setp(0, "cent"))
            dve.tensor_copy(cen_t[:, :], bank[4][:, 0:1]).then_inc(setv.sem, 1)
            dve.wait_ge(*setp(0, "ffb"))
            dve.tensor_tensor(ff_b1[:, :], bank[5][:, 0:2], W("ff_b1"), ALU.add).then_inc(setv.sem, 1)
            dve.wait_ge(*setp(0, "e0b"))
            for c in range(CH0):
                last = dve.tensor_tensor(e0_b1[:, :].rearrange("p (e c) -> p e c", c=CH0)[:, :, c],
                                         bank[6 + c][:, 0:NE],
                                         W("e0_b1").rearrange("p (e c) -> p e c", c=CH0)[:, :, c], ALU.add)
            last.then_inc(setv.sem, 1)
            dve.tensor_tensor(e0_w1, e0_w1, W("e0_g").unsqueeze(2).to_broadcast([P, NE, P]), ALU.mult)\
                .then_inc(setv.sem, 1)
            dve.wait_ge(*setp(0, "pos"))
            dve.tensor_scalar(pos[:, :], bank[0][:, 0:2 * S - 1], W("at_bp"), None, ALU.add).then_inc(setv.sem, 1)
            dve.wait_ge(*setp(0, "bo"))
            dve.tensor_tensor(bo_v[:, :], bank[1][:, 0:1], W("at_bo"), ALU.add).then_inc(setv.sem, 1)

            def normalise_x(i):
                dve.wait_ge(*x_s(i, "rs"))
                dve.tensor_tensor(xf[:, :], bank[0][:, :], rs[:, :], ALU.mult).then_inc(x_v.sem, 1)
                dve.tensor_tensor(xpad[D:P, :, TAPS - 2:TAPS - 2 + S],
                                  bank[0][D:P, :].rearrange("p (s t) -> p s t", s=GSEQ),
                                  rs[D:P, :].rearrange("p (s t) -> p s t", s=GSEQ), ALU.mult).then_inc(x_v.sem, 1)
                dve.wait_ge(*x_v(i, "x"))
                dve.scalar_tensor_tensor(out=hx[:, :], in0=xf[:, :], scalar=bn2_t[:, :], in1=h0[:, :],
                                         op0=ALU.add, op1=ALU.add).then_inc(x_v.sem, 1)

            def prepare(i):
                hi, lo = slice(2 * D - D, P), slice(P - 32, P)
                for d in range(2):
                    dve.wait_ge(*prep_s(i, f"part{d}"))
                    dve.tensor_tensor(rest[hi, :], bank[d][hi, :], bc[d][hi, :], ALU.subtract).then_inc(prep_v.sem, 1)
                    dve.wait_ge(*prep_v(i, f"rest{d}"))
                    dve.tensor_copy(bc[d][hi, :], rest[hi, :]).then_inc(prep_v.sem, 1)
                    dve.wait_ge(*prep_v(i, f"mid{d}"))
                    dve.tensor_tensor(bc[d][lo, :], rest[lo, :], bc[d][lo, :], ALU.subtract).then_inc(prep_v.sem, 1)
                    dve.wait_ge(*prep_s(i, f"ln{d}"))
                    dve.tensor_tensor(delta[d][:, :], ab[:, :], soft[:, :], ALU.add).then_inc(prep_v.sem, 1)
                    dve.wait_ge(*prep_v(i, f"delta{d}"))
                    dve.tensor_tensor(du[d][:, :], delta[d][:, :], u[d][:, :], ALU.mult).then_inc(prep_v.sem, 1)

            def scans(i):
                def driven(m):
                    dve.wait_ge(*bc_ready(i, m + 1))
                    if m % NSTATE == 0:
                        dve.wait_ge(*prep_v(i, f"du{m // NSTATE}"))
                    dve.wait_ge(*state_ready(i, max(m - 1, 0)))
                    dve.tensor_tensor(drive[m % 2][:, :], bank[m % 2][:, :], du[m // NSTATE][:, :], ALU.mult)\
                        .then_inc(drive_ready.sem, 1)

                def gated(d):
                    dve.wait_ge(*y_sum(i, f"y{d}"))
                    dve.tensor_tensor(y[d][:, :], bank[4][:, :], z[d][:, :], ALU.mult).then_inc(y_ready.sem, 1)

                driven(0)
                for m in range(NM):
                    if m + 1 < NM:
                        driven(m + 1)
                    dve.wait_ge(*drive_ready(i, m + 1))
                    dve.wait_ge(*decay_ready(i, m + 1))
                    dve.wait_ge(*hc_ready(i, max(m + 1 - RING, 0)))
                    way = slice(None) if m < NSTATE else slice(None, None, -1)
                    dve.tensor_tensor_scan(state[m % RING][:, way], decay[m // NSTATE][m % RING][:, way],
                                           drive[m % 2][:, way], 0.0, ALU.mult, ALU.add).then_inc(state_ready.sem, 1)
                    if m == NSTATE + 1:
                        gated(0)
                gated(1)

            def combine(i):
                dve.wait_ge(*comb_s(i, "rs"))
                dve.scalar_tensor_tensor(out=fb[:, :], in0=bank[0][:, :], scalar=cen_t[:, :], in1=rs[:, :],
                                         op0=ALU.add, op1=ALU.mult).then_inc(comb_v.sem, 1)
                dve.wait_ge(*comb_t(i, "ff"))
                dve.scalar_tensor_tensor(out=h1[:, :], in0=bank[0][:, :], scalar=bn2_s[:, :], in1=hx[:, :],
                                         op0=ALU.mult, op1=ALU.add).then_inc(comb_v.sem, 1)

            def experts(i, m):
                t, s, v = mt[m], ms[m], mv[m]
                dve.wait_ge(*s(i, "rs"))
                dve.tensor_tensor(xa[:, :], bank[5][:, :], rs[:, :], ALU.mult).then_inc(v.sem, 1)
                if m == 0:
                    dve.wait_ge(*s(i, "rs2"))
                    dve.tensor_tensor(xb[:, :], bank[5][:, :], rs2[:, :], ALU.mult).then_inc(v.sem, 1)
                dve.wait_ge(*t(i, "logits"))
                bias = W("e0_br") if m == 0 else W("e1_bg")
                dve.tensor_tensor(lg[:, :, :], bank[6][:, 0:TILES * NE].rearrange("p (b e) -> p b e", e=NE),
                                  bias.unsqueeze(1).to_broadcast([P, TILES, NE]), ALU.add).then_inc(v.sem, 1)
                dve.wait_ge(*v(i, "logits"))
                dve.tensor_reduce(mx[:, :], lg[:, :, :], AX.X, ALU.max).then_inc(v.sem, 1)
                dve.wait_ge(*v(i, "max"))
                dve.tensor_tensor(ls[:, :, :], lg[:, :, :], mx[:, :].unsqueeze(2).to_broadcast([P, TILES, NE]),
                                  ALU.subtract).then_inc(v.sem, 1)
                mine = lg[:, :, :].unsqueeze(3).to_broadcast([P, TILES, NE, NE])
                other = lg[:, :, :].unsqueeze(2).to_broadcast([P, TILES, NE, NE])
                dve.tensor_tensor(gt[:, :, :, :], other, mine, ALU.is_gt).then_inc(v.sem, 1)
                dve.tensor_tensor(eq[:, :, :, :], other, mine, ALU.is_equal).then_inc(v.sem, 1)
                dve.wait_ge(*v(i, "eq"))
                tri = W("tri").rearrange("p (a b) -> p a b", a=NE).unsqueeze(1).to_broadcast([P, TILES, NE, NE])
                dve.tensor_tensor(eq[:, :, :, :], eq[:, :, :, :], tri, ALU.mult).then_inc(v.sem, 1)
                dve.wait_ge(*v(i, "tie"))
                dve.tensor_tensor(gt[:, :, :, :], gt[:, :, :, :], eq[:, :, :, :], ALU.add).then_inc(v.sem, 1)
                dve.wait_ge(*v(i, "sum"))
                dve.tensor_reduce(rank[:, :, :], gt[:, :, :, :], AX.X, ALU.add).then_inc(v.sem, 1)
                dve.wait_ge(*v(i, "rank"))
                if m == 0:
                    dve.wait_ge(*s(i, "exp"))
                    dve.scalar_tensor_tensor(out=wt[:, :, :], in0=rank[:, :, :], scalar=1.5, in1=ex[:, :, :],
                                             op0=ALU.is_lt, op1=ALU.mult).then_inc(v.sem, 1)
                    dve.wait_ge(*v(i, "masked"))
                    dve.tensor_reduce(sw[:, :], wt[:, :, :], AX.X, ALU.add).then_inc(v.sem, 1)
                    dve.wait_ge(*v(i, "wsum"))
                    dve.reciprocal(rw[:, :], sw[:, :]).then_inc(v.sem, 1)
                    dve.wait_ge(*v(i, "wrec"))
                    dve.tensor_tensor(gate[:, :, :], wt[:, :, :], rw[:, :].unsqueeze(2).to_broadcast([P, TILES, NE]),
                                      ALU.mult).then_inc(v.sem, 1)
                else:
                    dve.tensor_scalar(gate[:, :, :], rank[:, :, :], 1.5, None, ALU.is_lt).then_inc(v.sem, 1)
                dve.wait_ge(*t(i, "gate_t"))
                dve.tensor_copy(gate_t[:, :], bank[7][0:NE, :]).then_inc(v.sem, 1)
                for q in range(NE // 2):
                    dve.wait_ge(*down_done[m](i, 2 * q + 2))
                    gates = gate[:, :, 2 * q:2 * q + 2].rearrange("p b e -> p e b").unsqueeze(3)
                    dve.tensor_tensor(yg[:, 2 * q:2 * q + 2, :].rearrange("p e (b n) -> p e b n", b=TILES),
                                      bank[YB[q % 2]][:, :].rearrange("p (e b n) -> p e b n", e=2, b=TILES),
                                      gates.to_broadcast([P, 2, TILES, D]), ALU.mult)\
                        .then_inc(yg_ready[m].sem, 1)
                dve.wait_ge(*yg_ready[m](i, NE // 2))
                dve.tensor_tensor(yg[:, 0:4, :], yg[:, 0:4, :], yg[:, 4:8, :], ALU.add).then_inc(v.sem, 1)
                dve.wait_ge(*v(i, "add1"))
                dve.tensor_tensor(yg[:, 0:2, :], yg[:, 0:2, :], yg[:, 2:4, :], ALU.add).then_inc(v.sem, 1)
                dve.wait_ge(*v(i, "add2"))
                if m == 0:
                    parts = (yg[:, k, :].rearrange("p (b n) -> p b n", b=TILES).unsqueeze(2)
                             .to_broadcast([P, TILES, 2, D]) for k in range(2))
                    dve.tensor_tensor(acc2[:, :, :].rearrange("p b (a n) -> p b a n", a=2), *parts, ALU.add)\
                        .then_inc(v.sem, 1)
                else:
                    dve.tensor_tensor(acc, yg[:, 0, :], yg[:, 1, :], ALU.add).then_inc(v.sem, 1)
                dve.wait_ge(*t(i, "sum"))
                if m == 0:
                    dve.tensor_tensor(h2[:, :], bank[5][:, :], h1[:, :], ALU.add).then_inc(v.sem, 1)
                else:
                    dve.wait_ge(*v(i, "add3"))
                    dve.wait_ge(*stored.before(i))
                    dve.tensor_tensor(fin[:, :, :].rearrange("p b n -> p (b n)"), bank[5][:, 0:TILES * D],
                                      acc, ALU.add).then_inc(v.sem, 1)

            def attention(i):
                dve.wait_ge(*att_s(i, "rs"))
                dve.tensor_tensor(xg[0:D, :], bank[5][0:D, :], rs[0:D, :], ALU.mult).then_inc(att_v.sem, 1)
                dve.wait_ge(*att_t(i, "k"))
                dve.tensor_scalar(kk[:, :], bank[6][:, :], W("at_bk"), None, ALU.add).then_inc(att_v.sem, 1)
                dve.wait_ge(*att_t(i, "v"))
                dve.tensor_copy(vv[:, :, :], bank[7][:, 0:TILES * D].rearrange("p (b n) -> p b n", b=TILES))\
                    .then_inc(att_v.sem, 1)

                def scores(b):
                    dve.wait_ge(skew_in[b].sem, (i + 1) * 16)
                    for h in range(NH):
                        j = b * NH + h
                        dve.wait_ge(*s_ready(i, j + 1))
                        dve.wait_ge(*p_ready(i, max(j + 1 - RING, 0)))
                        dve.memset(held[:, j:j + 1], 0.0)
                        dve.tensor_tensor_reduce(out=ss[h], in0=bank[SB[j % 2]][:, 0:S],
                                                 in1=ps[:, b, h, :], scale=1.0, scalar=-3.0e38, op0=ALU.add,
                                                 op1=ALU.max, accum_out=smax[:, j:j + 1]).then_inc(ss_ready.sem, 1)
                    dve.wait_ge(*ss_ready(i, (b + 1) * NH))
                    dve.tensor_scalar(nmax[:, b * NH:(b + 1) * NH], smax[:, b * NH:(b + 1) * NH], -HD ** -0.5, None,
                                      ALU.mult).then_inc(nmax_ready.sem, 1)

                def transposed(s):
                    for h in range(NH):
                        n = s * NH + h
                        dve.wait_ge(*pt_ready(i, n + 1))
                        dve.wait_ge(*ctx_ready(i, max(n - 1, 0)))
                        dve.tensor_copy(ptc[n % 2][:, :, :], bank[TB[n % 2]][:, :].rearrange("p (a t) -> p a t", a=2))\
                            .then_inc(ptc_ready.sem, 1)

                scores(0)
                scores(1)
                transposed(0)
                scores(2)
                scores(3)
                transposed(1)
                dve.wait_ge(*p_ready(i, NU))
                dve.reciprocal(rsum[:, :], ssum[:, :]).then_inc(att_v.sem, 1)
                dve.wait_ge(*att_v(i, "rsum"))
                dve.wait_ge(*ctx_ready(i, GSEQ * NH))
                dve.tensor_tensor(cn[:, :].rearrange("p (j n) -> p j n", n=HD),
                                  bank[7][:, 0:TILES * D].rearrange("p (j n) -> p j n", n=HD),
                                  rsum[:, :].unsqueeze(2).to_broadcast([P, NU, HD]), ALU.mult).then_inc(att_v.sem, 1)
                dve.wait_ge(*att_t(i, "out"))
                dve.scalar_tensor_tensor(out=h3[:, :], in0=bank[6][:, :], scalar=bo_v[:, :], in1=h2[:, :],
                                         op0=ALU.add, op1=ALU.add).then_inc(att_v.sem, 1)

            with dve.Fori(0, NG) as i:
                normalise_x(i)
                prepare(i)
                scans(i)
                combine(i)
                experts(i, 0)
                attention(i)
                experts(i, 1)

        @block.tensor
        def _(pe):
            def mm(out_, lhsT, rhs, start=True, stop=True):
                return pe.matmul(out_, lhsT, rhs, start=start, stop=stop)

            def rows(c):
                return slice(32 * c, 32 * c + FD)

            pe.wait_ge(loaded[1].sem, 16)
            pe.wait_ge(*tokv(0, "feat"))
            for c in range(NG):
                mm(bank[c][:, :], W("tok_w1", rows(c)), feat[rows(c), :]).then_inc(tokp.sem, 1)
            for c in range(NG):
                pe.wait_ge(*toks(0, f"relu{c}"))
                mm(bank[4 + c][:, :], W("tok_w2"), tok_h[:, c, :]).then_inc(tokp.sem, 1)
            for c in range(NG):
                pe.wait_ge(*toks(0, f"h2_{c}"))
                mm(bank[c][:, :], W("center"), tok_h[:, c, :]).then_inc(tokp.sem, 1)
            for c in range(NG):
                pe.wait_ge(*toks(0, f"sq{c}"))
                mm(bank[4 + c][:, :], W("mean"), tok_sq[:, c, :]).then_inc(tokp.sem, 1)
            for c in range(NG):
                pe.wait_ge(*toks(0, f"ln{c}"))
                mm(bank[4 + c][:, :], W("tok_wres", rows(c)), feat[rows(c), :]).then_inc(tokp.sem, 1)

            pe.wait_ge(loaded[2].sem, 16)
            pe.wait_ge(*setv(0, "taps"))
            for q in range(4):
                last = pe.transpose(bank[0][:, q * P:(q + 1) * P], conv_s[:, q, :], W("ident"))
            last.then_inc(setp.sem, 1)
            for d in range(2):
                last = mm(bank[1][:, d * P:(d + 1) * P], W("xp_dt", slice(0, RANK))[:, d * P:(d + 1) * P],
                          W("dt_w", slice(0, RANK))[:, d * P:(d + 1) * P])
            last.then_inc(setp.sem, 1)
            pe.wait_ge(*setv(0, "outs"))
            for d in range(2):
                r = slice(d * D, (d + 1) * D)
                last = mm(bank[2 + d][:, 0:D], out_s[r, :], W("centers", r))
            last.then_inc(setp.sem, 1)
            mm(bank[4][:, 0:1], W("center2"), bn_t[:, :]).then_inc(setp.sem, 1)
            for c in range(2):
                last = mm(bank[5][:, c:c + 1], W("ff_w1")[:, c * P:(c + 1) * P], W("ln_b"))
            last.then_inc(setp.sem, 1)
            pe.wait_ge(loaded[4].sem, 16)
            for c in range(CH0):
                r = slice(c * D, (c + 1) * D)
                for e in range(NE):
                    last = mm(bank[6 + c][:, e:e + 1], W("e0_w1", r)[:, e * P:(e + 1) * P],
                              W("e0_lb", r)[:, e:e + 1])
            last.then_inc(setp.sem, 1)
            lo = slice(0, D)
            pe.wait_ge(*setv(0, "deltaw"))
            mm(bank[0][:, 0:2 * S - 1], W("at_wp", lo), W("enc", lo)).then_inc(setp.sem, 1)
            mm(bank[1][:, 0:1], W("at_wo", lo), W("at_bv", lo)).then_inc(setp.sem, 1)
            pe.wait_ge(loaded[3].sem, 16)
            pe.wait_ge(*setv(0, "bo"))

            def normalised(i, t, s, src, bc_, bv_, sq_step="sq"):
                mm(bank[bc_][:, :], W("center"), src[:, :]).then_inc(t.sem, 1)
                pe.wait_ge(*s(i, sq_step))
                mm(bank[bv_][:, :], W("mean"), sq[:, :]).then_inc(t.sem, 1)

            def prepare(i):
                taps = ((0, 2), (TAPS - 1, TAPS + 1))
                pe.wait_ge(*x_v(i, "high"))
                pe.wait_ge(*x_s(i, "low"))
                for d in range(2):
                    o = bank[d][:, :].rearrange("p (s t) -> p s t", s=GSEQ)
                    for q in range(2):
                        last = mm(o, conv_w[:, 2 * d + q, :], xpad[:, :, taps[d][q]:taps[d][q] + S],
                                  start=(q == 0), stop=(q == 1))
                    last.then_inc(prep_t.sem, 1)
                    mm(bank[2 + d][:, :].rearrange("p (s t) -> p s t", s=GSEQ), W("inz", lo)[:, d * P:(d + 1) * P],
                       xpad[lo, :, TAPS - 1:TAPS - 1 + S]).then_inc(prep_t.sem, 1)
                for d in range(2):
                    pe.wait_ge(*prep_s(i, f"z{d}"))
                    mm(bank[d][:, :], W("bc_w")[:, d * P:(d + 1) * P], u[d][:, :]).then_inc(prep_t.sem, 1)
                    mm(bank[2 + d][:, :], delta_w[:, d, :], u[d][:, :]).then_inc(prep_t.sem, 1)

            def scans(i):
                LAG = 3

                def rows_out(m):
                    d, n = divmod(m, NSTATE)
                    if n == 0:
                        pe.wait_ge(*prep_v(i, f"low{d}"))
                    if m < 4:
                        pe.wait_ge(*prep_v(i, "du1"))
                    pe.wait_ge(*drive_ready(i, max(m - 1, 0)))
                    pe.wait_ge(*c_ready(i, max(m - 1, 0)))
                    mm(bank[m % 2][:, :], sel[:, n:n + 1].to_broadcast([P, P]), bc[d][:, :])
                    mm(bank[2 + m % 2][:, :], sel[:, NSTATE + n:NSTATE + n + 1].to_broadcast([P, P]),
                       bc[d][:, :]).then_inc(bc_ready.sem, 1)

                def summed(m):
                    d, n = divmod(m, NSTATE)
                    if m == NSTATE:
                        pe.wait_ge(*y_ready(i, "y0"))
                    pe.wait_ge(*hc_ready(i, m + 1))
                    mm(bank[4][:, :], W("ident"), hc[m % RING][:, :], start=(n == 0), stop=False)\
                        .then_inc(sum_done.sem, 1)
                    if n == NSTATE - 1:
                        mm(bank[4][:, :], skip_w[:, d, :], u[d][:, :], start=False).then_inc(y_sum.sem, 1)

                for m in range(NM + LAG):
                    if m < NM:
                        rows_out(m)
                    if m >= LAG:
                        summed(m - LAG)

            def combine(i):
                pe.wait_ge(*y_ready(i, "y1"))
                pe.wait_ge(*c_ready(i, NM))
                mm(bank[0][:, :].rearrange("p (s t) -> p s t", s=GSEQ), W("centerd", lo),
                   xpad[lo, :, TAPS - 1:TAPS - 1 + S], stop=False)
                for d in range(2):
                    last = mm(bank[0][d * D:(d + 1) * D, :], out_w[:, d, :], y[d][:, :], start=False)
                last.then_inc(comb_t.sem, 1)
                pe.wait_ge(*comb_s(i, "sq"))
                mm(bank[1][:, :], W("mean2"), sq[:, :]).then_inc(comb_t.sem, 1)
                pe.wait_ge(*comb_v(i, "fb"))
                for c in range(2):
                    mm(bank[2 + c][:, :], ff_w1[:, c * P:(c + 1) * P], fb[:, :]).then_inc(comb_t.sem, 1)
                for c in range(2):
                    pe.wait_ge(*comb_s(i, f"g{c}"))
                    last = mm(bank[0][:, :], W("ff_w2")[:, c * P:(c + 1) * P], f1[:, c, :], start=(c == 0),
                              stop=(c == 1))
                last.then_inc(comb_t.sem, 1)

            def experts(i, m, src):
                t, s, v = mt[m], ms[m], mv[m]
                normalised(i, t, s, src, 5, 6)
                pe.wait_ge(*v(i, "xa"))
                if m == 0:
                    pe.wait_ge(*v(i, "xb"))
                wr = W("e0_wr", lo) if m == 0 else W("e1_wg", lo)
                for b in range(TILES):
                    last = mm(bank[6][:, b * NE:(b + 1) * NE], xa[lo, b * P:(b + 1) * P], wr)
                last.then_inc(t.sem, 1)
                pe.wait_ge(*v(i, "gate"))
                for b in range(TILES):
                    last = mm(bank[7][0:NE, b * P:(b + 1) * P], gate[:, b, :], W("ident"))
                last.then_inc(t.sem, 1)
                ch = NC[m] // NE
                x = (xb, xa)[m]

                def up(c):
                    e, half = divmod(c, ch) if m == 0 else (c % 4, c // 4)
                    r = slice(half * D, (half + 1) * D)
                    w = e0_w1[r, e, :] if m == 0 else W("e1_w1", r)[:, e * P:(e + 1) * P]
                    if c >= 2:
                        pe.wait_ge(*gelu_ready[m](i, c - 1))
                    mm(bank[5 + c % 2][:, :], w, x[r, :]).then_inc(hid_ready[m].sem, 1)

                def down(e):
                    pe.wait_ge(*gelu_ready[m](i, (e + 1) * ch))
                    if e < 4:
                        pe.wait_ge(*v(i, "gate_t"))
                    else:
                        pe.wait_ge(*yg_ready[m](i, e // 2 - 1))
                    w2 = W("e0_w2") if m == 0 else W("e1_w2")
                    for b in range(TILES):
                        at_ = (e % 2) * TILES * D + b * D
                        for c in range(ch):
                            n = (e * ch + c) * D
                            last = mm(bank[YB[e // 2 % 2]][:, at_:at_ + D], hid[(e * ch + c) % RING][:, b * P:(b + 1) * P],
                                      w2[:, n:n + D], start=(c == 0), stop=(c == ch - 1))
                    last.then_inc(down_done[m].sem, 1)

                for e in range(NE + 1):
                    if e < NE:
                        for c in range(ch):
                            up(e * ch + c)
                    if e >= 1:
                        down(e - 1)
                pe.wait_ge(*v(i, "add3"))
                if m == 0:
                    mm(bank[5][:, :], W("e0_b2", slice(0, NE)), gate_t[:, :], stop=False)
                    for b in range(TILES):
                        last = mm(bank[5][:, b * P:(b + 1) * P], acc2[:, b, :], W("ident"), start=False,
                                  stop=(b == TILES - 1))
                else:
                    for b in range(TILES):
                        o = bank[5][:, b * D:(b + 1) * D]
                        mm(o, gate_t[:, b * P:(b + 1) * P], W("e1_b2", slice(0, NE)), stop=False)
                        last = mm(o, src[lo, b * P:(b + 1) * P], W("ident", lo)[:, 0:D], start=False)
                last.then_inc(t.sem, 1)

            def attention(i):
                normalised(i, att_t, att_s, h2, 5, 6)
                pe.wait_ge(*att_s(i, "xg"))
                mm(bank[5][:, :], W("at_wq", lo), xg[lo, :]).then_inc(att_t.sem, 1)
                mm(bank[6][:, :], W("at_wk", lo), xg[lo, :]).then_inc(att_t.sem, 1)
                for b in range(TILES):
                    last = mm(bank[7][:, b * D:(b + 1) * D], xg[lo, b * P:(b + 1) * P], W("at_wv", lo))
                last.then_inc(att_t.sem, 1)
                pe.wait_ge(*att_s(i, "qv"))
                pe.wait_ge(*att_v(i, "v"))
                for j in range(NU):
                    b, h = divmod(j, NH)
                    r = slice(32 * h, 32 * h + HD)
                    first = P if b % 2 == 0 else 0
                    if j >= 3:
                        pe.wait_ge(*es_ready(i, j - 2))
                    mm(bank[5 + j % 3][:, 0:SKEW], qv[r, b * P:(b + 1) * P], pos[r, first:first + SKEW])\
                        .then_inc(e_ready.sem, 1)
                pe.wait_ge(*es_ready(i, NU))

                def scores(b):
                    for h in range(NH):
                        j = b * NH + h
                        r = slice(32 * h, 32 * h + HD)
                        if j >= 2:
                            pe.wait_ge(*ss_ready(i, j - 1))
                        mm(bank[SB[j % 2]][:, 0:S], qu[r, b * P:(b + 1) * P],
                           kk[r, (b // 2) * S:(b // 2 + 1) * S]).then_inc(s_ready.sem, 1)

                def context(s):
                    for h in range(NH):
                        n = s * NH + h
                        pe.wait_ge(*p_ready(i, (2 * s + 1) * NH + h + 1))
                        pe.wait_ge(*ptc_ready(i, max(n - 1, 0)))
                        for a in range(2):
                            for q in range(2):
                                last = pe.transpose(bank[TB[n % 2]][:, a * S + q * P:a * S + (q + 1) * P],
                                                    pb[:, q * NH + h, a * P:(a + 1) * P], W("ident"))
                        last.then_inc(pt_ready.sem, 1)
                        if h >= 1:
                            weighted(s, h - 1)
                    weighted(s, NH - 1)

                def weighted(s, h):
                    n = s * NH + h
                    pe.wait_ge(*ptc_ready(i, n + 1))
                    for q in range(2):
                        at_ = (2 * s + q) * D + h * HD
                        for a in range(2):
                            last = mm(bank[7][:, at_:at_ + HD], ptc[n % 2][:, a, q * P:(q + 1) * P],
                                      vv[:, 2 * s + a, h * HD:(h + 1) * HD], start=(a == 0), stop=(a == 1))
                    last.then_inc(ctx_ready.sem, 1)

                scores(0)
                scores(1)
                context(0)
                scores(2)
                scores(3)
                context(1)
                pe.wait_ge(*att_v(i, "cn"))
                for b in range(TILES):
                    last = mm(bank[5][0:D, b * P:(b + 1) * P], cn[:, b * D:(b + 1) * D], W("ident"))
                last.then_inc(att_t.sem, 1)
                pe.wait_ge(*att_s(i, "ctx_t"))
                mm(bank[6][:, :], W("at_wo", lo), ct).then_inc(att_t.sem, 1)

            with pe.Fori(0, NG) as i:
                pe.wait_ge(*x_s(i, "h0"))
                normalised(i, x_t, x_s, h0, 0, 1)
                prepare(i)
                scans(i)
                combine(i)
                pe.wait_ge(*comb_v(i, "h1"))
                experts(i, 0, h1)
                pe.wait_ge(*mv[0](i, "h"))
                attention(i)
                pe.wait_ge(*att_v(i, "h"))
                experts(i, 1, h3)


def host_arrays(a):
    f = np.float32
    part = {}

    def put(name, rows, value):
        k, at, n = places()[name]
        value = np.asarray(value, f)
        part.setdefault(k, np.zeros((P, WIDTHS[k]), f))[rows, at:at + n] = value.reshape(value.shape[0], n)

    def col(v, times=1):
        return np.tile(np.asarray(v, f).reshape(-1), times)[:, None]

    every, lo, hi = slice(0, P), slice(0, D), slice(D, P)
    for c in range(NG):
        r = slice(32 * c, 32 * c + FD)
        per, harm, kind = np.meshgrid(np.arange(4), np.arange(HARM), np.arange(2), indexing="ij")
        put("invp", r, col(1.0 / np.array(PERIODS)[per]))
        put("harm", r, col(harm + 1.0))
        put("phase", r, col(a["L0_tok_ph"][per, harm]))
        put("amp", r, col(a["L0_tok_hw"][per, harm]))
        put("quarter", r, col(0.25 * kind))
        put("halfpi", r, col(0.5 * math.pi * kind))
        put("tok_w1", r, a["L0_tok_W1"])
        put("tok_wres", r, np.tile(a["L0_tok_Wres"], (1, 2)))
    put("tok_b1", every, col(a["L0_tok_b1"]))
    put("tok_b2", every, col(a["L0_tok_b2"], 2))
    put("tok_g", every, col(a["L0_tok_gamma"], 2))
    put("tok_b", every, col(a["L0_tok_beta"], 2))
    put("tok_bres", every, col(a["L0_tok_bres"], 2))
    put("tok_w2", every, np.tile(a["L0_tok_W2"], (1, 2)))
    cen = np.eye(D) - 1.0 / D
    zero = np.zeros((D, D))
    put("center", every, np.eye(P) - 1.0 / P * np.ones((P, P)))
    put("mean", every, np.full((P, P), 1.0 / P))
    put("ident", every, np.eye(P))
    put("mean2", every, np.kron(np.eye(2), np.full((D, D), 1.0 / D)))
    put("center2", every, np.block([[cen, zero], [zero, cen]]))
    put("centerd", lo, np.tile(cen, (1, 2)))
    put("centers", every, np.tile(cen, (2, 1)))

    m = {k[len("L0_attn_mamba_"):]: v for k, v in a.items() if k.startswith("L0_attn_mamba_")}
    both = lambda fn: np.concatenate([fn(d) for d in range(2)], axis=1)
    inner = 2 * D
    put("inx", every, both(lambda d: m["in_w"][d, :inner]))
    put("conv_w", every, both(lambda d: m["conv_w"][d]))
    put("conv_b", every, m["conv_b"].T)
    put("inz", lo, both(lambda d: m["in_w"][d, inner:].T))
    put("bc_w", every, both(lambda d: np.tile(m["xproj_w"][d, RANK:].T, (1, 4))))
    put("xp_dt", slice(0, RANK), both(lambda d: m["xproj_w"][d, :RANK]))
    put("dt_w", slice(0, RANK), both(lambda d: m["dt_w"][d].T))
    put("dt_b", every, m["dt_b"].T)
    put("alog", every, both(lambda d: m["Alog"][d]))
    put("dskip", every, m["D"].T)
    put("out_w", every, m["out_w"].reshape(P, P))
    for name, key in (("g", "gamma"), ("b", "beta"), ("m", "mean"), ("v", "var")):
        v = a["L0_attn_bn_" + key]
        put("bn_" + name, every, col(v[:2]))
        put("bn2_" + name, every, col(v[2], 2))
    put("ln_g", every, col(a["L0_attn_ln_gamma"][:2]))
    put("ln_b", every, col(a["L0_attn_ln_beta"][:2]))
    put("ff_w1", every, np.tile(a["L0_attn_ff_w1"].T, (2, 1)))
    put("ff_b1", every, a["L0_attn_ff_b1"].reshape(2, P).T)
    put("ff_w2", every, np.concatenate([np.tile(a["L0_attn_ff_w2"].T[c * P:(c + 1) * P], (1, 2)) for c in range(2)], 1))
    put("ff_b2", every, col(a["L0_attn_ff_b2"], 2))

    put("tri", every, np.tile(np.tril(np.ones((NE, NE)), -1).reshape(1, -1), (P, 1)))
    e = {k[len("L0_ffn_"):]: v for k, v in a.items() if k.startswith("L0_ffn_")}
    for c, r in enumerate((lo, hi)):
        put("e0_w1", r, e["W1"][:, :, c * P:(c + 1) * P].transpose(1, 0, 2))
    put("e0_g", every, np.tile(e["ln_g"].T, (2, 1)))
    put("e0_lb", every, np.tile(e["ln_b"].T, (2, 1)))
    put("e0_b1", every, e["b1"].reshape(NE * CH0, P).T)
    put("e0_w2", every, e["W2"].reshape(NE * CH0, P, D).transpose(1, 0, 2))
    put("e0_b2", slice(0, NE), np.tile(e["b2"], (1, 2)))
    put("e0_wr", lo, e["Wr"])
    put("e0_br", every, np.tile(e["br"], (P, 1)))

    t = {k[len("L1_attn_"):]: v for k, v in a.items() if k.startswith("L1_attn_")}

    def padded(v):
        v = np.asarray(v, f).reshape(NH, HD, -1)
        return np.concatenate([v, np.zeros_like(v)], axis=1).reshape(P, -1)

    put("at_g", lo, col(t["ln_gamma"]))
    put("at_b", lo, col(t["ln_beta"]))
    for name, key in (("wq", "Wq"), ("wk", "Wk"), ("wp", "Wpos")):
        put("at_" + name, lo, padded(t[key]).T)
    for name, key in (("bq", "bq"), ("bk", "bk"), ("bp", "bpos"), ("u", "u_bias"), ("v", "v_bias")):
        put("at_" + name, every, padded(t[key]))
    put("at_wv", lo, t["Wv"].T)
    put("at_wo", lo, np.tile(t["Wo"].T, (1, 2)))
    put("at_bv", lo, col(t["bv"]))
    put("at_bo", every, col(t["bo"], 2))
    dist = np.clip(np.arange(2 * S - 1) - (S - 1), -MAXREL, MAXREL) + MAXREL
    div = np.exp(np.arange(0, D, 2, dtype=f) * f(-math.log(10000.0) / D)).astype(f)
    ang = dist.astype(f)[:, None] * div
    put("enc", lo, np.stack([np.sin(ang), np.cos(ang)], axis=-1).reshape(-1, D).T)

    g = {k[len("L1_ffn_"):]: v for k, v in a.items() if k.startswith("L1_ffn_")}
    for c, r in enumerate((lo, hi)):
        put("e1_w1", r, g["W1"][c * 4:(c + 1) * 4].transpose(1, 0, 2))
    put("e1_b1", every, g["b1"].T)
    put("e1_w2", every, g["W2"].transpose(1, 0, 2))
    put("e1_b2", slice(0, NE), g["b2"])
    put("e1_wg", lo, g["Wg"])
    put("e1_bg", every, np.tile(g["bg"], (P, 1)))

    tokens = np.stack([a["x"], a["itok_BS_0_23"], a["itok_BS_0_11"], a["itok_BS_0_30"]]).reshape(4, NG, T)
    idx = np.zeros((NG, 32, T), np.int32)
    idx[:, :FD] = np.repeat(tokens.transpose(1, 0, 2), FD // 4, axis=1)
    sel = np.eye(P, 2 * NSTATE) + np.eye(P, 2 * NSTATE, -64) + np.eye(P, 2 * NSTATE, -96)
    return idx.reshape(P, T), part[0], part[1], part[2], sel


def kernel(**inputs):
    import ml_dtypes
    import concourse.bacc as bacc
    from concourse.bass_utils import run_bass_kernel_spmd

    a = {k: np.asarray(v) for k, v in inputs.items()}
    idx, w0, w1, w2, sel = host_arrays(a)
    arrays = {"idx_dram": idx, "w0_dram": w0, "w1_dram": w1, "w2_dram": w2, "sel_dram": sel.astype(ml_dtypes.bfloat16)}
    nc = bacc.Bacc("TRN2", target_bir_lowering=False, num_devices=1)
    ins = [nc.dram_tensor(n, v.shape, mybir.dt.from_np(v.dtype), kind="ExternalInput").ap() for n, v in arrays.items()]
    out = nc.dram_tensor("out_dram", (NG, P, TILES, D), F32, kind="ExternalOutput").ap()
    tower(nc, *ins, out)
    r = run_bass_kernel_spmd(nc, [arrays], core_ids=[0])
    got = np.asarray(r.results[0]["out_dram"])
    return got.transpose(0, 2, 1, 3).reshape(NSEQ, S, D)
```

```python
import math
from contextlib import ExitStack

import numpy as np
import concourse.bass as bass
from concourse import mybir

F32 = mybir.dt.float32
BF16 = mybir.dt.bfloat16
I32 = mybir.dt.int32
ALU = mybir.AluOpType
ACT = mybir.ActivationFunctionType
AX = mybir.AxisListType

D, S, NSEQ = 64, 256, 8
GSEQ = 2
T = GSEQ * S
NG = NSEQ // GSEQ
P = 128
TILES = T // P
HARM, PERIODS = 3, (7.0, 24.0, 12.0, 1.0)
FD = len(PERIODS) * 2 * HARM
TAPS, NSTATE, RANK = 4, 16, 4
PADW = S + 2 * (TAPS - 1)
NE, CH0 = 8, 2
NH, HD, MAXREL = 4, 16, 30
SKEW = P + S - 1
EPS = 1e-5
TWO_PI = 2.0 * math.pi
TURN = (6.28125, 0.0019350051879882812, 3.0199159819574e-07)
ROUND = 12582912.0
PI_LO = 3.1415925
RING = 4

PACKED = [
    [("invp", 1), ("harm", 1), ("phase", 1), ("quarter", 1), ("halfpi", 1), ("amp", 1), ("tok_b1", 1),
     ("tok_b2", 1), ("tok_g", 1), ("tok_b", 1), ("tok_bres", 1), ("tok_w1", P), ("tok_w2", P), ("tok_wres", P),
     ("center", P), ("mean", P)],
    [("ident", P), ("mean2", P), ("center2", P), ("centerd", P), ("centers", D),
     ("inx", 2 * D), ("conv_w", 2 * TAPS), ("conv_b", 2), ("inz", 2 * P), ("bc_w", 2 * P), ("xp_dt", 2 * P),
     ("dt_w", 2 * P), ("dt_b", 2), ("alog", 2 * NSTATE), ("dskip", 2), ("out_w", P), ("bn_g", 1), ("bn_b", 1),
     ("bn_m", 1), ("bn_v", 1), ("bn2_g", 1), ("bn2_b", 1), ("bn2_m", 1), ("bn2_v", 1), ("ln_g", 1), ("ln_b", 1),
     ("ff_w1", 2 * P), ("ff_b1", 2), ("ff_w2", 2 * P), ("ff_b2", 1)],
    [("tri", NE * NE), ("e0_w1", NE * P), ("e0_g", NE), ("e0_lb", NE), ("e0_b1", NE * CH0),
     ("e0_w2", NE * CH0 * D), ("e0_b2", P), ("e0_wr", NE), ("e0_br", NE),
     ("at_g", 1), ("at_b", 1), ("at_wq", P), ("at_wk", P), ("at_wp", P), ("at_bq", 1), ("at_bk", 1), ("at_bp", 1),
     ("at_u", 1), ("at_v", 1), ("at_wv", D), ("at_wo", P), ("at_bv", 1), ("at_bo", 1), ("enc", 2 * S - 1), ("heads", NH), ("heads_q", NH),
     ("e1_w1", NE // 2 * P), ("e1_b1", NE), ("e1_w2", NE * D), ("e1_b2", D), ("e1_wg", NE), ("e1_bg", NE)],
]
WIDTHS = [sum(n for _, n in part) for part in PACKED]


def places():
    out = {}
    for k, part in enumerate(PACKED):
        at = 0
        for name, n in part:
            out[name] = (k, at, n)
            at += n
    return out


class Signal:

    def __init__(self, sem, steps):
        self.sem, self.steps = sem, steps

    def __call__(self, i, step):
        n = step if isinstance(step, int) else self.steps.index(step) + 1
        return self.sem, i * len(self.steps) + n


def tower(nc, idx, w0, w1, w2, sel_in, out):
    where = places()
    ctx = ExitStack()
    with ctx:
        def sb(name, shape, dt=F32):
            return ctx.enter_context(nc.sbuf_tensor(name, shape, dt))

        def signal(name, steps):
            return Signal(ctx.enter_context(nc.semaphore(name)), steps)

        bank = [ctx.enter_context(nc.psum_tensor(f"bank{b}", [P, T], F32)) for b in range(8)]
        packed = [sb(f"packed{k}", [P, n]) for k, n in enumerate(WIDTHS)]

        def W(name, rows=slice(0, P)):
            k, at, n = where[name]
            return packed[k][rows, at:at + n]

        h_all = sb("h_all", [P, NG * T])
        sel = sb("sel", [P, 2 * NSTATE], BF16)

        conv_w = sb("conv_w", [P, 4, P])
        eps_c = sb("eps_c", [P, 2])
        tok_bias = sb("tok_bias", [P, 1])
        bn2_d = sb("bn2_d", [P, 1])
        eps1, eps2 = eps_c[:, 0:1], eps_c[:, 1:2]
        delta_w = sb("delta_w", [P, 2, P])
        skip_w = sb("skip_w", [P, 2, P])
        a_neg = sb("a_neg", [P, 2 * NSTATE])
        bn_s, bn_t, bn2_s, bn2_t = (sb(n, [P, 1]) for n in ("bn_s", "bn_t", "bn2_s", "bn2_t"))
        out_s = sb("out_s", [P, P])
        out_w = sb("out_w", [P, 2, D])
        cen_t = sb("cen_t", [P, 1])
        ff_w1 = sb("ff_w1", [P, 2 * P])
        ff_b1 = sb("ff_b1", [P, 2])
        e0_w1 = W("e0_w1").rearrange("p (e n) -> p e n", e=NE)
        e0_b1 = sb("e0_b1", [P, NE * CH0])
        pos = sb("pos", [P, 2 * S - 1])
        bq_u, bq_v, bo_v = (sb(n, [P, 1]) for n in ("bq_u", "bq_v", "bo_v"))

        h0 = sb("h0", [P, T])
        sq, rs, rs2 = sb("sq", [P, T]), sb("rs", [P, T]), sb("rs2", [P, T])
        conv_s = sq[:, :].rearrange("p (q n) -> p q n", q=4)
        xpad = sb("xpad", [P, GSEQ, PADW])
        hx = sb("hx", [P, T])
        u = [sb(f"u{d}", [P, T]) for d in range(2)]
        z = [sb(f"z{d}", [P, T]) for d in range(2)]
        bc = [sb(f"bc{d}", [P, T], BF16) for d in range(2)]
        delta = [sb(f"delta{d}", [P, T]) for d in range(2)]
        du = [sb(f"du{d}", [P, T]) for d in range(2)]
        decay = [[sb(f"decay{d}_{r}", [P, T]) for r in range(RING)] for d in range(2)]
        drive = [sb(f"drive{r}", [P, T]) for r in range(2)]
        state = [sb(f"state{r}", [P, T]) for r in range(RING)]
        c_sb = [sb(f"c_sb{r}", [P, T]) for r in range(RING)]
        hc = [sb(f"hc{r}", [P, T]) for r in range(RING)]
        y = z
        xf, fb = drive
        ab, soft, rest = state[:3]
        sqm, rsm = hc[:2]
        f1 = c_sb[:2]
        idx_i = fb[:, :].bitcast(I32)
        h1, h2, h3 = sb("h1", [P, T]), sb("h2", [P, T]), sb("h3", [P, T])
        angle, turns, feat = h1, h2, h3

        xa = sb("xa", [P, T])
        x_half = [sb(f"x_half{r}", [P, T]) for r in range(2)]
        lg, ls, ex, wt, gate = (sb(n, [P, TILES, NE]) for n in ("lg", "ls", "ex", "wt", "gate"))
        gt, eq = sb("gt", [P, TILES, NE, NE]), sb("eq", [P, TILES, NE, NE])
        rank = sb("rank", [P, TILES, NE])
        mx, sw, rw = (sb(n, [P, TILES]) for n in ("mx", "sw", "rw"))
        gate_t = sb("gate_t", [NE, T])
        yg = sb("yg", [P, NE, TILES * D])
        acc2 = sb("acc2", [P, TILES, P])
        acc = acc2[:, 0:2, :].rearrange("p a n -> p (a n)")
        held = sb("held", [P, TILES * NH])
        fin = sb("fin", [P, TILES, D])

        qu = xa
        qv, kk = ([sb(f"{n}{h}", [P, T]) for h in range(NH)] for n in ("qv", "kk"))
        bq_vh = sb("bq_vh", [P, NH])
        xg = sb("xg", [P, T])
        vv = sb("vv", [P, TILES, D])
        es = [sb(f"es{r}", [P, NH, SKEW]) for r in range(2)]
        hid = [es[r // 2][:, :, :].rearrange("p h n -> p (h n)")[:, r % 2 * T:(r % 2 + 1) * T] for r in range(RING)]
        ps = sb("ps", [P, TILES, NH, S])
        early = ps[:, :, :, :].rearrange("p b h s -> p (b h s)").rearrange("p (a c t) -> p a c t", a=2, c=NG)
        tok_h, tok_sq = early[:, 0], early[:, 1]
        tok_rs = yg[:, :, :].rearrange("p e n -> p (e n)").rearrange("p (c t) -> p c t", c=NG)
        ss = [xg[:, 0:S], xg[:, S:T], *(r[:, :, :, :].rearrange("p b e f -> p (b e f)") for r in (gt, eq))]
        smin, ssum, rsum = (sb(n, [P, TILES * NH]) for n in ("smin", "ssum", "rsum"))
        pb = yg
        ptc = [sb(f"ptc{r}", [P, 2, S]) for r in range(2)]
        cn = sb("cn", [P, TILES, 2, D])
        ct = sb("ct", [P, T])
        skew = nc.dram_tensor("skew", [TILES, P, NH, SKEW], F32, kind="Internal").ap()

        loaded = [signal(f"loaded{k}", ["done"]) for k in range(5)]
        tokv = signal("tok_vector", ["eps", "bias", "t", "norm", "angle", "k", "kr", "r1", "r2", "r3", "r4", "r5", "feat",
                                     *(f"xn{c}" for c in range(NG)), *(f"h{c}" for c in range(NG))])
        toks = signal("tok_scalar", ["sin", *(f"{s}{c}" for s in ("relu", "h2_", "sq", "ln", "rs", "aff")
                                              for c in range(NG))])
        tokp = signal("tok_tensor", [f"{s}{c}" for s in ("w1_", "w2_", "cen", "var", "res") for c in range(NG)])
        setg = signal("setup_pool", ["pad", "zero"])
        setv = signal("setup_vector", ["taps", "aneg", "bns", "bnt0", "bnt", "bn2d", "bn2s", "bn2t0", "bn2t", "outs", "skip",
                                       "sums", "ffw", "convw", "deltaw", "outw", "cent", "ffb", "e0b", "e0w",
                                       "pos", "bqv", "bo"])
        sets = signal("setup_scalar", ["alog", "ln", "rsq", "ln2", "rsq2"])
        setp = signal("setup_tensor", ["conv", "delta", "outw", "cent", "ffb", "e0b", "pos", "bo"])

        x_t = signal("x_tensor", ["center", "var"])
        x_s = signal("x_scalar", ["h0", "sq", "ln", "rs", "low"])
        x_v = signal("x_vector", ["x", "high", "hx"])
        prep_t = signal("prep_tensor", ["conv0", "z0", "conv1", "z1", "bc0", "dt0", "bc1", "dt1"])
        prep_s = signal("prep_scalar", ["u0", "z0", "u1", "z1",
                                     *(f"{s}{d}" for d in range(2) for s in ("part", "abs", "relu", "exp", "ln"))])
        prep_v = signal("prep_vector", [f"{s}{d}" for d in range(2) for s in ("rest", "mid", "low", "delta", "du")])
        NM = 2 * NSTATE
        bc_ready = signal("bc_ready", list(range(NM)))
        decay_ready = signal("decay_ready", list(range(NM)))
        c_ready = signal("c_ready", list(range(NM)))
        drive_ready = signal("drive_ready", list(range(NM)))
        state_ready = signal("state_ready", list(range(NM)))
        hc_ready = signal("hc_ready", list(range(NM)))
        pair_ready = signal("pair_ready", list(range(NSTATE)))
        sum_done = signal("sum_done", list(range(NM)))
        y_sum = signal("y_sum", ["y0", "y1"])
        y_ready = signal("y_ready", ["y0", "y1"])
        comb_t = signal("out_tensor", ["center", "var", "f0", "f1", "ff"])
        comb_s = signal("out_scalar", ["sq", "ln", "rs", "g0", "g1"])
        comb_v = signal("out_vector", ["fb", "h1"])

        route = ["logits", "max", "shift", "gt", "eq", "tie", "sum", "rank"]
        mt = [signal("moe0_tensor", ["center", "var", "logits", "gate_t", "sum"]),
              signal("moe1_tensor", ["center", "var", "logits", "gate_t", "sum"])]
        ms = [signal("moe0_scalar", ["sq", "ln", "rs", "ln2", "rs2", "exp"]),
              signal("moe1_scalar", ["sq", "ln", "rs"])]
        mv = [signal("moe0_vector", ["xa", "x0", "x1", *route, "masked", "wsum", "wrec", "gate", "add1",
                                     "gate_t", "add2", "add3", "h"]),
              signal("moe1_vector", ["x0", "x1", "logits", *route[3:], "gate", "add1", "gate_t", "add2", "add3", "h"])]
        NC = [NE * CH0, NE]
        down_done = [signal(f"down_done{m}", list(range(NE))) for m in range(2)]
        hid_ready = [signal(f"hid_ready{m}", list(range(NC[m]))) for m in range(2)]
        gelu_ready = [signal(f"gelu_ready{m}", list(range(NC[m]))) for m in range(2)]
        yg_ready = [signal(f"yg_ready{m}", list(range(NE // 2))) for m in range(2)]
        RB, YSUM = (0, 1, 2), 3
        XB, VB, LB, UB, YB = (7, 5), (4, 6), 4, (6, 5), (7, 4)
        EB, SB, TB, CB = (6, 7), (4, 5), 6, 7
        LAG, EARLY = 3, 4
        E_AT, S_AT, P_AT, T_AT, END = 5, 13, 14, (21, 27), 32

        NU = TILES * NH
        att_t = signal("attn_tensor", ["center", "var", "q", "k", "v", "ctx_t", "out"])
        att_s = signal("attn_scalar", ["sq", "ln", "rs", "xg", *(f"qv{h}" for h in range(NH)), "qu", "ctx_t"])
        att_v = signal("attn_vector", ["xn", "k", "v", "rsum", "cn", "h"])
        e_ready = signal("e_ready", list(range(NU)))
        es_ready = signal("es_ready", list(range(NU)))
        s_ready = signal("s_ready", list(range(NU)))
        ss_ready = signal("ss_ready", list(range(NU)))
        p_ready = signal("p_ready", list(range(NU)))
        pt_ready = signal("pt_ready", list(range(GSEQ * NH)))
        ptc_ready = signal("ptc_ready", list(range(GSEQ * NH)))
        ctx_ready = signal("ctx_ready", list(range(GSEQ * NH)))
        skew_out = [signal(f"skew_out{b}", list(range(16))) for b in range(TILES)]
        skew_in = [signal(f"skew_in{b}", list(range(16))) for b in range(TILES)]
        stored = signal("stored", list(range(16)))

        block = ctx.enter_context(nc.Block())

        @block.sync
        def _(sp):
            for k, (dst, src) in enumerate([(idx_i, idx), (packed[0], w0), (packed[1], w1), (sel, sel_in),
                                            (packed[2], w2)]):
                sp.dma_start(dst[:, :] if k else dst, src).then_inc(loaded[k].sem, 16)

            def skews(i):
                for b in range(TILES):
                    sp.wait_ge(*es_ready(i, NH * (b + 1)))
                    sp.dma_start(skew[b], es[b % 2][:, :, :]).then_inc(skew_out[b].sem, 16)
                    sp.wait_ge(*skew_out[b](i, 16))
                    rows = skew[b]
                    shifted = bass.AP(rows.tensor, rows.offset + P - 1,
                                      [[NH * SKEW - 1, P], [SKEW, NH], [1, S]])
                    sp.dma_start(ps[:, b, :, :], shifted).then_inc(skew_in[b].sem, 16)

            def store(i):
                sp.wait_ge(*mv[1](i, "h"))
                sp.dma_start(out[i], fin[:, :, :]).then_inc(stored.sem, 16)

            for i in range(NG):
                skews(i)
                store(i)
                sp.wait_ge(*stored(i, 16))

        @block.gpsimd
        def _(pool):
            pool.memset(xpad[:, :, :], 0.0).then_inc(setg.sem, 1)
            for d in range(2):
                edge = 0 if d == 0 else S - 1
                for r in range(RING):
                    v = decay[d][r][:, :].rearrange("p (s t) -> p s t", s=GSEQ)
                    last = pool.memset(v[:, :, edge:edge + 1], 0.0)
            last.then_inc(setg.sem, 1)

            def scan_outputs(i, paired):
                for m in range(NM):
                    pool.wait_ge(*state_ready(i, m + 1))
                    pool.wait_ge(*c_ready(i, m + 1))
                    if m >= RING and paired and m % 2 == 0:
                        pool.wait_ge(*pair_ready(i - 1, m // 2 - 1))
                    elif m >= RING:
                        pool.wait_ge(*sum_done(i, m + 1 - RING))
                    pool.tensor_tensor(hc[m % RING][:, :], state[m % RING][:, :], c_sb[m % RING][:, :],
                                       ALU.mult).then_inc(hc_ready.sem, 1)
                    if paired and m % 2 == 1:
                        pool.wait_ge(*hc_ready(i, m + 1))
                        pool.tensor_tensor(hc[m % RING][:, :], hc[m % RING][:, :], hc[(m - 1) % RING][:, :],
                                           ALU.add).then_inc(pair_ready.sem, 1)

            scan_outputs(0, False)
            with pool.Fori(1, NG) as i:
                scan_outputs(i, True)

        @block.scalar
        def _(act):
            def afn(out_, in_, fn, **kw):
                return act.activation(out_, in_, fn, **kw)

            act.wait_ge(*tokv(0, "r5"))
            afn(feat[:, :], angle[:, :], ACT.Sin).then_inc(toks.sem, 1)
            act.wait_ge(loaded[1].sem, 16)
            for c in range(NG):
                act.wait_ge(*tokp(0, f"w1_{c}"))
                afn(tok_h[:, c, :], bank[c][:, :], ACT.Relu, bias=W("tok_b1")).then_inc(toks.sem, 1)
            for c in range(NG):
                act.wait_ge(*tokp(0, f"w2_{c}"))
                afn(tok_h[:, c, :], bank[4 + c][:, :], ACT.Identity, bias=W("tok_b2")).then_inc(toks.sem, 1)
            for c in range(NG):
                act.wait_ge(*tokp(0, f"cen{c}"))
                afn(tok_sq[:, c, :], bank[c][:, :], ACT.Square).then_inc(toks.sem, 1)
            act.preload_act_table_set("natural_log_exp_and_others")
            act.wait_ge(*tokv(0, "bias"))
            for c in range(NG):
                act.wait_ge(*tokp(0, f"var{c}"))
                afn(tok_rs[:, c, :], bank[4 + c][:, :], ACT.Ln, bias=eps1).then_inc(toks.sem, 1)
            for c in range(NG):
                act.wait_ge(*toks(0, f"ln{c}"))
                afn(tok_rs[:, c, :], tok_rs[:, c, :], ACT.Exp, scale=-0.5).then_inc(toks.sem, 1)
            for c in range(NG):
                act.wait_ge(*tokv(0, f"xn{c}"))
                afn(tok_sq[:, c, :], tok_sq[:, c, :], ACT.Identity, scale=W("tok_g"), bias=tok_bias[:, :])\
                    .then_inc(toks.sem, 1)
            act.wait_ge(loaded[2].sem, 16)
            afn(a_neg[:, :], W("alog"), ACT.Exp).then_inc(sets.sem, 1)
            afn(bn_s[:, :], W("bn_v"), ACT.Ln, bias=eps1).then_inc(sets.sem, 1)
            act.wait_ge(*sets(0, "ln"))
            afn(bn_s[:, :], bn_s[:, :], ACT.Exp, scale=-0.5).then_inc(sets.sem, 1)
            afn(bn2_s[:, :], W("bn2_v"), ACT.Ln, bias=eps1).then_inc(sets.sem, 1)
            act.wait_ge(*sets(0, "ln2"))
            afn(bn2_s[:, :], bn2_s[:, :], ACT.Exp, scale=-0.5).then_inc(sets.sem, 1)
            act.wait_ge(*setg(0, "zero"))
            act.wait_ge(*setv(0, "bo"))

            def rsqrt(pe_sig, s_sig, i, b, ln="ln", rs_="rs", dst=rs, bias=None, scale=1.0):
                act.wait_ge(*pe_sig(i, "var"))
                afn(dst[:, :], bank[b][:, :], ACT.Ln, bias=bias, scale=scale).then_inc(s_sig.sem, 1)
                act.wait_ge(*s_sig(i, ln))
                afn(dst[:, :], dst[:, :], ACT.Exp, scale=-0.5).then_inc(s_sig.sem, 1)

            def take(i):
                afn(h0[:, :], h_all[:, bass.ds(i * T, T)], ACT.Copy).then_inc(x_s.sem, 1)

            def square_x(i):
                act.wait_ge(*x_t(i, "center"))
                afn(sqm[:, :], bank[3][:, :], ACT.Square).then_inc(x_s.sem, 1)

            def normalise_x(i):
                rsqrt(x_t, x_s, i, 2, dst=rsm, bias=eps1)
                act.wait_ge(*x_v(i, "x"))
                afn(xpad[0:D, :, TAPS - 1:TAPS - 1 + S], xf[:, :][0:D, :].rearrange("p (s t) -> p s t", s=GSEQ),
                    ACT.Copy).then_inc(x_s.sem, 1)

            def square(i, m):
                act.wait_ge(*mt[m](i, "center"))
                afn(sq[:, :], bank[XB[m]][:, :], ACT.Square).then_inc(ms[m].sem, 1)

            def normalise(i, m):
                t, s = mt[m], ms[m]
                rsqrt(t, s, i, VB[m], bias=eps1)
                if m == 0:
                    rsqrt(t, s, i, VB[m], "ln2", "rs2", rs2, bias=eps2, scale=1.0 + EPS)

            def prepare_silu(i):
                act.preload_act_table_set("silu_and_others")
                for d in range(2):
                    act.wait_ge(*prep_t(i, f"conv{d}"))
                    afn(u[d][:, :], bank[2 * d][:, :], ACT.Silu, bias=W("conv_b")[:, d:d + 1]).then_inc(prep_s.sem, 1)
                    act.wait_ge(*prep_t(i, f"z{d}"))
                    afn(z[d][:, :], bank[2 * d + 1][:, :], ACT.Silu).then_inc(prep_s.sem, 1)

            def prepare_delta(i, d):
                if True:
                    dtb = W("dt_b")[:, d:d + 1]
                    act.wait_ge(*prep_t(i, f"bc{d}"))
                    afn(bc[d][:, :], bank[2 * d][:, :], ACT.Copy).then_inc(prep_s.sem, 1)
                    act.wait_ge(*prep_t(i, f"dt{d}"))
                    if d:
                        act.wait_ge(*prep_v(i, "delta0"))
                    afn(ab[:, :], bank[2 * d + 1][:, :], ACT.Abs, bias=dtb).then_inc(prep_s.sem, 1)
                    afn(soft[:, :], bank[2 * d + 1][:, :], ACT.Relu, bias=dtb).then_inc(prep_s.sem, 1)
                    act.wait_ge(*prep_s(i, f"abs{d}"))
                    afn(ab[:, :], ab[:, :], ACT.Exp, scale=-1.0).then_inc(prep_s.sem, 1)
                    act.wait_ge(*prep_s(i, f"exp{d}"))
                    afn(ab[:, :], ab[:, :], ACT.Ln, bias=1.0).then_inc(prep_s.sem, 1)

            def scan_inputs(i, m):
                d, n = divmod(m, NSTATE)
                cut = slice(1, S) if d == 0 else slice(0, S - 1)
                if n == 0:
                    act.wait_ge(*prep_v(i, f"delta{d}"))
                if m >= RING:
                    act.wait_ge(*state_ready(i, m + 1 - RING))
                afn(decay[d][m % RING][:, :].rearrange("p (s t) -> p s t", s=GSEQ)[:, :, cut],
                    delta[d][:, :].rearrange("p (s t) -> p s t", s=GSEQ)[:, :, cut], ACT.Exp,
                    scale=a_neg[:, m:m + 1]).then_inc(decay_ready.sem, 1)
                act.wait_ge(*bc_ready(i, m + 1))
                if m >= RING:
                    act.wait_ge(*hc_ready(i, m + 1 - RING))
                afn(c_sb[m % RING][:, :], bank[RB[(2 * m + 1) % 3]][:, :], ACT.Copy).then_inc(c_ready.sem, 1)

            def combine_square(i):
                act.wait_ge(*comb_t(i, "center"))
                afn(sqm[:, :], bank[0][:, :], ACT.Square, bias=cen_t[:, :]).then_inc(comb_s.sem, 1)

            def combine_norm(i):
                rsqrt(comb_t, comb_s, i, 1, dst=rsm, bias=eps1)

            def combine_ff(i):
                for c in range(2):
                    act.wait_ge(*comb_t(i, f"f{c}"))
                    afn(f1[c][:, :], bank[1 + c][:, :], ACT.Relu, bias=ff_b1[:, c:c + 1]).then_inc(comb_s.sem, 1)

            def exp_logits(i):
                act.wait_ge(*mv[0](i, "shift"))
                afn(ex[:, :, :], ls[:, :, :], ACT.Exp).then_inc(ms[0].sem, 1)

            def hidden(i, m):
                act.preload_act_table_set("gelu_and_others")
                bias = (e0_b1[:, :], W("e1_b1"))[m]
                ch = NC[m] // NE
                for c in range(NC[m]):
                    act.wait_ge(*hid_ready[m](i, c + 1))
                    if c >= RING:
                        act.wait_ge(*down_done[m](i, (c - RING) // ch + 1))
                    afn(hid[c % RING], bank[UB[c % len(UB)]][:, :], ACT.Gelu, bias=bias[:, c:c + 1])\
                        .then_inc(gelu_ready[m].sem, 1)
                act.preload_act_table_set("natural_log_exp_and_others")

            def attention(i, k):
                if k == 0:
                    act.wait_ge(*att_t(i, "center"))
                    afn(sq[:, :], bank[5][:, :], ACT.Square).then_inc(att_s.sem, 1)
                if k == 1:
                    rsqrt(att_t, att_s, i, 6, bias=eps2, scale=1.0 + EPS)
                if k == 2:
                    act.wait_ge(*att_v(i, "xn"))
                    afn(xg[:, :], xg[:, :], ACT.Identity, scale=W("at_g"), bias=W("at_b")).then_inc(att_s.sem, 1)
                if k == 3:
                    act.wait_ge(*att_t(i, "q"))
                    for h in range(NH):
                        afn(qv[h][:, :], bank[5][:, :], ACT.Identity, scale=W("heads_q")[:, h:h + 1],
                            bias=bq_vh[:, h:h + 1]).then_inc(att_s.sem, 1)
                if k == 4:
                    afn(qu[:, :], bank[5][:, :], ACT.Identity, scale=-HD ** -0.5, bias=bq_u[:, :])\
                        .then_inc(att_s.sem, 1)
                j = k - E_AT
                if 0 <= j < NU:
                    b, h = divmod(j, NH)
                    act.wait_ge(*e_ready(i, j + 1))
                    if h == 0 and b >= 2:
                        act.wait_ge(*skew_out[b - 2](i, 16))
                    afn(es[b % 2][:, h, :], bank[EB[j % 2]][:, 0:SKEW], ACT.Copy).then_inc(es_ready.sem, 1)
                j = k - P_AT
                if 0 <= j < NU:
                    b, h = divmod(j, NH)
                    act.wait_ge(*ss_ready(i, j + 1))
                    if b >= 2:
                        act.wait_ge(*pt_ready(i, h + 1))
                    afn(pb[:, (b % 2) * NH + h, :], ss[h], ACT.Exp, scale=-1.0, bias=smin[:, j:j + 1],
                        accum_out=ssum[:, j:j + 1]).then_inc(p_ready.sem, 1)
                if k == END:
                    act.wait_ge(*att_t(i, "ctx_t"))
                    afn(ct[:, :], bank[5][:, :], ACT.Copy).then_inc(att_s.sem, 1)

            def inputs(after):
                take(after)
                square_x(after)
                normalise_x(after)
                prepare_silu(after)

            def start(i, after):
                if i is not None:
                    square(i, 0)
                if after is not None:
                    prepare_delta(after, 0)
                if i is not None:
                    normalise(i, 0)
                if after is not None:
                    prepare_delta(after, 1)
                if i is not None:
                    exp_logits(i)
                    hidden(i, 0)

            def together(before, i, after):
                for k in range(-EARLY, END + 2):
                    if i is not None and k + EARLY < NM:
                        scan_inputs(i, k + EARLY)
                    if i is not None and k == END:
                        combine_square(i)
                    if before is not None:
                        attention(before, k)
                if i is not None:
                    combine_norm(i)
                if before is not None:
                    square(before, 1)
                if i is not None:
                    combine_ff(i)
                if before is not None:
                    normalise(before, 1)
                if after is not None:
                    inputs(after)
                if before is not None:
                    hidden(before, 1)
                else:
                    act.preload_act_table_set("natural_log_exp_and_others")
                start(i, after)

            inputs(0)
            act.preload_act_table_set("natural_log_exp_and_others")
            start(None, 0)
            together(None, 0, 1)
            with act.Fori(1, NG - 1) as i:
                together(i - 1, i, i + 1)
            together(NG - 2, NG - 1, None)
            together(NG - 1, None, None)

        @block.vector
        def _(dve):
            for half in range(2):
                dve.memset(x_half[half][(1 - half) * D:(2 - half) * D, :], 0.0)
            dve.memset(eps_c[:, 0:1], EPS)
            dve.memset(eps_c[:, 1:2], EPS * EPS).then_inc(tokv.sem, 1)
            dve.wait_ge(loaded[0].sem, 16)
            dve.wait_ge(loaded[1].sem, 16)
            dve.tensor_scalar(tok_bias[:, :], W("tok_bres"), 0.1, W("tok_b"), ALU.mult, ALU.add).then_inc(tokv.sem, 1)
            dve.tensor_copy(angle[:, :], idx_i).then_inc(tokv.sem, 1)
            dve.wait_ge(*tokv(0, "t"))
            dve.tensor_scalar(angle[:, :], angle[:, :], TWO_PI, W("invp"), ALU.mult, ALU.mult).then_inc(tokv.sem, 1)
            dve.wait_ge(*tokv(0, "norm"))
            dve.tensor_scalar(angle[:, :], angle[:, :], W("harm"), W("phase"), ALU.mult, ALU.add)\
                .then_inc(tokv.sem, 1)
            dve.wait_ge(*tokv(0, "angle"))
            dve.tensor_scalar(turns[:, :], angle[:, :], 1.0 / TWO_PI, W("quarter"), ALU.mult, ALU.add)\
                .then_inc(tokv.sem, 1)
            dve.wait_ge(*tokv(0, "k"))
            dve.tensor_scalar(turns[:, :], turns[:, :], ROUND, ROUND, ALU.add, ALU.subtract).then_inc(tokv.sem, 1)
            for n, part in enumerate(TURN):
                dve.wait_ge(*tokv(0, ("kr", "r1", "r2")[n]))
                dve.scalar_tensor_tensor(out=angle[:, :], in0=turns[:, :], scalar=-part, in1=angle[:, :],
                                         op0=ALU.mult, op1=ALU.add).then_inc(tokv.sem, 1)
            dve.wait_ge(*tokv(0, "r3"))
            dve.tensor_scalar(angle[:, :], angle[:, :], W("halfpi"), PI_LO, ALU.add, ALU.min).then_inc(tokv.sem, 1)
            dve.wait_ge(*tokv(0, "r4"))
            dve.tensor_scalar(angle[:, :], angle[:, :], -PI_LO, None, ALU.max).then_inc(tokv.sem, 1)
            dve.wait_ge(*toks(0, "sin"))
            dve.tensor_scalar(feat[:, :], feat[:, :], W("amp"), None, ALU.mult).then_inc(tokv.sem, 1)
            for c in range(NG):
                dve.wait_ge(*toks(0, f"rs{c}"))
                dve.tensor_tensor(tok_sq[:, c, :], bank[c][:, :], tok_rs[:, c, :], ALU.mult).then_inc(tokv.sem, 1)
            for c in range(NG):
                dve.wait_ge(*toks(0, f"aff{c}"))
                dve.wait_ge(*tokp(0, f"res{c}"))
                dve.scalar_tensor_tensor(out=h_all[:, c * T:(c + 1) * T], in0=bank[4 + c][:, :], scalar=0.1,
                                         in1=tok_sq[:, c, :], op0=ALU.mult, op1=ALU.add).then_inc(tokv.sem, 1)

            dve.wait_ge(loaded[2].sem, 16)
            for d in range(2):
                for k in range(TAPS):
                    pair, half = divmod(k if d == 0 else TAPS - 1 - k, 2)
                    last = dve.tensor_scalar(conv_s[:, 2 * d + pair, half * D:(half + 1) * D],
                                             W("inx")[:, d * D:(d + 1) * D],
                                             W("conv_w")[:, d * TAPS + k:d * TAPS + k + 1], None, ALU.mult)
            last.then_inc(setv.sem, 1)
            dve.wait_ge(*sets(0, "rsq2"))
            dve.tensor_scalar(a_neg[:, :], a_neg[:, :], -1.0, None, ALU.mult).then_inc(setv.sem, 1)
            dve.tensor_scalar(bn_s[:, :], bn_s[:, :], W("bn_g"), None, ALU.mult).then_inc(setv.sem, 1)
            dve.wait_ge(*setv(0, "bns"))
            dve.tensor_scalar(bn_t[:, :], W("bn_m"), bn_s[:, :], -1.0, ALU.mult, ALU.mult).then_inc(setv.sem, 1)
            dve.wait_ge(*setv(0, "bnt0"))
            dve.tensor_scalar(bn_t[:, :], bn_t[:, :], W("bn_b"), None, ALU.add).then_inc(setv.sem, 1)
            dve.tensor_tensor(bn2_d[:, :], W("bn2_m"), W("ff_b2"), ALU.subtract).then_inc(setv.sem, 1)
            dve.tensor_scalar(bn2_s[:, :], bn2_s[:, :], W("bn2_g"), None, ALU.mult).then_inc(setv.sem, 1)
            dve.wait_ge(*setv(0, "bn2s"))
            dve.tensor_scalar(bn2_t[:, :], bn2_d[:, :], bn2_s[:, :], -1.0, ALU.mult, ALU.mult).then_inc(setv.sem, 1)
            dve.wait_ge(*setv(0, "bn2t0"))
            dve.tensor_scalar(bn2_t[:, :], bn2_t[:, :], W("bn2_b"), None, ALU.add).then_inc(setv.sem, 1)
            dve.tensor_scalar(out_s[:, :], W("out_w"), bn_s[:, :], None, ALU.mult).then_inc(setv.sem, 1)
            for d in range(2):
                last = dve.tensor_scalar(skip_w[:, d, :], W("ident"), W("dskip")[:, d:d + 1], None, ALU.mult)
            last.then_inc(setv.sem, 1)
            dve.wait_ge(loaded[4].sem, 16)
            dve.tensor_scalar(bq_u[:, :], W("at_bq"), W("at_u"), -HD ** -0.5, ALU.add, ALU.mult)
            dve.tensor_tensor(bq_v[:, :], W("at_bq"), W("at_v"), ALU.add).then_inc(setv.sem, 1)
            dve.tensor_scalar(ff_w1[:, :], W("ff_w1"), W("ln_g"), None, ALU.mult).then_inc(setv.sem, 1)
            dve.wait_ge(*setp(0, "conv"))
            dve.tensor_copy(conv_w[:, :, :], bank[0][:, :].rearrange("p (q n) -> p q n", q=4)).then_inc(setv.sem, 1)
            dve.wait_ge(*setp(0, "delta"))
            dve.tensor_copy(delta_w[:, :, :], bank[1][:, 0:2 * P].rearrange("p (d n) -> p d n", d=2))\
                .then_inc(setv.sem, 1)
            dve.wait_ge(*setp(0, "outw"))
            for d in range(2):
                last = dve.tensor_copy(out_w[:, d, :], bank[2 + d][:, 0:D])
            last.then_inc(setv.sem, 1)
            dve.wait_ge(*setp(0, "cent"))
            dve.tensor_copy(cen_t[:, :], bank[4][:, 0:1]).then_inc(setv.sem, 1)
            dve.wait_ge(*setp(0, "ffb"))
            dve.tensor_tensor(ff_b1[:, :], bank[5][:, 0:2], W("ff_b1"), ALU.add).then_inc(setv.sem, 1)
            dve.wait_ge(*setp(0, "e0b"))
            for c in range(CH0):
                last = dve.tensor_tensor(e0_b1[:, :].rearrange("p (e c) -> p e c", c=CH0)[:, :, c],
                                         bank[6 + c][:, 0:NE],
                                         W("e0_b1").rearrange("p (e c) -> p e c", c=CH0)[:, :, c], ALU.add)
            last.then_inc(setv.sem, 1)
            dve.tensor_tensor(e0_w1, e0_w1, W("e0_g").unsqueeze(2).to_broadcast([P, NE, P]), ALU.mult)\
                .then_inc(setv.sem, 1)
            dve.wait_ge(*setp(0, "pos"))
            dve.tensor_scalar(pos[:, :], bank[0][:, 0:2 * S - 1], W("at_bp"), None, ALU.add).then_inc(setv.sem, 1)
            dve.tensor_scalar(bq_vh[:, :], W("heads_q"), bq_v[:, :], None, ALU.mult).then_inc(setv.sem, 1)
            dve.wait_ge(*setp(0, "bo"))
            dve.tensor_tensor(bo_v[:, :], bank[1][:, 0:1], W("at_bo"), ALU.add).then_inc(setv.sem, 1)

            def normalise_x(i):
                dve.wait_ge(*x_s(i, "rs"))
                dve.tensor_tensor(xf[:, :], bank[3][:, :], rsm[:, :], ALU.mult).then_inc(x_v.sem, 1)
                dve.tensor_tensor(xpad[D:P, :, TAPS - 2:TAPS - 2 + S],
                                  bank[3][D:P, :].rearrange("p (s t) -> p s t", s=GSEQ),
                                  rsm[:, :][D:P, :].rearrange("p (s t) -> p s t", s=GSEQ), ALU.mult)\
                    .then_inc(x_v.sem, 1)
                dve.wait_ge(*x_v(i, "x"))
                dve.scalar_tensor_tensor(out=hx[:, :], in0=xf[:, :], scalar=bn2_t[:, :], in1=h0[:, :],
                                         op0=ALU.add, op1=ALU.add).then_inc(x_v.sem, 1)

            def prepare(i, d):
                hi, lo = slice(D, P), slice(P - 32, P)
                for d in (d,):
                    dve.wait_ge(*prep_s(i, f"part{d}"))
                    dve.tensor_tensor(rest[hi, :], bank[2 * d][hi, :], bc[d][hi, :], ALU.subtract)\
                        .then_inc(prep_v.sem, 1)
                    dve.wait_ge(*prep_v(i, f"rest{d}"))
                    dve.tensor_copy(bc[d][hi, :], rest[hi, :]).then_inc(prep_v.sem, 1)
                    dve.wait_ge(*prep_v(i, f"mid{d}"))
                    dve.tensor_tensor(bc[d][lo, :], rest[lo, :], bc[d][lo, :], ALU.subtract).then_inc(prep_v.sem, 1)
                    dve.wait_ge(*prep_s(i, f"ln{d}"))
                    dve.tensor_tensor(delta[d][:, :], ab[:, :], soft[:, :], ALU.add).then_inc(prep_v.sem, 1)
                    dve.wait_ge(*prep_v(i, f"delta{d}"))
                    dve.tensor_tensor(du[d][:, :], delta[d][:, :], u[d][:, :], ALU.mult).then_inc(prep_v.sem, 1)

            def driven(i, m):
                dve.wait_ge(*bc_ready(i, m + 1))
                if m % NSTATE == 0:
                    dve.wait_ge(*prep_v(i, f"du{m // NSTATE}"))
                if m >= 2:
                    dve.wait_ge(*state_ready(i, m - 1))
                dve.tensor_tensor(drive[m % 2][:, :], bank[RB[2 * m % 3]][:, :], du[m // NSTATE][:, :], ALU.mult)\
                    .then_inc(drive_ready.sem, 1)

            def gated(i, d):
                dve.wait_ge(*y_sum(i, f"y{d}"))
                dve.tensor_tensor(y[d][:, :], bank[YSUM][:, :], z[d][:, :], ALU.mult).then_inc(y_ready.sem, 1)

            def scan(i, m):
                if m == 0:
                    driven(i, 0)
                if m + 1 < NM:
                    driven(i, m + 1)
                dve.wait_ge(*drive_ready(i, m + 1))
                dve.wait_ge(*decay_ready(i, m + 1))
                if m >= RING:
                    dve.wait_ge(*hc_ready(i, m + 1 - RING))
                way = slice(None) if m < NSTATE else slice(None, None, -1)
                dve.tensor_tensor_scan(state[m % RING][:, way], decay[m // NSTATE][m % RING][:, way],
                                       drive[m % 2][:, way], 0.0, ALU.mult, ALU.add).then_inc(state_ready.sem, 1)

            def combine_fb(i):
                dve.wait_ge(*comb_s(i, "rs"))
                dve.scalar_tensor_tensor(out=fb[:, :], in0=bank[0][:, :], scalar=cen_t[:, :], in1=rsm[:, :],
                                         op0=ALU.add, op1=ALU.mult).then_inc(comb_v.sem, 1)

            def combine_h(i):
                dve.wait_ge(*comb_t(i, "ff"))
                dve.scalar_tensor_tensor(out=h1[:, :], in0=bank[0][:, :], scalar=bn2_s[:, :], in1=hx[:, :],
                                         op0=ALU.mult, op1=ALU.add).then_inc(comb_v.sem, 1)

            def normalise(i, m):
                s, v = ms[m], mv[m]
                dve.wait_ge(*s(i, "rs"))
                if m == 0:
                    lo = slice(0, D)
                    dve.tensor_tensor(xa[lo, :], bank[XB[0]][lo, :], rs[lo, :], ALU.mult).then_inc(v.sem, 1)
                    dve.wait_ge(*s(i, "rs2"))
                for half in range(2):
                    r = slice(half * D, (half + 1) * D)
                    dve.tensor_tensor(x_half[half][r, :], bank[XB[m]][r, :], (rs2, rs)[m][r, :], ALU.mult)\
                        .then_inc(v.sem, 1)

            def ranks(i, m):
                v = mv[m]
                dve.wait_ge(*mt[m](i, "logits"))
                bias = W("e0_br") if m == 0 else W("e1_bg")
                dve.tensor_tensor(lg[:, :, :], bank[LB][:, 0:TILES * NE].rearrange("p (b e) -> p b e", e=NE),
                                  bias.unsqueeze(1).to_broadcast([P, TILES, NE]), ALU.add).then_inc(v.sem, 1)
                dve.wait_ge(*v(i, "logits"))
                if m == 0:
                    dve.tensor_reduce(mx[:, :], lg[:, :, :], AX.X, ALU.max).then_inc(v.sem, 1)
                    dve.wait_ge(*v(i, "max"))
                    dve.tensor_tensor(ls[:, :, :], lg[:, :, :], mx[:, :].unsqueeze(2).to_broadcast([P, TILES, NE]),
                                      ALU.subtract).then_inc(v.sem, 1)
                mine = lg[:, :, :].unsqueeze(3).to_broadcast([P, TILES, NE, NE])
                other = lg[:, :, :].unsqueeze(2).to_broadcast([P, TILES, NE, NE])
                dve.tensor_tensor(gt[:, :, :, :], other, mine, ALU.is_gt).then_inc(v.sem, 1)
                dve.tensor_tensor(eq[:, :, :, :], other, mine, ALU.is_equal).then_inc(v.sem, 1)
                dve.wait_ge(*v(i, "eq"))
                tri = W("tri").rearrange("p (a b) -> p a b", a=NE).unsqueeze(1).to_broadcast([P, TILES, NE, NE])
                dve.tensor_tensor(eq[:, :, :, :], eq[:, :, :, :], tri, ALU.mult).then_inc(v.sem, 1)
                dve.wait_ge(*v(i, "tie"))
                dve.tensor_tensor(gt[:, :, :, :], gt[:, :, :, :], eq[:, :, :, :], ALU.add).then_inc(v.sem, 1)
                dve.wait_ge(*v(i, "sum"))
                dve.tensor_reduce(rank[:, :, :], gt[:, :, :, :], AX.X, ALU.add).then_inc(v.sem, 1)

            def gates(i, m):
                s, v = ms[m], mv[m]
                dve.wait_ge(*v(i, "rank"))
                if m == 0:
                    dve.wait_ge(*s(i, "exp"))
                    dve.scalar_tensor_tensor(out=wt[:, :, :], in0=rank[:, :, :], scalar=1.5, in1=ex[:, :, :],
                                             op0=ALU.is_lt, op1=ALU.mult).then_inc(v.sem, 1)
                    dve.wait_ge(*v(i, "masked"))
                    dve.tensor_reduce(sw[:, :], wt[:, :, :], AX.X, ALU.add).then_inc(v.sem, 1)
                    dve.wait_ge(*v(i, "wsum"))
                    dve.reciprocal(rw[:, :], sw[:, :]).then_inc(v.sem, 1)
                    dve.wait_ge(*v(i, "wrec"))
                    dve.tensor_tensor(gate[:, :, :], wt[:, :, :], rw[:, :].unsqueeze(2).to_broadcast([P, TILES, NE]),
                                      ALU.mult).then_inc(v.sem, 1)
                else:
                    dve.tensor_scalar(gate[:, :, :], rank[:, :, :], 1.5, None, ALU.is_lt).then_inc(v.sem, 1)

            def weigh(i, m):
                v = mv[m]
                dve.wait_ge(*v(i, "gate"))
                for q in range(NE // 2):
                    dve.wait_ge(*down_done[m](i, 2 * q + 2))
                    gates_ = gate[:, :, 2 * q:2 * q + 2].rearrange("p b e -> p e b").unsqueeze(3)
                    dve.tensor_tensor(yg[:, 2 * q:2 * q + 2, :].rearrange("p e (b n) -> p e b n", b=TILES),
                                      bank[YB[q % 2]][:, :].rearrange("p (e b n) -> p e b n", e=2, b=TILES),
                                      gates_.to_broadcast([P, 2, TILES, D]), ALU.mult)\
                        .then_inc(yg_ready[m].sem, 1)

            def add_up(i, m, step):
                t, v = mt[m], mv[m]
                if step == 0:
                    dve.wait_ge(*yg_ready[m](i, NE // 2))
                    dve.tensor_tensor(yg[:, 0:4, :], yg[:, 0:4, :], yg[:, 4:8, :], ALU.add).then_inc(v.sem, 1)
                    dve.wait_ge(*t(i, "gate_t"))
                    dve.tensor_copy(gate_t[:, :], bank[5][0:NE, :]).then_inc(v.sem, 1)
                if step == 1:
                    dve.wait_ge(*v(i, "add1"))
                    dve.tensor_tensor(yg[:, 0:2, :], yg[:, 0:2, :], yg[:, 2:4, :], ALU.add).then_inc(v.sem, 1)
                if step == 2:
                    dve.wait_ge(*v(i, "add2"))
                    if m == 0:
                        parts = (yg[:, k, :].rearrange("p (b n) -> p b n", b=TILES).unsqueeze(2)
                                 .to_broadcast([P, TILES, 2, D]) for k in range(2))
                        dve.tensor_tensor(acc2[:, :, :].rearrange("p b (a n) -> p b a n", a=2), *parts, ALU.add)\
                            .then_inc(v.sem, 1)
                    else:
                        dve.tensor_tensor(acc, yg[:, 0, :], yg[:, 1, :], ALU.add).then_inc(v.sem, 1)
                if step == 3:
                    dve.wait_ge(*t(i, "sum"))
                    if m == 0:
                        dve.tensor_tensor(h2[:, :], bank[6][:, :], h1[:, :], ALU.add).then_inc(v.sem, 1)
                    else:
                        dve.wait_ge(*v(i, "add3"))
                        dve.tensor_tensor(fin[:, :, :].rearrange("p b n -> p (b n)"), bank[6][:, 0:TILES * D],
                                          acc, ALU.add).then_inc(v.sem, 1)

            def attention(i, k):
                if k == 2:
                    dve.wait_ge(*att_s(i, "rs"))
                    dve.tensor_tensor(xg[:, :], bank[5][:, :], rs[:, :], ALU.mult).then_inc(att_v.sem, 1)
                if k == 4:
                    dve.wait_ge(*att_t(i, "k"))
                    for h in range(NH):
                        last = dve.tensor_scalar(kk[h][:, :], bank[6][:, :], W("at_bk"), W("heads")[:, h:h + 1],
                                                 ALU.add, ALU.mult)
                    last.then_inc(att_v.sem, 1)
                    dve.wait_ge(*att_t(i, "v"))
                    dve.tensor_copy(vv[:, :, :], bank[7][:, 0:TILES * D].rearrange("p (b n) -> p b n", b=TILES))\
                        .then_inc(att_v.sem, 1)
                j = k - S_AT
                if 0 <= j < NU:
                    b, h = divmod(j, NH)
                    if h == 0:
                        dve.wait_ge(*skew_in[b](i, 16))
                    dve.wait_ge(*s_ready(i, j + 1))
                    if j >= RING:
                        dve.wait_ge(*p_ready(i, j + 1 - RING))
                    dve.memset(held[:, j:j + 1], 0.0)
                    dve.tensor_tensor_reduce(out=ss[h], in0=bank[SB[j % 2]][:, 0:S],
                                             in1=ps[:, b, h, :], scale=1.0, scalar=3.0e38, op0=ALU.add,
                                             op1=ALU.min, accum_out=smin[:, j:j + 1]).then_inc(ss_ready.sem, 1)
                for s, at_ in enumerate(T_AT):
                    h = k - at_
                    if 0 <= h < NH:
                        n = s * NH + h
                        dve.wait_ge(*pt_ready(i, n + 1))
                        if n >= 2:
                            dve.wait_ge(*ctx_ready(i, n - 1))
                        dve.tensor_copy(ptc[n % 2][:, :, :], bank[TB][:, :].rearrange("p (a t) -> p a t", a=2))\
                            .then_inc(ptc_ready.sem, 1)
                if k == END - 1:
                    dve.wait_ge(*p_ready(i, NU))
                    dve.reciprocal(rsum[:, :], ssum[:, :]).then_inc(att_v.sem, 1)
                if k == END:
                    dve.wait_ge(*att_v(i, "rsum"))
                    dve.wait_ge(*ctx_ready(i, GSEQ * NH))
                    for a in range(2):
                        last = dve.tensor_tensor(
                            cn[:, :, a, :].rearrange("p b (h n) -> p b h n", n=HD),
                            bank[CB][:, 0:TILES * D].rearrange("p (b h n) -> p b h n", h=NH, n=HD),
                            rsum[:, :].rearrange("p (b h) -> p b h", h=NH).unsqueeze(3)
                            .to_broadcast([P, TILES, NH, HD]), ALU.mult)
                    last.then_inc(att_v.sem, 1)
                if k == END + 1:
                    dve.wait_ge(*att_t(i, "out"))
                    dve.scalar_tensor_tensor(out=h3[:, :], in0=bank[6][:, :], scalar=bo_v[:, :], in1=h2[:, :],
                                             op0=ALU.add, op1=ALU.add).then_inc(att_v.sem, 1)

            def start(i, after):
                if after is not None:
                    prepare(after, 0)
                if i is not None:
                    normalise(i, 0)
                    ranks(i, 0)
                if after is not None:
                    prepare(after, 1)
                if i is not None:
                    gates(i, 0)
                    weigh(i, 0)

            def together(before, i, after):
                for k in range(-EARLY, END + 2):
                    if before is not None:
                        if k < 0:
                            add_up(before, 0, k + EARLY)
                        attention(before, k)
                    if i is not None and k + EARLY < NM:
                        scan(i, k + EARLY)
                    if i is not None and k + EARLY == NSTATE - 1 + LAG:
                        gated(i, 0)
                    if i is not None and k + EARLY == NM + LAG:
                        gated(i, 1)
                if i is not None:
                    combine_fb(i)
                if before is not None:
                    normalise(before, 1)
                if i is not None:
                    combine_h(i)
                if after is not None:
                    normalise_x(after)
                if before is not None:
                    ranks(before, 1)
                    gates(before, 1)
                    weigh(before, 1)
                    for step in range(4):
                        add_up(before, 1, step)
                start(i, after)

            normalise_x(0)
            start(None, 0)
            together(None, 0, 1)
            with dve.Fori(1, NG - 1) as i:
                together(i - 1, i, i + 1)
            together(NG - 2, NG - 1, None)
            together(NG - 1, None, None)

        @block.tensor
        def _(pe):
            def mm(out_, lhsT, rhs, start=True, stop=True):
                return pe.matmul(out_, lhsT, rhs, start=start, stop=stop)

            def rows(c):
                return slice(32 * c, 32 * c + FD)

            pe.wait_ge(loaded[1].sem, 16)
            pe.wait_ge(*tokv(0, "feat"))
            for c in range(NG):
                mm(bank[c][:, :], W("tok_w1", rows(c)), feat[rows(c), :]).then_inc(tokp.sem, 1)
            for c in range(NG):
                pe.wait_ge(*toks(0, f"relu{c}"))
                mm(bank[4 + c][:, :], W("tok_w2"), tok_h[:, c, :]).then_inc(tokp.sem, 1)
            for c in range(NG):
                pe.wait_ge(*toks(0, f"h2_{c}"))
                mm(bank[c][:, :], W("center"), tok_h[:, c, :]).then_inc(tokp.sem, 1)
            for c in range(NG):
                pe.wait_ge(*toks(0, f"sq{c}"))
                mm(bank[4 + c][:, :], W("mean"), tok_sq[:, c, :]).then_inc(tokp.sem, 1)
            for c in range(NG):
                pe.wait_ge(*toks(0, f"ln{c}"))
                mm(bank[4 + c][:, :], W("tok_wres", rows(c)), feat[rows(c), :]).then_inc(tokp.sem, 1)

            pe.wait_ge(loaded[2].sem, 16)
            pe.wait_ge(*setv(0, "taps"))
            for q in range(4):
                last = pe.transpose(bank[0][:, q * P:(q + 1) * P], conv_s[:, q, :], W("ident"))
            last.then_inc(setp.sem, 1)
            for d in range(2):
                last = mm(bank[1][:, d * P:(d + 1) * P], W("xp_dt", slice(0, RANK))[:, d * P:(d + 1) * P],
                          W("dt_w", slice(0, RANK))[:, d * P:(d + 1) * P])
            last.then_inc(setp.sem, 1)
            pe.wait_ge(*setv(0, "outs"))
            for d in range(2):
                r = slice(d * D, (d + 1) * D)
                last = mm(bank[2 + d][:, 0:D], out_s[r, :], W("centers", r))
            last.then_inc(setp.sem, 1)
            mm(bank[4][:, 0:1], W("center2"), bn_t[:, :]).then_inc(setp.sem, 1)
            for c in range(2):
                last = mm(bank[5][:, c:c + 1], W("ff_w1")[:, c * P:(c + 1) * P], W("ln_b"))
            last.then_inc(setp.sem, 1)
            pe.wait_ge(loaded[4].sem, 16)
            for c in range(CH0):
                r = slice(c * D, (c + 1) * D)
                for e in range(NE):
                    last = mm(bank[6 + c][:, e:e + 1], W("e0_w1", r)[:, e * P:(e + 1) * P],
                              W("e0_lb", r)[:, e:e + 1])
            last.then_inc(setp.sem, 1)
            lo = slice(0, D)
            pe.wait_ge(*setv(0, "deltaw"))
            mm(bank[0][:, 0:2 * S - 1], W("at_wp", lo), W("enc", lo)).then_inc(setp.sem, 1)
            mm(bank[1][:, 0:1], W("at_wo", lo), W("at_bv", lo)).then_inc(setp.sem, 1)
            pe.wait_ge(loaded[3].sem, 16)
            pe.wait_ge(*setv(0, "bo"))

            def centred(t, src, b):
                mm(bank[b][:, :], W("center"), src[:, :]).then_inc(t.sem, 1)

            def variances(i, t, s, b, squares):
                pe.wait_ge(*s(i, "sq"))
                mm(bank[b][:, :], W("mean"), squares[:, :]).then_inc(t.sem, 1)

            def prepare_in(i):
                taps = ((0, 2), (TAPS - 1, TAPS + 1))
                pe.wait_ge(*x_v(i, "high"))
                pe.wait_ge(*x_s(i, "low"))
                for d in range(2):
                    o = bank[2 * d][:, :].rearrange("p (s t) -> p s t", s=GSEQ)
                    for q in range(2):
                        last = mm(o, conv_w[:, 2 * d + q, :], xpad[:, :, taps[d][q]:taps[d][q] + S],
                                  start=(q == 0), stop=(q == 1))
                    last.then_inc(prep_t.sem, 1)
                    mm(bank[2 * d + 1][:, :].rearrange("p (s t) -> p s t", s=GSEQ), W("inz")[:, d * P:(d + 1) * P],
                       xpad[:, :, TAPS - 1:TAPS - 1 + S]).then_inc(prep_t.sem, 1)

            def prepare_xp(i):
                for d in range(2):
                    pe.wait_ge(*prep_s(i, f"z{d}"))
                    mm(bank[2 * d][:, :], W("bc_w")[:, d * P:(d + 1) * P], u[d][:, :]).then_inc(prep_t.sem, 1)
                    mm(bank[2 * d + 1][:, :], delta_w[:, d, :], u[d][:, :]).then_inc(prep_t.sem, 1)

            def rows_out(i, m):
                d, n = divmod(m, NSTATE)
                if n == 0:
                    pe.wait_ge(*prep_v(i, f"low{d}"))
                if m == 0:
                    pe.wait_ge(*prep_v(i, "delta0"))
                if m == 1:
                    pe.wait_ge(*prep_v(i, "rest1"))
                    pe.wait_ge(*drive_ready(i, 1))
                if m >= 2:
                    pe.wait_ge(*drive_ready(i, m))
                    pe.wait_ge(*c_ready(i, m - 1))
                mm(bank[RB[2 * m % 3]][:, :], sel[:, n:n + 1].to_broadcast([P, P]), bc[d][:, :])
                mm(bank[RB[(2 * m + 1) % 3]][:, :], sel[:, NSTATE + n:NSTATE + n + 1].to_broadcast([P, P]),
                   bc[d][:, :]).then_inc(bc_ready.sem, 1)

            def summed(i, m, paired):
                d, n = divmod(m, NSTATE)
                if m == 0:
                    pe.wait_ge(*prep_s(i, "ln1"))
                if m == NSTATE:
                    pe.wait_ge(*y_ready(i, "y0"))
                if paired and m % 2 == 0:
                    return
                pe.wait_ge(*(pair_ready(i - 1, (m + 1) // 2) if paired else hc_ready(i, m + 1)))
                mm(bank[YSUM][:, :], W("ident"), hc[m % RING][:, :], start=(n == paired), stop=False)\
                    .then_inc(sum_done.sem, 1 + paired)
                if n == NSTATE - 1:
                    mm(bank[YSUM][:, :], skip_w[:, d, :], u[d][:, :], start=False).then_inc(y_sum.sem, 1)

            def combine_out(i):
                pe.wait_ge(*y_ready(i, "y1"))
                pe.wait_ge(*c_ready(i, NM))
                mm(bank[0][:, :].rearrange("p (s t) -> p s t", s=GSEQ), W("centerd"),
                   xpad[:, :, TAPS - 1:TAPS - 1 + S], stop=False)
                for d in range(2):
                    last = mm(bank[0][d * D:(d + 1) * D, :], out_w[:, d, :], y[d][:, :], start=False)
                last.then_inc(comb_t.sem, 1)

            def combine_var(i):
                pe.wait_ge(*comb_s(i, "sq"))
                mm(bank[1][:, :], W("mean2"), sqm[:, :]).then_inc(comb_t.sem, 1)

            def combine_f(i):
                pe.wait_ge(*comb_v(i, "fb"))
                for c in range(2):
                    mm(bank[1 + c][:, :], ff_w1[:, c * P:(c + 1) * P], fb[:, :]).then_inc(comb_t.sem, 1)

            def combine_ff(i):
                for c in range(2):
                    pe.wait_ge(*comb_s(i, f"g{c}"))
                    last = mm(bank[0][:, :], W("ff_w2")[:, c * P:(c + 1) * P], f1[c][:, :], start=(c == 0),
                              stop=(c == 1))
                last.then_inc(comb_t.sem, 1)

            def logits(i, m):
                t, v = mt[m], mv[m]
                pe.wait_ge(*v(i, "x0"))
                wr = W("e0_wr", lo) if m == 0 else W("e1_wg", lo)
                for b in range(TILES):
                    last = mm(bank[LB][:, b * NE:(b + 1) * NE], (xa, x_half[0])[m][lo, b * P:(b + 1) * P], wr)
                last.then_inc(t.sem, 1)

            def experts(i, m, after=None):
                v, ch = mv[m], NC[m] // NE

                def up(c):
                    e, half = divmod(c, ch) if m == 0 else (c % 4, c // 4)
                    w = e0_w1[:, e, :] if m == 0 else W("e1_w1")[:, e * P:(e + 1) * P]
                    if c == 0:
                        pe.wait_ge(*v(i, "x0"))
                    if c == 1:
                        pe.wait_ge(*v(i, "x1"))
                    if c >= len(UB):
                        pe.wait_ge(*gelu_ready[m](i, c + 1 - len(UB)))
                    mm(bank[UB[c % len(UB)]][:, :], w, x_half[half][:, :]).then_inc(hid_ready[m].sem, 1)

                def down(e):
                    pe.wait_ge(*gelu_ready[m](i, (e + 1) * ch))
                    if e == 2:
                        pe.wait_ge(*v(i, "logits"))
                    if e >= 4:
                        pe.wait_ge(*yg_ready[m](i, e // 2 - 1))
                    w2 = W("e0_w2") if m == 0 else W("e1_w2")
                    for b in range(TILES):
                        at_ = (e % 2) * TILES * D + b * D
                        for c in range(ch):
                            n = (e * ch + c) * D
                            last = mm(bank[YB[e // 2 % 2]][:, at_:at_ + D], hid[(e * ch + c) % RING][:, b * P:(b + 1) * P],
                                      w2[:, n:n + D], start=(c == 0), stop=(c == ch - 1))
                    last.then_inc(down_done[m].sem, 1)

                for e in range(NE + 1):
                    if e < NE:
                        for c in range(ch):
                            up(e * ch + c)
                    if e == 1 and after is not None:
                        prepare_xp(after)
                    if e >= 1:
                        down(e - 1)
            def turn_gates(i, m):
                t, v = mt[m], mv[m]
                pe.wait_ge(*v(i, "gate"))
                for b in range(TILES):
                    last = mm(bank[5][0:NE, b * P:(b + 1) * P], gate[:, b, :], W("ident"))
                last.then_inc(t.sem, 1)

            def sum_up(i, m, src):
                t, v = mt[m], mv[m]
                pe.wait_ge(*v(i, "add3"))
                if m == 0:
                    mm(bank[6][:, :], W("e0_b2", slice(0, NE)), gate_t[:, :], stop=False)
                    for b in range(TILES):
                        last = mm(bank[6][:, b * P:(b + 1) * P], acc2[:, b, :], W("ident"), start=False,
                                  stop=(b == TILES - 1))
                else:
                    for b in range(TILES):
                        o = bank[6][:, b * D:(b + 1) * D]
                        mm(o, gate_t[:, b * P:(b + 1) * P], W("e1_b2", slice(0, NE)), stop=False)
                        last = mm(o, src[lo, b * P:(b + 1) * P], W("ident", lo)[:, 0:D], start=False)
                last.then_inc(t.sem, 1)

            def weighted(i, n):
                s, h = divmod(n, NH)
                pe.wait_ge(*ptc_ready(i, n + 1))
                for q in range(2):
                    at_ = (2 * s + q) * D + h * HD
                    for a in range(2):
                        last = mm(bank[CB][:, at_:at_ + HD], ptc[n % 2][:, a, q * P:(q + 1) * P],
                                  vv[:, 2 * s + a, h * HD:(h + 1) * HD], start=(a == 0), stop=(a == 1))
                last.then_inc(ctx_ready.sem, 1)

            def attention(i, k):
                if k == 0:
                    pe.wait_ge(*mv[0](i, "h"))
                    centred(att_t, h2, 5)
                if k == 1:
                    variances(i, att_t, att_s, 6, sq)
                if k == 3:
                    pe.wait_ge(*att_s(i, "xg"))
                    mm(bank[5][:, :], W("at_wq"), xg[:, :]).then_inc(att_t.sem, 1)
                    mm(bank[6][:, :], W("at_wk"), xg[:, :]).then_inc(att_t.sem, 1)
                    for b in range(TILES):
                        last = mm(bank[7][:, b * D:(b + 1) * D], xg[lo, b * P:(b + 1) * P], W("at_wv", lo))
                    last.then_inc(att_t.sem, 1)
                j = k - E_AT
                if 0 <= j < NU:
                    b, h = divmod(j, NH)
                    if b == 0:
                        pe.wait_ge(*att_s(i, f"qv{h}"))
                    first = P if b % 2 == 0 else 0
                    if j < 2:
                        pe.wait_ge(*att_v(i, ("k", "v")[j]))
                    else:
                        pe.wait_ge(*es_ready(i, j - 1))
                    mm(bank[EB[j % 2]][:, 0:SKEW], qv[h][:, b * P:(b + 1) * P], pos[:, first:first + SKEW])\
                        .then_inc(e_ready.sem, 1)
                j = k - S_AT
                if 0 <= j < NU:
                    b, h = divmod(j, NH)
                    if j == 0:
                        pe.wait_ge(*att_s(i, "qu"))
                    if j >= 2:
                        pe.wait_ge(*ss_ready(i, j - 1))
                    mm(bank[SB[j % 2]][:, 0:S], qu[:, b * P:(b + 1) * P],
                       kk[h][:, (b // 2) * S:(b // 2 + 1) * S]).then_inc(s_ready.sem, 1)
                for s, at_ in enumerate(T_AT):
                    h = k - at_
                    n = s * NH + h
                    if 0 < h <= NH:
                        weighted(i, n - 1)
                    if 0 <= h < NH:
                        pe.wait_ge(*p_ready(i, (2 * s + 1) * NH + h + 1))
                        if n == 0:
                            pe.wait_ge(*es_ready(i, NU))
                        for a in range(2):
                            for q in range(2):
                                last = pe.transpose(bank[TB][:, a * S + q * P:a * S + (q + 1) * P],
                                                    pb[:, q * NH + h, a * P:(a + 1) * P], W("ident"))
                        last.then_inc(pt_ready.sem, 1)
                if k == END:
                    pe.wait_ge(*att_v(i, "cn"))
                    for b in range(TILES):
                        last = mm(bank[5][:, b * P:(b + 1) * P], cn[:, b, :, :].rearrange("p a n -> p (a n)"), W("ident"))
                    last.then_inc(att_t.sem, 1)
                if k == END + 1:
                    pe.wait_ge(*att_s(i, "ctx_t"))
                    mm(bank[6][:, :], W("at_wo"), ct[:, :]).then_inc(att_t.sem, 1)

            def inputs(i):
                pe.wait_ge(*x_s(i, "h0"))
                centred(x_t, h0, 3)
                variances(i, x_t, x_s, 2, sqm)
                prepare_in(i)

            def together(before, i, after):
                for k in range(-EARLY, END + 2):
                    if i is not None and k + EARLY < NM:
                        rows_out(i, k + EARLY)
                    if before is not None:
                        if k == -EARLY:
                            turn_gates(before, 0)
                        if k == -1:
                            sum_up(before, 0, h1)
                        attention(before, k)
                    if i is not None and LAG <= k + EARLY < NM + LAG:
                        summed(i, k + EARLY - LAG, before is not None)
                    if i is not None and k + EARLY == NM + LAG:
                        combine_out(i)
                    if i is not None and k == END:
                        combine_var(i)
                if before is not None:
                    pe.wait_ge(*att_v(before, "h"))
                    centred(mt[1], h3, 5)
                if i is not None:
                    combine_f(i)
                if before is not None:
                    variances(before, mt[1], ms[1], VB[1], sq)
                if i is not None:
                    combine_ff(i)
                if after is not None:
                    inputs(after)
                if before is not None:
                    logits(before, 1)
                    experts(before, 1, after)
                elif after is not None:
                    prepare_xp(after)
                if i is not None:
                    pe.wait_ge(*comb_v(i, "h1"))
                    if before is not None:
                        pe.wait_ge(*yg_ready[1](before, 3))
                    centred(mt[0], h1, XB[0])
                if before is not None:
                    turn_gates(before, 1)
                if i is not None:
                    if before is not None:
                        pe.wait_ge(*yg_ready[1](before, 4))
                    variances(i, mt[0], ms[0], VB[0], sq)
                if before is not None:
                    sum_up(before, 1, h3)
                if i is not None:
                    logits(i, 0)
                    experts(i, 0)

            inputs(0)
            prepare_xp(0)
            together(None, 0, 1)
            with pe.Fori(1, NG - 1) as i:
                together(i - 1, i, i + 1)
            together(NG - 2, NG - 1, None)
            together(NG - 1, None, None)


def host_arrays(a):
    f = np.float32
    part = {}

    def put(name, rows, value):
        k, at, n = places()[name]
        value = np.asarray(value, f)
        part.setdefault(k, np.zeros((P, WIDTHS[k]), f))[rows, at:at + n] = value.reshape(value.shape[0], n)

    def col(v, times=1):
        return np.tile(np.asarray(v, f).reshape(-1), times)[:, None]

    every, lo, hi = slice(0, P), slice(0, D), slice(D, P)
    for c in range(NG):
        r = slice(32 * c, 32 * c + FD)
        per, harm, kind = np.meshgrid(np.arange(4), np.arange(HARM), np.arange(2), indexing="ij")
        put("invp", r, col(1.0 / np.array(PERIODS)[per]))
        put("harm", r, col(harm + 1.0))
        put("phase", r, col(a["L0_tok_ph"][per, harm]))
        put("amp", r, col(a["L0_tok_hw"][per, harm]))
        put("quarter", r, col(0.25 * kind))
        put("halfpi", r, col(0.5 * math.pi * kind))
        put("tok_w1", r, a["L0_tok_W1"])
        put("tok_wres", r, np.tile(a["L0_tok_Wres"], (1, 2)))
    put("tok_b1", every, col(a["L0_tok_b1"]))
    put("tok_b2", every, col(a["L0_tok_b2"], 2))
    put("tok_g", every, col(a["L0_tok_gamma"], 2))
    put("tok_b", every, col(a["L0_tok_beta"], 2))
    put("tok_bres", every, col(a["L0_tok_bres"], 2))
    put("tok_w2", every, np.tile(a["L0_tok_W2"], (1, 2)))
    cen = np.eye(D) - 1.0 / D
    zero = np.zeros((D, D))
    put("center", every, np.eye(P) - 1.0 / P * np.ones((P, P)))
    put("mean", every, np.full((P, P), 1.0 / P))
    put("ident", every, np.eye(P))
    put("mean2", every, np.kron(np.eye(2), np.full((D, D), 1.0 / D)))
    put("center2", every, np.block([[cen, zero], [zero, cen]]))
    put("centerd", lo, np.tile(cen, (1, 2)))
    put("centers", every, np.tile(cen, (2, 1)))

    m = {k[len("L0_attn_mamba_"):]: v for k, v in a.items() if k.startswith("L0_attn_mamba_")}
    both = lambda fn: np.concatenate([fn(d) for d in range(2)], axis=1)
    inner = 2 * D
    put("inx", every, both(lambda d: m["in_w"][d, :inner]))
    put("conv_w", every, both(lambda d: m["conv_w"][d]))
    put("conv_b", every, m["conv_b"].T)
    put("inz", lo, both(lambda d: m["in_w"][d, inner:].T))
    put("bc_w", every, both(lambda d: np.tile(m["xproj_w"][d, RANK:].T, (1, 4))))
    put("xp_dt", slice(0, RANK), both(lambda d: m["xproj_w"][d, :RANK]))
    put("dt_w", slice(0, RANK), both(lambda d: m["dt_w"][d].T))
    put("dt_b", every, m["dt_b"].T)
    put("alog", every, both(lambda d: m["Alog"][d]))
    put("dskip", every, m["D"].T)
    put("out_w", every, m["out_w"].reshape(P, P))
    for name, key in (("g", "gamma"), ("b", "beta"), ("m", "mean"), ("v", "var")):
        v = a["L0_attn_bn_" + key]
        put("bn_" + name, every, col(v[:2]))
        put("bn2_" + name, every, col(v[2], 2))
    put("ln_g", every, col(a["L0_attn_ln_gamma"][:2]))
    put("ln_b", every, col(a["L0_attn_ln_beta"][:2]))
    put("ff_w1", every, np.tile(a["L0_attn_ff_w1"].T, (2, 1)))
    put("ff_b1", every, a["L0_attn_ff_b1"].reshape(2, P).T)
    put("ff_w2", every, np.concatenate([np.tile(a["L0_attn_ff_w2"].T[c * P:(c + 1) * P], (1, 2)) for c in range(2)], 1))
    put("ff_b2", every, col(a["L0_attn_ff_b2"], 2))

    put("tri", every, np.tile(np.tril(np.ones((NE, NE)), -1).reshape(1, -1), (P, 1)))
    e = {k[len("L0_ffn_"):]: v for k, v in a.items() if k.startswith("L0_ffn_")}
    for c, r in enumerate((lo, hi)):
        put("e0_w1", r, e["W1"][:, :, c * P:(c + 1) * P].transpose(1, 0, 2))
    put("e0_g", every, np.tile(e["ln_g"].T, (2, 1)))
    put("e0_lb", every, np.tile(e["ln_b"].T, (2, 1)))
    put("e0_b1", every, e["b1"].reshape(NE * CH0, P).T)
    put("e0_w2", every, e["W2"].reshape(NE * CH0, P, D).transpose(1, 0, 2))
    put("e0_b2", slice(0, NE), np.tile(e["b2"], (1, 2)))
    put("e0_wr", lo, e["Wr"])
    put("e0_br", every, np.tile(e["br"], (P, 1)))

    t = {k[len("L1_attn_"):]: v for k, v in a.items() if k.startswith("L1_attn_")}

    def padded(v):
        v = np.asarray(v, f).reshape(NH, HD, -1)
        return np.concatenate([v, np.zeros_like(v)], axis=1).reshape(P, -1)

    put("at_g", every, col(t["ln_gamma"], 2))
    put("at_b", every, col(t["ln_beta"], 2))
    for name, key in (("wq", "Wq"), ("wk", "Wk"), ("wp", "Wpos")):
        put("at_" + name, lo, padded(t[key]).T)
    for name, key in (("bq", "bq"), ("bk", "bk"), ("bp", "bpos"), ("u", "u_bias"), ("v", "v_bias")):
        put("at_" + name, every, padded(t[key]))
    heads = np.kron(np.eye(NH), np.ones((P // NH, 1)))
    put("heads", every, heads)
    put("heads_q", every, -HD ** -0.5 * heads)
    put("at_wv", lo, t["Wv"].T)
    put("at_wo", lo, np.tile(t["Wo"].T, (1, 2)))
    put("at_bv", lo, col(t["bv"]))
    put("at_bo", every, col(t["bo"], 2))
    dist = np.clip(np.arange(2 * S - 1) - (S - 1), -MAXREL, MAXREL) + MAXREL
    div = np.exp(np.arange(0, D, 2, dtype=f) * f(-math.log(10000.0) / D)).astype(f)
    ang = dist.astype(f)[:, None] * div
    put("enc", lo, np.stack([np.sin(ang), np.cos(ang)], axis=-1).reshape(-1, D).T)

    g = {k[len("L1_ffn_"):]: v for k, v in a.items() if k.startswith("L1_ffn_")}
    for c, r in enumerate((lo, hi)):
        put("e1_w1", r, g["W1"][c * 4:(c + 1) * 4].transpose(1, 0, 2))
    put("e1_b1", every, g["b1"].T)
    put("e1_w2", every, g["W2"].transpose(1, 0, 2))
    put("e1_b2", slice(0, NE), g["b2"])
    put("e1_wg", lo, g["Wg"])
    put("e1_bg", every, np.tile(g["bg"], (P, 1)))

    tokens = np.stack([a["x"], a["itok_BS_0_23"], a["itok_BS_0_11"], a["itok_BS_0_30"]]).reshape(4, NG, T)
    idx = np.zeros((NG, 32, T), np.int32)
    idx[:, :FD] = np.repeat(tokens.transpose(1, 0, 2), FD // 4, axis=1)
    sel = np.eye(P, 2 * NSTATE) + np.eye(P, 2 * NSTATE, -64) + np.eye(P, 2 * NSTATE, -96)
    return idx.reshape(P, T), part[0], part[1], part[2], sel


def kernel(**inputs):
    import ml_dtypes
    import concourse.bacc as bacc
    from concourse.bass_utils import run_bass_kernel_spmd

    a = {k: np.asarray(v) for k, v in inputs.items()}
    idx, w0, w1, w2, sel = host_arrays(a)
    arrays = {"idx_dram": idx, "w0_dram": w0, "w1_dram": w1, "w2_dram": w2, "sel_dram": sel.astype(ml_dtypes.bfloat16)}
    nc = bacc.Bacc("TRN2", target_bir_lowering=False, num_devices=1)
    ins = [nc.dram_tensor(n, v.shape, mybir.dt.from_np(v.dtype), kind="ExternalInput").ap() for n, v in arrays.items()]
    out = nc.dram_tensor("out_dram", (NG, P, TILES, D), F32, kind="ExternalOutput").ap()
    tower(nc, *ins, out)
    r = run_bass_kernel_spmd(nc, [arrays], core_ids=[0])
    got = np.asarray(r.results[0]["out_dram"])
    return got.transpose(0, 2, 1, 3).reshape(NSEQ, S, D)
```

```python
import math
from contextlib import ExitStack

import numpy as np
import concourse.bass as bass
from concourse import mybir

F32 = mybir.dt.float32
BF16 = mybir.dt.bfloat16
I32 = mybir.dt.int32
ALU = mybir.AluOpType
ACT = mybir.ActivationFunctionType
AX = mybir.AxisListType

D, S, NSEQ = 64, 256, 8
GSEQ = 2
T = GSEQ * S
NG = NSEQ // GSEQ
P = 128
TILES = T // P
HARM, PERIODS = 3, (7.0, 24.0, 12.0, 1.0)
FD = len(PERIODS) * 2 * HARM
TAPS, NSTATE, RANK = 4, 16, 4
PADW = S + 2 * (TAPS - 1)
NE, CH0 = 8, 2
NH, HD, MAXREL = 4, 16, 30
SKEW = P + S - 1
EPS = 1e-5
TWO_PI = 2.0 * math.pi
TURN = (6.28125, 0.0019350051879882812, 3.0199159819574e-07)
ROUND = 12582912.0
PI_LO = 3.1415925
RING = 4

PACKED = [
    [("invp", 1), ("harm", 1), ("phase", 1), ("quarter", 1), ("halfpi", 1), ("amp", 1), ("tok_b1", 1),
     ("tok_b2", 1), ("tok_g", 1), ("tok_b", 1), ("tok_bres", 1), ("tok_w1", P), ("tok_w2", P), ("tok_wres", P),
     ("center", P), ("mean", P)],
    [("ident", P), ("mean2", P), ("center2", P), ("centerd", P),
     ("inx", 2 * D), ("conv_w", 2 * TAPS), ("conv_b", 2), ("inz", 2 * P), ("bc_w", 2 * P), ("xp_dt", 2 * P),
     ("dt_w", 2 * P), ("dt_b", 2), ("alog", 2 * NSTATE), ("dskip", 2), ("out_w", P), ("bn_g", 1), ("bn_b", 1),
     ("bn_m", 1), ("bn_v", 1), ("bn2_g", 1), ("bn2_b", 1), ("bn2_m", 1), ("bn2_v", 1), ("ln_g", 1), ("ln_b", 1),
     ("ff_w1", 2 * P), ("ff_b1", 2), ("ff_w2", 2 * P), ("ff_b2", 1)],
    [("tri", NE * NE), ("w1_g", NE * (CH0 + 1)), ("e0_lb", NE), ("e0_b1", NE * CH0),
     ("e0_w2", NE * CH0 * D), ("e0_b2", P), ("e0_wr", NE), ("e0_br", NE),
     ("at_g", 1), ("at_b", 1), ("at_wq", P), ("at_wk", P), ("at_wp", P), ("at_bq", 1), ("at_bk", 1), ("at_bp", 1),
     ("at_u", 1), ("at_v", 1), ("at_wv", D), ("at_wo", P), ("at_bv", 1), ("at_bo", 1), ("enc", 2 * S - 1), ("heads", NH), ("heads_q", NH),
     ("e1_b1", NE), ("e1_w2", NE * D), ("e1_b2", D), ("e1_wg", NE), ("e1_bg", NE)],
    [("w1", NE * (CH0 + 1) * P)],
]
WIDTHS = [sum(n for _, n in part) for part in PACKED]


def places():
    out = {}
    for k, part in enumerate(PACKED):
        at = 0
        for name, n in part:
            out[name] = (k, at, n)
            at += n
    return out


class Signal:

    def __init__(self, sem, steps):
        self.sem, self.steps = sem, steps

    def __call__(self, i, step):
        n = step if isinstance(step, int) else self.steps.index(step) + 1
        return self.sem, i * len(self.steps) + n


def tower(nc, idx, w0, w1, w2, w3, sel_in, out):
    where = places()
    ctx = ExitStack()
    with ctx:
        def sb(name, shape, dt=F32):
            return ctx.enter_context(nc.sbuf_tensor(name, shape, dt))

        def signal(name, steps):
            return Signal(ctx.enter_context(nc.semaphore(name)), steps)

        bank = [ctx.enter_context(nc.psum_tensor(f"bank{b}", [P, T], F32)) for b in range(8)]
        packed = [sb(f"packed{k}", [P, n])[:, :] for k, n in enumerate(WIDTHS[:3])]
        qk = sb("qk", [P, 2 * NH * T])
        packed.append(qk[:, 0:WIDTHS[3]])

        def W(name, rows=slice(0, P)):
            k, at, n = where[name]
            return packed[k][rows, at:at + n]

        h_all = sb("h_all", [P, NG * T])
        sel = sb("sel", [P, 2 * NSTATE], BF16)

        conv_w = sb("conv_w", [P, 4, P])
        eps_c = sb("eps_c", [P, 2])
        tok_bias = sb("tok_bias", [P, 1])
        bn2_d = sb("bn2_d", [P, 1])
        eps1, eps2 = eps_c[:, 0:1], eps_c[:, 1:2]
        delta_w = sb("delta_w", [P, 2, P])
        skip_w = sb("skip_w", [P, 2, P])
        a_neg = sb("a_neg", [P, 2 * NSTATE])
        bn_s, bn_t, bn2_s, bn2_t = (sb(n, [P, 1]) for n in ("bn_s", "bn_t", "bn2_s", "bn2_t"))
        out_s = sb("out_s", [P, P])
        out_w = sb("out_w", [P, 2, D])
        cen_t = sb("cen_t", [P, 1])
        ff_w1 = sb("ff_w1", [P, 2 * P])
        ff_b1 = sb("ff_b1", [P, 2])
        NCH, FIRST = NE * (CH0 + 1), (0, NE * CH0)
        es_all = sb("es_all", [P, max(2 * NH * SKEW, NCH * P)])
        w1_f = es_all[:, 0:NCH * P]
        w1_a, w1_b = (sb(n, [P, NCH * P], BF16) for n in ("w1_a", "w1_b"))
        e0_b1 = sb("e0_b1", [P, NE * CH0])
        pos = sb("pos", [P, 2 * S - 1])
        bq_u, bq_v, bo_v = (sb(n, [P, 1]) for n in ("bq_u", "bq_v", "bo_v"))

        h0 = sb("h0", [P, T])
        sq, rs, rs2 = sb("sq", [P, T]), sb("rs", [P, T]), sb("rs2", [P, T])
        conv_s = sq[:, :].rearrange("p (q n) -> p q n", q=4)
        xpad = sb("xpad", [P, GSEQ, PADW])
        hx = sb("hx", [P, T])
        u = [sb(f"u{d}", [P, T]) for d in range(2)]
        z = [sb(f"z{d}", [P, T]) for d in range(2)]
        bc = [sb(f"bc{d}", [P, T], BF16) for d in range(2)]
        delta = [sb(f"delta{d}", [P, T]) for d in range(2)]
        du = [sb(f"du{d}", [P, T]) for d in range(2)]
        decay = [[sb(f"decay{d}_{r}", [P, T]) for r in range(RING)] for d in range(2)]
        drive = [sb(f"drive{r}", [P, T]) for r in range(2)]
        state = [sb(f"state{r}", [P, T]) for r in range(RING)]
        c_sb = [sb(f"c_sb{r}", [P, T]) for r in range(RING)]
        hc = [sb(f"hc{r}", [P, T]) for r in range(RING)]
        y = z
        xf, fb = drive
        sqm, rsm, sqx, rsx = hc
        f1 = c_sb[:2]
        idx_i = fb[:, :].bitcast(I32)
        h1, h2, h3 = sb("h1", [P, T]), sb("h2", [P, T]), sb("h3", [P, T])
        angle, turns, feat = h1, h2, h3

        xa = sb("xa", [P, T])
        xn, xr = c_sb[2:], hc[:2]
        x_hi, x_mid, x_lo = ([sb(f"{n}{m}", [P, T], BF16) for m in range(2)] for n in ("x_hi", "x_mid", "x_lo"))
        lg, ls, ex, wt = (sb(n, [P, TILES, NE]) for n in ("lg", "ls", "ex", "wt"))
        gate = [sb(f"gate{m}", [P, TILES, NE]) for m in range(2)]
        gt, eq = sb("gt", [P, TILES, NE, NE]), sb("eq", [P, TILES, NE, NE])
        rank = sb("rank", [P, TILES, NE])
        mx, sw, rw = (sb(n, [P, TILES]) for n in ("mx", "sw", "rw"))
        gate_t = sb("gate_t", [NE, T])
        yg = sb("yg", [P, NE, TILES * D])
        acc2 = sb("acc2", [P, TILES, P])
        acc = acc2[:, 0:2, :].rearrange("p a n -> p (a n)")
        held = sb("held", [P, TILES * NH])
        fin = sb("fin", [P, TILES, D])

        qu = xa
        qv, kk = ([qk[:, (n * NH + h) * T:(n * NH + h + 1) * T] for h in range(NH)] for n in range(2))
        bq_vh = sb("bq_vh", [P, NH])
        xg = sb("xg", [P, T])
        vv = sb("vv", [P, TILES, D])
        es = [es_all[:, r * NH * SKEW:(r + 1) * NH * SKEW].rearrange("p (h n) -> p h n", h=NH) for r in range(2)]
        hid = [es[r // 2][:, :, :].rearrange("p h n -> p (h n)")[:, r % 2 * T:(r % 2 + 1) * T] for r in range(RING)]
        ps = sb("ps", [P, TILES, NH, S])
        early = ps[:, :, :, :].rearrange("p b h s -> p (b h s)").rearrange("p (a c t) -> p a c t", a=2, c=NG)
        tok_h, tok_sq = early[:, 0], early[:, 1]
        tok_rs = yg[:, :, :].rearrange("p e n -> p (e n)").rearrange("p (c t) -> p c t", c=NG)
        ss = [xg[:, 0:S], xg[:, S:T], *(r[:, :, :, :].rearrange("p b e f -> p (b e f)") for r in (gt, eq))]
        smin, ssum, rsum = (sb(n, [P, TILES * NH]) for n in ("smin", "ssum", "rsum"))
        pb = yg
        ptc = [sb(f"ptc{r}", [P, 2, S]) for r in range(2)]
        ab, soft, rest = (state[0], kk[2]), (state[1], kk[3]), state[2:4]
        sq1, rs1 = kk[:2]
        cn, ct = qv[0][:, :].rearrange("p (b a n) -> p b a n", b=TILES, a=2), qv[1]
        skew = nc.dram_tensor("skew", [TILES, P, NH, SKEW], F32, kind="Internal").ap()

        loaded = [signal(f"loaded{k}", ["done"]) for k in range(6)]
        tokv = signal("tok_vector", ["eps", "bias", "t", "norm", "angle", "k", "kr", "r1", "r2", "r3", "r4", "r5", "feat",
                                     *(f"xn{c}" for c in range(NG)), *(f"h{c}" for c in range(NG))])
        toks = signal("tok_scalar", ["sin", *(f"{s}{c}" for s in ("relu", "h2_", "sq", "ln", "rs", "aff")
                                              for c in range(NG))])
        tokp = signal("tok_tensor", [f"{s}{c}" for s in ("w1_", "w2_", "cen", "var", "res") for c in range(NG)])
        setg = signal("setup_pool", ["pad", "zero", "w1", "high", "copy", "rest", "mid", "low"])
        setv = signal("setup_vector", ["taps", "aneg", "bns", "bnt0", "bnt", "bn2d", "bn2s", "bn2t0", "bn2t", "outs", "skip",
                                       "ffw", "convw", "deltaw", "outw", "cent", "ffb", "sums", "e0b",
                                       "pos", "bqv", "bo"])
        sets = signal("setup_scalar", ["alog", "ln", "rsq", "ln2", "rsq2"])
        setp = signal("setup_tensor", ["conv", "delta", "outw", "cent", "ffb", "e0b", "pos", "bo"])

        x_t = signal("x_tensor", ["center", "var"])
        x_s = signal("x_scalar", ["h0", "sq", "ln", "rs", "low"])
        x_v = signal("x_vector", ["x", "high", "hx"])
        prep_t = signal("prep_tensor", ["conv0", "z0", "conv1", "z1", "bc0", "dt0", "bc1", "dt1"])
        prep_s = signal("prep_scalar", ["u0", "z0", "u1", "z1",
                                     *(f"{s}{d}" for d in range(2) for s in ("part", "abs", "relu", "exp", "ln"))])
        prep_v = signal("prep_vector", [f"{s}{d}" for d in range(2) for s in ("rest", "mid", "low", "delta", "du")])
        NM = 2 * NSTATE
        bc_ready = signal("bc_ready", list(range(NM)))
        decay_ready = signal("decay_ready", list(range(NM)))
        c_ready = signal("c_ready", list(range(NM)))
        drive_ready = signal("drive_ready", list(range(NM)))
        state_ready = signal("state_ready", list(range(NM)))
        hc_ready = signal("hc_ready", list(range(NM)))
        PAIRED = 16
        pair_ready = signal("pair_ready", list(range((NM - PAIRED) // 2)))
        sum_done = signal("sum_done", list(range(NM)))
        y_sum = signal("y_sum", ["y0", "y1"])
        y_ready = signal("y_ready", ["y0", "y1"])
        comb_t = signal("out_tensor", ["center", "var", "f0", "f1", "ff"])
        comb_s = signal("out_scalar", ["sq", "ln", "rs", "g0", "g1"])
        comb_v = signal("out_vector", ["fb", "h1"])

        route = ["logits", "max", "shift", "gt", "eq", "tie", "sum", "rank"]
        mt = [signal("moe0_tensor", ["center", "var", "logits", "gate_t", "sum"]),
              signal("moe1_tensor", ["center", "var", "logits", "gate_t", "sum"])]
        ms = [signal("moe0_scalar", ["sq", "ln", "rs", "ln2", "rs2", "exp", "gate_t"]),
              signal("moe1_scalar", ["sq", "ln", "rs"])]
        mv = [signal("moe0_vector", ["xa", "x", "high", *route, "masked", "wsum", "wrec", "gate",
                                     "add2", "add3", "h"]),
              signal("moe1_vector", ["x", "high", "logits", *route[3:], "gate", "add1", "gate_t", "add2", "add3", "h"])]
        x_parts = [signal(f"x_parts{m}", ["mid", "rest", "low", "again"]) for m in range(2)]
        NC = [NE * CH0, NE]
        halves_added = signal("halves_added", ["done"])
        down_done = [signal(f"down_done{m}", list(range(NE))) for m in range(2)]
        hid_ready = [signal(f"hid_ready{m}", list(range(NC[m]))) for m in range(2)]
        gelu_ready = [signal(f"gelu_ready{m}", list(range(NC[m]))) for m in range(2)]
        yg_ready = [signal(f"yg_ready{m}", list(range(NE // 2))) for m in range(2)]
        RB, YSUM = (0, 1, 2), 3
        XB, VB, LB, UB, YB = (7, 5), (4, 6), (4, 5), (6, 5), (7, 4)
        GB, OB = (5, 0), (6, 1)
        SB, TB, CB = (4, 5), 6, 7
        LAG, EARLY = 3, 8
        TURN_AT, GATE_AT, BIAS_AT, SUM_AT, ADD_AT = -8, -7, -5, -4, (-7, -6, -4)
        Q_AT, E_AT, S_AT, P_AT, T_AT, END = 4, 6, 14, 15, (23, 28), 33

        def rel_bank(j):
            return bank[(4 if j < 8 else 6, 7)[j % 2]]


        NU = TILES * NH
        att_t = signal("attn_tensor", ["center", "var", "q", "k", "v", "ctx_t", "out"])
        att_s = signal("attn_scalar", ["sq", "ln", "rs", "xg", *(f"qv{h}" for h in range(NH)), "qu", "ctx_t"])
        att_v = signal("attn_vector", ["xn", "v", "k", "rsum", "cn", "h"])
        e_ready = signal("e_ready", list(range(NU)))
        es_ready = signal("es_ready", list(range(NU)))
        s_ready = signal("s_ready", list(range(NU)))
        ss_ready = signal("ss_ready", list(range(NU)))
        p_ready = signal("p_ready", list(range(NU)))
        pt_ready = signal("pt_ready", list(range(GSEQ * NH)))
        ptc_ready = signal("ptc_ready", list(range(GSEQ * NH)))
        ctx_ready = signal("ctx_ready", list(range(GSEQ * NH)))
        skew_out = [signal(f"skew_out{b}", list(range(16))) for b in range(TILES)]
        skew_in = [signal(f"skew_in{b}", list(range(16))) for b in range(TILES)]
        stored = signal("stored", list(range(16)))

        block = ctx.enter_context(nc.Block())

        @block.sync
        def _(sp):
            for k, (dst, src) in enumerate([(idx_i, idx), (packed[0], w0), (packed[1], w1), (sel, sel_in),
                                            (packed[2], w2), (packed[3], w3)]):
                sp.dma_start(dst[:, :] if k else dst, src).then_inc(loaded[k].sem, 16)

            def skews(i):
                for b in range(TILES):
                    sp.wait_ge(*es_ready(i, NH * (b + 1)))
                    sp.dma_start(skew[b], es[b % 2][:, :, :]).then_inc(skew_out[b].sem, 16)
                    sp.wait_ge(*skew_out[b](i, 16))
                    rows = skew[b]
                    shifted = bass.AP(rows.tensor, rows.offset + P - 1,
                                      [[NH * SKEW - 1, P], [SKEW, NH], [1, S]])
                    sp.dma_start(ps[:, b, :, :], shifted).then_inc(skew_in[b].sem, 16)

            def store(i):
                sp.wait_ge(*mv[1](i, "h"))
                sp.dma_start(out[i], fin[:, :, :]).then_inc(stored.sem, 16)

            for i in range(NG):
                skews(i)
                store(i)
                sp.wait_ge(*stored(i, 16))

        @block.gpsimd
        def _(pool):
            pool.memset(xpad[:, :, :], 0.0).then_inc(setg.sem, 1)
            for d in range(2):
                edge = 0 if d == 0 else S - 1
                for r in range(RING):
                    v = decay[d][r][:, :].rearrange("p (s t) -> p s t", s=GSEQ)
                    last = pool.memset(v[:, :, edge:edge + 1], 0.0)
            last.then_inc(setg.sem, 1)

            dn, up = slice(0, D), slice(D, P)
            pool.wait_ge(loaded[4].sem, 16)
            pool.wait_ge(loaded[5].sem, 16)
            f, a, b, w = (v.rearrange("p (c n) -> p c n", n=P) for v in (w1_f, w1_a[:, :], w1_b[:, :], W("w1")))
            g = W("w1_g").unsqueeze(2).to_broadcast([P, NCH, P])
            pool.tensor_tensor(f, w, g, ALU.mult).then_inc(setg.sem, 1)
            pool.tensor_tensor(a, w, g, ALU.mult).then_inc(setg.sem, 1)
            pool.wait_ge(*setg(0, "high"))
            pool.tensor_tensor(b[dn], w[dn], g[dn], ALU.mult).then_inc(setg.sem, 1)
            pool.wait_ge(*setg(0, "copy"))
            pool.tensor_tensor(w[up], f[up], a[up], ALU.subtract).then_inc(setg.sem, 1)
            pool.wait_ge(*setg(0, "rest"))
            pool.tensor_tensor(a[up], f[up], a[up], ALU.subtract).then_inc(setg.sem, 1)
            pool.wait_ge(*setg(0, "mid"))
            pool.tensor_tensor(b[up], w[up], a[up], ALU.subtract).then_inc(setg.sem, 1)

            def split(i, m):
                p = x_parts[m]
                pool.wait_ge(*mv[m](i, "high"))
                pool.tensor_tensor(x_mid[m][:, :], xn[m][:, :], x_hi[m][:, :], ALU.subtract).then_inc(p.sem, 1)
                pool.tensor_tensor(xr[m][:, :], xn[m][:, :], x_hi[m][:, :], ALU.subtract).then_inc(p.sem, 1)
                pool.wait_ge(*p(i, "rest"))
                pool.tensor_tensor(x_lo[m][dn, :], xr[m][dn, :], x_mid[m][dn, :], ALU.subtract).then_inc(p.sem, 1)
                pool.wait_ge(*p(i, "low"))
                pool.tensor_tensor(x_lo[m][up, :], xn[m][up, :], xr[m][up, :], ALU.subtract).then_inc(p.sem, 1)
                pool.wait_ge(*p(i, "again"))

            def scan_outputs(i, paired):
                for m in range(NM):
                    pool.wait_ge(*state_ready(i, m + 1))
                    pool.wait_ge(*c_ready(i, m + 1))
                    if paired and m >= PAIRED + RING and m % 2 == 0:
                        pool.wait_ge(*pair_ready(i - 1, (m - PAIRED) // 2 - 1))
                    elif m >= RING:
                        pool.wait_ge(*sum_done(i, m + 1 - RING))
                    pool.tensor_tensor(hc[m % RING][:, :], state[m % RING][:, :], c_sb[m % RING][:, :],
                                       ALU.mult).then_inc(hc_ready.sem, 1)
                    if paired and m >= PAIRED and m % 2 == 1:
                        pool.wait_ge(*hc_ready(i, m + 1))
                        pool.tensor_tensor(hc[m % RING][:, :], hc[m % RING][:, :], hc[(m - 1) % RING][:, :],
                                           ALU.add).then_inc(pair_ready.sem, 1)

            def add_halves(i):
                pool.wait_ge(*yg_ready[0](i, NE // 2))
                pool.tensor_tensor(yg[:, 0:4, :], yg[:, 0:4, :], yg[:, 4:8, :], ALU.add).then_inc(halves_added.sem, 1)

            pool.wait_ge(*setg(0, "low"))
            scan_outputs(0, False)
            split(0, 0)
            with pool.Fori(1, NG) as i:
                add_halves(i - 1)
                scan_outputs(i, True)
                split(i - 1, 1)
                split(i, 0)
            add_halves(NG - 1)
            split(NG - 1, 1)

        @block.scalar
        def _(act):
            def afn(out_, in_, fn, **kw):
                return act.activation(out_, in_, fn, **kw)

            act.wait_ge(*tokv(0, "r5"))
            afn(feat[:, :], angle[:, :], ACT.Sin).then_inc(toks.sem, 1)
            act.wait_ge(loaded[1].sem, 16)
            for c in range(NG):
                act.wait_ge(*tokp(0, f"w1_{c}"))
                afn(tok_h[:, c, :], bank[c][:, :], ACT.Relu, bias=W("tok_b1")).then_inc(toks.sem, 1)
            for c in range(NG):
                act.wait_ge(*tokp(0, f"w2_{c}"))
                afn(tok_h[:, c, :], bank[4 + c][:, :], ACT.Identity, bias=W("tok_b2")).then_inc(toks.sem, 1)
            for c in range(NG):
                act.wait_ge(*tokp(0, f"cen{c}"))
                afn(tok_sq[:, c, :], bank[c][:, :], ACT.Square).then_inc(toks.sem, 1)
            act.preload_act_table_set("natural_log_exp_and_others")
            act.wait_ge(*tokv(0, "bias"))
            for c in range(NG):
                act.wait_ge(*tokp(0, f"var{c}"))
                afn(tok_rs[:, c, :], bank[4 + c][:, :], ACT.Ln, bias=eps1).then_inc(toks.sem, 1)
            for c in range(NG):
                act.wait_ge(*toks(0, f"ln{c}"))
                afn(tok_rs[:, c, :], tok_rs[:, c, :], ACT.Exp, scale=-0.5).then_inc(toks.sem, 1)
            act.wait_ge(loaded[2].sem, 16)
            afn(a_neg[:, :], W("alog"), ACT.Exp).then_inc(sets.sem, 1)
            afn(bn_s[:, :], W("bn_v"), ACT.Ln, bias=eps1).then_inc(sets.sem, 1)
            act.wait_ge(*sets(0, "ln"))
            afn(bn_s[:, :], bn_s[:, :], ACT.Exp, scale=-0.5).then_inc(sets.sem, 1)
            afn(bn2_s[:, :], W("bn2_v"), ACT.Ln, bias=eps1).then_inc(sets.sem, 1)
            act.wait_ge(*sets(0, "ln2"))
            afn(bn2_s[:, :], bn2_s[:, :], ACT.Exp, scale=-0.5).then_inc(sets.sem, 1)
            for c in range(NG):
                act.wait_ge(*tokv(0, f"xn{c}"))
                afn(tok_sq[:, c, :], tok_sq[:, c, :], ACT.Identity, scale=W("tok_g"), bias=tok_bias[:, :])\
                    .then_inc(toks.sem, 1)
            act.wait_ge(*setg(0, "zero"))
            act.wait_ge(*tokv(0, "h0"))

            def rsqrt(pe_sig, s_sig, i, b, ln="ln", rs_="rs", dst=rs, bias=None, scale=1.0):
                act.wait_ge(*pe_sig(i, "var"))
                afn(dst[:, :], bank[b][:, :], ACT.Ln, bias=bias, scale=scale).then_inc(s_sig.sem, 1)
                act.wait_ge(*s_sig(i, ln))
                afn(dst[:, :], dst[:, :], ACT.Exp, scale=-0.5).then_inc(s_sig.sem, 1)

            def take(i):
                afn(h0[:, :], h_all[:, bass.ds(i * T, T)], ACT.Copy).then_inc(x_s.sem, 1)

            def square_x(i):
                act.wait_ge(*x_t(i, "center"))
                afn(sqx[:, :], bank[3][:, :], ACT.Square).then_inc(x_s.sem, 1)

            def normalise_x(i):
                rsqrt(x_t, x_s, i, 2, dst=rsx, bias=eps1)

            def low_x(i):
                act.wait_ge(*x_v(i, "x"))
                afn(xpad[0:D, :, TAPS - 1:TAPS - 1 + S], xf[:, :][0:D, :].rearrange("p (s t) -> p s t", s=GSEQ),
                    ACT.Copy).then_inc(x_s.sem, 1)

            def square(i, m):
                act.wait_ge(*mt[m](i, "center"))
                afn((sq, sq1)[m][:, :], bank[XB[m]][:, :], ACT.Square).then_inc(ms[m].sem, 1)

            def normalise(i, m):
                t, s = mt[m], ms[m]
                rsqrt(t, s, i, VB[m], dst=(rs, rs1)[m], bias=eps1)
                if m == 0:
                    rsqrt(t, s, i, VB[m], "ln2", "rs2", rs2, bias=eps2, scale=1.0 + EPS)

            def prepare_silu(i):
                act.preload_act_table_set("silu_and_others")
                for d in range(2):
                    act.wait_ge(*prep_t(i, f"conv{d}"))
                    afn(u[d][:, :], bank[2 * d][:, :], ACT.Silu, bias=W("conv_b")[:, d:d + 1]).then_inc(prep_s.sem, 1)
                    act.wait_ge(*prep_t(i, f"z{d}"))
                    afn(z[d][:, :], bank[2 * d + 1][:, :], ACT.Silu).then_inc(prep_s.sem, 1)

            def prepare_delta(i, d):
                dtb = W("dt_b")[:, d:d + 1]
                act.wait_ge(*prep_t(i, f"bc{d}"))
                afn(bc[d][:, :], bank[2 * d][:, :], ACT.Copy).then_inc(prep_s.sem, 1)
                act.wait_ge(*prep_t(i, f"dt{d}"))
                afn(ab[d][:, :], bank[2 * d + 1][:, :], ACT.Abs, bias=dtb).then_inc(prep_s.sem, 1)
                afn(soft[d][:, :], bank[2 * d + 1][:, :], ACT.Relu, bias=dtb).then_inc(prep_s.sem, 1)
                act.wait_ge(*prep_s(i, f"abs{d}"))
                afn(ab[d][:, :], ab[d][:, :], ACT.Exp, scale=-1.0).then_inc(prep_s.sem, 1)
                act.wait_ge(*prep_s(i, f"exp{d}"))
                afn(ab[d][:, :], ab[d][:, :], ACT.Ln, bias=1.0).then_inc(prep_s.sem, 1)

            def scan_inputs(i, m):
                d, n = divmod(m, NSTATE)
                cut = slice(1, S) if d == 0 else slice(0, S - 1)
                if n == 0:
                    act.wait_ge(*prep_v(i, f"delta{d}"))
                if m >= RING:
                    act.wait_ge(*state_ready(i, m + 1 - RING))
                afn(decay[d][m % RING][:, :].rearrange("p (s t) -> p s t", s=GSEQ)[:, :, cut],
                    delta[d][:, :].rearrange("p (s t) -> p s t", s=GSEQ)[:, :, cut], ACT.Exp,
                    scale=a_neg[:, m:m + 1]).then_inc(decay_ready.sem, 1)
                act.wait_ge(*bc_ready(i, m + 1))
                if m >= RING:
                    act.wait_ge(*hc_ready(i, m + 1 - RING))
                afn(c_sb[m % RING][:, :], bank[RB[(2 * m + 1) % 3]][:, :], ACT.Copy).then_inc(c_ready.sem, 1)

            def combine_square(i):
                act.wait_ge(*comb_t(i, "center"))
                afn(sqm[:, :], bank[0][:, :], ACT.Square, bias=cen_t[:, :]).then_inc(comb_s.sem, 1)

            def combine_norm(i):
                rsqrt(comb_t, comb_s, i, 1, dst=rsm, bias=eps1)

            def combine_ff(i):
                for c in range(2):
                    act.wait_ge(*comb_t(i, f"f{c}"))
                    afn(f1[c][:, :], bank[1 + c][:, :], ACT.Relu, bias=ff_b1[:, c:c + 1]).then_inc(comb_s.sem, 1)

            def take_gates(i):
                act.wait_ge(*mt[0](i, "gate_t"))
                afn(gate_t[:, :], bank[GB[0]][0:NE, :], ACT.Copy).then_inc(ms[0].sem, 1)

            def exp_logits(i):
                act.wait_ge(*mv[0](i, "shift"))
                afn(ex[:, :, :], ls[:, :, :], ACT.Exp).then_inc(ms[0].sem, 1)

            def hidden(i, m, before=None):
                bias = (e0_b1[:, :], W("e1_b1"))[m]
                ch = NC[m] // NE
                for c in range(NC[m]):
                    act.wait_ge(*hid_ready[m](i, c + 1))
                    if c >= RING:
                        act.wait_ge(*down_done[m](i, (c - RING) // ch + 1))
                    elif before is not None:
                        act.wait_ge(*down_done[1](before, NE - RING + c + 1))
                    afn(hid[c % RING], bank[UB[c % len(UB)]][:, :], ACT.Gelu, bias=bias[:, c:c + 1])\
                        .then_inc(gelu_ready[m].sem, 1)

            def attention(i, k):
                if k == -1:
                    act.wait_ge(*att_t(i, "center"))
                    afn(sq[:, :], bank[5][:, :], ACT.Square).then_inc(att_s.sem, 1)
                if k == 1:
                    rsqrt(att_t, att_s, i, 6, bias=eps2, scale=1.0 + EPS)
                if k == 3:
                    act.wait_ge(*att_v(i, "xn"))
                    afn(xg[:, :], xg[:, :], ACT.Identity, scale=W("at_g"), bias=W("at_b")).then_inc(att_s.sem, 1)
                h = k - Q_AT
                if 0 <= h < NH:
                    act.wait_ge(*att_t(i, "q"))
                    afn(qv[h][:, :], bank[5][:, :], ACT.Identity, scale=W("heads_q")[:, h:h + 1],
                        bias=bq_vh[:, h:h + 1]).then_inc(att_s.sem, 1)
                if h == NH:
                    afn(qu[:, :], bank[5][:, :], ACT.Identity, scale=-HD ** -0.5, bias=bq_u[:, :])\
                        .then_inc(att_s.sem, 1)
                j = k - E_AT
                if 0 <= j < NU:
                    b, h = divmod(j, NH)
                    act.wait_ge(*e_ready(i, j + 1))
                    if h == 0 and b >= 2:
                        act.wait_ge(*skew_out[b - 2](i, 16))
                    afn(es[b % 2][:, h, :], rel_bank(j)[:, 0:SKEW], ACT.Copy).then_inc(es_ready.sem, 1)
                j = k - P_AT
                if 0 <= j < NU:
                    b, h = divmod(j, NH)
                    act.wait_ge(*ss_ready(i, j + 1))
                    if b >= 2:
                        act.wait_ge(*pt_ready(i, h + 1))
                    afn(pb[:, (b % 2) * NH + h, :], ss[h], ACT.Exp, scale=-1.0, bias=smin[:, j:j + 1],
                        accum_out=ssum[:, j:j + 1]).then_inc(p_ready.sem, 1)
                if k == END:
                    act.wait_ge(*att_t(i, "ctx_t"))
                    afn(ct[:, :], bank[5][:, :], ACT.Copy).then_inc(att_s.sem, 1)

            def together(before, i, after):
                for k in range(-EARLY, END + 2):
                    if i is not None and k + EARLY < NM:
                        scan_inputs(i, k + EARLY)
                    if before is not None and k == GATE_AT:
                        take_gates(before)
                    if before is not None:
                        attention(before, k)
                    if i is not None and k == END - 4:
                        combine_square(i)
                    if after is not None and k == END - 4:
                        take(after)
                    if i is not None and k == END - 3:
                        combine_norm(i)
                    if after is not None and k == END - 3:
                        square_x(after)
                    if after is not None and k == END - 2:
                        normalise_x(after)
                    if i is not None and k == END - 1:
                        combine_ff(i)
                    if after is not None and k == END:
                        low_x(after)
                if before is not None:
                    square(before, 1)
                if i is not None:
                    square(i, 0)
                if before is not None:
                    normalise(before, 1)
                if i is not None:
                    normalise(i, 0)
                if after is not None:
                    prepare_silu(after)
                    act.preload_act_table_set("natural_log_exp_and_others")
                    prepare_delta(after, 0)
                if i is not None:
                    exp_logits(i)
                if after is not None:
                    prepare_delta(after, 1)
                act.preload_act_table_set("gelu_and_others")
                if before is not None:
                    hidden(before, 1)
                if i is not None:
                    hidden(i, 0, before)
                    act.preload_act_table_set("natural_log_exp_and_others")

            take(0)
            square_x(0)
            normalise_x(0)
            low_x(0)
            prepare_silu(0)
            act.preload_act_table_set("natural_log_exp_and_others")
            prepare_delta(0, 0)
            prepare_delta(0, 1)
            together(None, 0, 1)
            with act.Fori(1, NG - 1) as i:
                together(i - 1, i, i + 1)
            together(NG - 2, NG - 1, None)
            together(NG - 1, None, None)

        @block.vector
        def _(dve):
            dve.memset(eps_c[:, 0:1], EPS)
            dve.memset(eps_c[:, 1:2], EPS * EPS).then_inc(tokv.sem, 1)
            dve.wait_ge(loaded[0].sem, 16)
            dve.wait_ge(loaded[1].sem, 16)
            dve.tensor_scalar(tok_bias[:, :], W("tok_bres"), 0.1, W("tok_b"), ALU.mult, ALU.add).then_inc(tokv.sem, 1)
            dve.tensor_copy(angle[:, :], idx_i).then_inc(tokv.sem, 1)
            dve.wait_ge(*tokv(0, "t"))
            dve.tensor_scalar(angle[:, :], angle[:, :], TWO_PI, W("invp"), ALU.mult, ALU.mult).then_inc(tokv.sem, 1)
            dve.wait_ge(*tokv(0, "norm"))
            dve.tensor_scalar(angle[:, :], angle[:, :], W("harm"), W("phase"), ALU.mult, ALU.add)\
                .then_inc(tokv.sem, 1)
            dve.wait_ge(*tokv(0, "angle"))
            dve.tensor_scalar(turns[:, :], angle[:, :], 1.0 / TWO_PI, W("quarter"), ALU.mult, ALU.add)\
                .then_inc(tokv.sem, 1)
            dve.wait_ge(*tokv(0, "k"))
            dve.tensor_scalar(turns[:, :], turns[:, :], ROUND, ROUND, ALU.add, ALU.subtract).then_inc(tokv.sem, 1)
            for n, part in enumerate(TURN):
                dve.wait_ge(*tokv(0, ("kr", "r1", "r2")[n]))
                dve.scalar_tensor_tensor(out=angle[:, :], in0=turns[:, :], scalar=-part, in1=angle[:, :],
                                         op0=ALU.mult, op1=ALU.add).then_inc(tokv.sem, 1)
            dve.wait_ge(*tokv(0, "r3"))
            dve.tensor_scalar(angle[:, :], angle[:, :], W("halfpi"), PI_LO, ALU.add, ALU.min).then_inc(tokv.sem, 1)
            dve.wait_ge(*tokv(0, "r4"))
            dve.tensor_scalar(angle[:, :], angle[:, :], -PI_LO, None, ALU.max).then_inc(tokv.sem, 1)
            dve.wait_ge(*toks(0, "sin"))
            dve.tensor_scalar(feat[:, :], feat[:, :], W("amp"), None, ALU.mult).then_inc(tokv.sem, 1)
            dve.wait_ge(loaded[2].sem, 16)
            for d in range(2):
                for k in range(TAPS):
                    pair, half = divmod(k if d == 0 else TAPS - 1 - k, 2)
                    last = dve.tensor_scalar(conv_s[:, 2 * d + pair, half * D:(half + 1) * D],
                                             W("inx")[:, d * D:(d + 1) * D],
                                             W("conv_w")[:, d * TAPS + k:d * TAPS + k + 1], None, ALU.mult)
            last.then_inc(setv.sem, 1)
            for c in range(NG):
                dve.wait_ge(*toks(0, f"rs{c}"))
                dve.tensor_tensor(tok_sq[:, c, :], bank[c][:, :], tok_rs[:, c, :], ALU.mult).then_inc(tokv.sem, 1)
            def embedded(c):
                dve.wait_ge(*toks(0, f"aff{c}"))
                dve.wait_ge(*tokp(0, f"res{c}"))
                dve.scalar_tensor_tensor(out=h_all[:, c * T:(c + 1) * T], in0=bank[4 + c][:, :], scalar=0.1,
                                         in1=tok_sq[:, c, :], op0=ALU.mult, op1=ALU.add).then_inc(tokv.sem, 1)

            embedded(0)
            dve.wait_ge(*sets(0, "rsq2"))
            dve.tensor_scalar(a_neg[:, :], a_neg[:, :], -1.0, None, ALU.mult).then_inc(setv.sem, 1)
            dve.tensor_scalar(bn_s[:, :], bn_s[:, :], W("bn_g"), None, ALU.mult).then_inc(setv.sem, 1)
            dve.wait_ge(*setv(0, "bns"))
            dve.tensor_scalar(bn_t[:, :], W("bn_m"), bn_s[:, :], -1.0, ALU.mult, ALU.mult).then_inc(setv.sem, 1)
            dve.wait_ge(*setv(0, "bnt0"))
            dve.tensor_scalar(bn_t[:, :], bn_t[:, :], W("bn_b"), None, ALU.add).then_inc(setv.sem, 1)
            dve.tensor_tensor(bn2_d[:, :], W("bn2_m"), W("ff_b2"), ALU.subtract).then_inc(setv.sem, 1)
            dve.tensor_scalar(bn2_s[:, :], bn2_s[:, :], W("bn2_g"), None, ALU.mult).then_inc(setv.sem, 1)
            dve.wait_ge(*setv(0, "bn2s"))
            dve.tensor_scalar(bn2_t[:, :], bn2_d[:, :], bn2_s[:, :], -1.0, ALU.mult, ALU.mult).then_inc(setv.sem, 1)
            dve.wait_ge(*setv(0, "bn2t0"))
            dve.tensor_scalar(bn2_t[:, :], bn2_t[:, :], W("bn2_b"), None, ALU.add).then_inc(setv.sem, 1)
            dve.tensor_scalar(out_s[:, :], W("out_w"), bn_s[:, :], None, ALU.mult).then_inc(setv.sem, 1)
            for d in range(2):
                last = dve.tensor_scalar(skip_w[:, d, :], W("ident"), W("dskip")[:, d:d + 1], None, ALU.mult)
            last.then_inc(setv.sem, 1)
            dve.tensor_scalar(ff_w1[:, :], W("ff_w1"), W("ln_g"), None, ALU.mult).then_inc(setv.sem, 1)
            dve.wait_ge(*setp(0, "ffb"))
            dve.tensor_copy(conv_w[:, :, :], bank[0][:, :].rearrange("p (q n) -> p q n", q=4)).then_inc(setv.sem, 1)
            dve.tensor_copy(delta_w[:, :, :], bank[1][:, 0:2 * P].rearrange("p (d n) -> p d n", d=2))\
                .then_inc(setv.sem, 1)
            dve.tensor_copy(out_w[:, :, :], bank[1][:, 2 * P:2 * P + 2 * D].rearrange("p (d n) -> p d n", d=2))\
                .then_inc(setv.sem, 1)
            dve.tensor_copy(cen_t[:, :], bank[1][:, 3 * P:3 * P + 1]).then_inc(setv.sem, 1)
            dve.tensor_tensor(ff_b1[:, :], bank[1][:, 3 * P + 1:3 * P + 3], W("ff_b1"), ALU.add).then_inc(setv.sem, 1)
            for c in range(1, NG):
                embedded(c)

            def experts_setup():
                dve.wait_ge(loaded[4].sem, 16)
                dve.tensor_scalar(bq_u[:, :], W("at_bq"), W("at_u"), -HD ** -0.5, ALU.add, ALU.mult)
                dve.tensor_tensor(bq_v[:, :], W("at_bq"), W("at_v"), ALU.add).then_inc(setv.sem, 1)
                dve.wait_ge(*setp(0, "e0b"))
                dve.tensor_tensor(e0_b1[:, :], bank[4][:, 0:NE * CH0], W("e0_b1"), ALU.add).then_inc(setv.sem, 1)
                dve.wait_ge(*setp(0, "pos"))
                dve.tensor_scalar(pos[:, :], bank[6][:, 0:2 * S - 1], W("at_bp"), None, ALU.add).then_inc(setv.sem, 1)
                dve.wait_ge(*setv(0, "sums"))
                dve.tensor_scalar(bq_vh[:, :], W("heads_q"), bq_v[:, :], None, ALU.mult).then_inc(setv.sem, 1)
                dve.wait_ge(*setp(0, "bo"))
                dve.tensor_tensor(bo_v[:, :], bank[7][:, 0:1], W("at_bo"), ALU.add).then_inc(setv.sem, 1)

            def normalise_x(i):
                dve.wait_ge(*x_s(i, "rs"))
                dve.tensor_tensor(xf[:, :], bank[3][:, :], rsx[:, :], ALU.mult).then_inc(x_v.sem, 1)
                dve.tensor_tensor(xpad[D:P, :, TAPS - 2:TAPS - 2 + S],
                                  bank[3][D:P, :].rearrange("p (s t) -> p s t", s=GSEQ),
                                  rsx[:, :][D:P, :].rearrange("p (s t) -> p s t", s=GSEQ), ALU.mult)\
                    .then_inc(x_v.sem, 1)

            def residual_x(i):
                dve.wait_ge(*x_v(i, "x"))
                dve.scalar_tensor_tensor(out=hx[:, :], in0=xf[:, :], scalar=bn2_t[:, :], in1=h0[:, :],
                                         op0=ALU.add, op1=ALU.add).then_inc(x_v.sem, 1)

            def prepare(i, d):
                hi, lo = slice(D, P), slice(P - 32, P)
                dve.wait_ge(*prep_s(i, f"part{d}"))
                dve.tensor_tensor(rest[d][hi, :], bank[2 * d][hi, :], bc[d][hi, :], ALU.subtract)\
                    .then_inc(prep_v.sem, 1)
                dve.wait_ge(*prep_v(i, f"rest{d}"))
                dve.tensor_copy(bc[d][hi, :], rest[d][hi, :]).then_inc(prep_v.sem, 1)
                dve.wait_ge(*prep_v(i, f"mid{d}"))
                dve.tensor_tensor(bc[d][lo, :], rest[d][lo, :], bc[d][lo, :], ALU.subtract).then_inc(prep_v.sem, 1)
                dve.wait_ge(*prep_s(i, f"ln{d}"))
                dve.tensor_tensor(delta[d][:, :], ab[d][:, :], soft[d][:, :], ALU.add).then_inc(prep_v.sem, 1)
                dve.wait_ge(*prep_v(i, f"delta{d}"))
                dve.tensor_tensor(du[d][:, :], delta[d][:, :], u[d][:, :], ALU.mult).then_inc(prep_v.sem, 1)

            def driven(i, m):
                dve.wait_ge(*bc_ready(i, m + 1))
                if m % NSTATE == 0:
                    dve.wait_ge(*prep_v(i, f"du{m // NSTATE}"))
                if m >= 2:
                    dve.wait_ge(*state_ready(i, m - 1))
                dve.tensor_tensor(drive[m % 2][:, :], bank[RB[2 * m % 3]][:, :], du[m // NSTATE][:, :], ALU.mult)\
                    .then_inc(drive_ready.sem, 1)

            def gated(i, d):
                dve.wait_ge(*y_sum(i, f"y{d}"))
                dve.tensor_tensor(y[d][:, :], bank[YSUM][:, :], z[d][:, :], ALU.mult).then_inc(y_ready.sem, 1)

            def scan(i, m):
                if m == 0:
                    driven(i, 0)
                if m + 1 < NM:
                    driven(i, m + 1)
                dve.wait_ge(*drive_ready(i, m + 1))
                dve.wait_ge(*decay_ready(i, m + 1))
                if m >= RING:
                    dve.wait_ge(*hc_ready(i, m + 1 - RING))
                way = slice(None) if m < NSTATE else slice(None, None, -1)
                dve.tensor_tensor_scan(state[m % RING][:, way], decay[m // NSTATE][m % RING][:, way],
                                       drive[m % 2][:, way], 0.0, ALU.mult, ALU.add).then_inc(state_ready.sem, 1)

            def combine_fb(i):
                dve.wait_ge(*comb_s(i, "rs"))
                dve.scalar_tensor_tensor(out=fb[:, :], in0=bank[0][:, :], scalar=cen_t[:, :], in1=rsm[:, :],
                                         op0=ALU.add, op1=ALU.mult).then_inc(comb_v.sem, 1)

            def combine_h(i):
                dve.wait_ge(*comb_t(i, "ff"))
                dve.scalar_tensor_tensor(out=h1[:, :], in0=bank[0][:, :], scalar=bn2_s[:, :], in1=hx[:, :],
                                         op0=ALU.mult, op1=ALU.add).then_inc(comb_v.sem, 1)

            def normalise(i, m):
                s, v = ms[m], mv[m]
                dve.wait_ge(*s(i, "rs"))
                if m == 0:
                    lo = slice(0, D)
                    dve.tensor_tensor(xa[lo, :], bank[XB[0]][lo, :], rs[lo, :], ALU.mult).then_inc(v.sem, 1)
                    dve.wait_ge(*s(i, "rs2"))
                for x in (xn[m], x_hi[m]):
                    dve.tensor_tensor(x[:, :], bank[XB[m]][:, :], (rs2, rs1)[m][:, :], ALU.mult).then_inc(v.sem, 1)

            def ranks(i, m):
                v = mv[m]
                dve.wait_ge(*mt[m](i, "logits"))
                bias = W("e0_br") if m == 0 else W("e1_bg")
                dve.tensor_tensor(lg[:, :, :], bank[LB[m]][:, 0:TILES * NE].rearrange("p (b e) -> p b e", e=NE),
                                  bias.unsqueeze(1).to_broadcast([P, TILES, NE]), ALU.add).then_inc(v.sem, 1)
                dve.wait_ge(*v(i, "logits"))
                if m == 0:
                    dve.tensor_reduce(mx[:, :], lg[:, :, :], AX.X, ALU.max).then_inc(v.sem, 1)
                    dve.wait_ge(*v(i, "max"))
                    dve.tensor_tensor(ls[:, :, :], lg[:, :, :], mx[:, :].unsqueeze(2).to_broadcast([P, TILES, NE]),
                                      ALU.subtract).then_inc(v.sem, 1)
                mine = lg[:, :, :].unsqueeze(3).to_broadcast([P, TILES, NE, NE])
                other = lg[:, :, :].unsqueeze(2).to_broadcast([P, TILES, NE, NE])
                dve.tensor_tensor(gt[:, :, :, :], other, mine, ALU.is_gt).then_inc(v.sem, 1)
                dve.tensor_tensor(eq[:, :, :, :], other, mine, ALU.is_equal).then_inc(v.sem, 1)
                dve.wait_ge(*v(i, "eq"))
                tri = W("tri").rearrange("p (a b) -> p a b", a=NE).unsqueeze(1).to_broadcast([P, TILES, NE, NE])
                dve.tensor_tensor(eq[:, :, :, :], eq[:, :, :, :], tri, ALU.mult).then_inc(v.sem, 1)
                dve.wait_ge(*v(i, "tie"))
                dve.tensor_tensor(gt[:, :, :, :], gt[:, :, :, :], eq[:, :, :, :], ALU.add).then_inc(v.sem, 1)
                dve.wait_ge(*v(i, "sum"))
                dve.tensor_reduce(rank[:, :, :], gt[:, :, :, :], AX.X, ALU.add).then_inc(v.sem, 1)

            def gates(i, m):
                s, v = ms[m], mv[m]
                dve.wait_ge(*v(i, "rank"))
                if m == 0:
                    dve.wait_ge(*s(i, "exp"))
                    dve.scalar_tensor_tensor(out=wt[:, :, :], in0=rank[:, :, :], scalar=1.5, in1=ex[:, :, :],
                                             op0=ALU.is_lt, op1=ALU.mult).then_inc(v.sem, 1)
                    dve.wait_ge(*v(i, "masked"))
                    dve.tensor_reduce(sw[:, :], wt[:, :, :], AX.X, ALU.add).then_inc(v.sem, 1)
                    dve.wait_ge(*v(i, "wsum"))
                    dve.reciprocal(rw[:, :], sw[:, :]).then_inc(v.sem, 1)
                    dve.wait_ge(*v(i, "wrec"))
                    dve.tensor_tensor(gate[0][:, :, :], wt[:, :, :], rw[:, :].unsqueeze(2).to_broadcast([P, TILES, NE]),
                                      ALU.mult).then_inc(v.sem, 1)
                else:
                    dve.tensor_scalar(gate[1][:, :, :], rank[:, :, :], 1.5, None, ALU.is_lt).then_inc(v.sem, 1)

            def weigh(i, m):
                v = mv[m]
                dve.wait_ge(*v(i, "gate"))
                for q in range(NE // 2):
                    dve.wait_ge(*down_done[m](i, 2 * q + 2))
                    gates_ = gate[m][:, :, 2 * q:2 * q + 2].rearrange("p b e -> p e b").unsqueeze(3)
                    dve.tensor_tensor(yg[:, 2 * q:2 * q + 2, :].rearrange("p e (b n) -> p e b n", b=TILES),
                                      bank[YB[q % 2]][:, :].rearrange("p (e b n) -> p e b n", e=2, b=TILES),
                                      gates_.to_broadcast([P, 2, TILES, D]), ALU.mult)\
                        .then_inc(yg_ready[m].sem, 1)

            def add_up(i, m, step):
                t, v = mt[m], mv[m]
                if step == 0:
                    dve.wait_ge(*yg_ready[m](i, NE // 2))
                    dve.tensor_tensor(yg[:, 0:4, :], yg[:, 0:4, :], yg[:, 4:8, :], ALU.add).then_inc(v.sem, 1)
                    dve.wait_ge(*t(i, "gate_t"))
                    dve.tensor_copy(gate_t[:, :], bank[GB[m]][0:NE, :]).then_inc(v.sem, 1)
                if step == 1:
                    dve.wait_ge(*(v(i, "add1") if m else halves_added(i, "done")))
                    dve.tensor_tensor(yg[:, 0:2, :], yg[:, 0:2, :], yg[:, 2:4, :], ALU.add).then_inc(v.sem, 1)
                if step == 2:
                    dve.wait_ge(*v(i, "add2"))
                    if m == 0:
                        parts = (yg[:, k, :].rearrange("p (b n) -> p b n", b=TILES).unsqueeze(2)
                                 .to_broadcast([P, TILES, 2, D]) for k in range(2))
                        dve.tensor_tensor(acc2[:, :, :].rearrange("p b (a n) -> p b a n", a=2), *parts, ALU.add)\
                            .then_inc(v.sem, 1)
                    else:
                        dve.tensor_tensor(acc, yg[:, 0, :], yg[:, 1, :], ALU.add).then_inc(v.sem, 1)
                if step == 3:
                    dve.wait_ge(*t(i, "sum"))
                    if m == 0:
                        dve.tensor_tensor(h2[:, :], bank[OB[0]][:, :], h1[:, :], ALU.add).then_inc(v.sem, 1)
                    else:
                        dve.wait_ge(*v(i, "add3"))
                        dve.tensor_tensor(fin[:, :, :].rearrange("p b n -> p (b n)"), bank[OB[1]][:, 0:TILES * D],
                                          acc, ALU.add).then_inc(v.sem, 1)

            def attention(i, k):
                if k == 2:
                    dve.wait_ge(*att_s(i, "rs"))
                    dve.tensor_tensor(xg[:, :], bank[5][:, :], rs[:, :], ALU.mult).then_inc(att_v.sem, 1)
                h = k - Q_AT - 1
                if 0 <= h < NH:
                    last = dve.tensor_scalar(kk[h][:, :], bank[6][:, :], W("at_bk"), W("heads")[:, h:h + 1],
                                             ALU.add, ALU.mult)
                    if h == NH - 1:
                        last.then_inc(att_v.sem, 1)
                if k == Q_AT:
                    dve.wait_ge(*att_t(i, "v"))
                    dve.tensor_copy(vv[:, :, :], bank[7][:, 0:TILES * D].rearrange("p (b n) -> p b n", b=TILES))\
                        .then_inc(att_v.sem, 1)
                j = k - S_AT
                if 0 <= j < NU:
                    b, h = divmod(j, NH)
                    if h == 0:
                        dve.wait_ge(*skew_in[b](i, 16))
                    dve.wait_ge(*s_ready(i, j + 1))
                    if j >= RING:
                        dve.wait_ge(*p_ready(i, j + 1 - RING))
                    dve.memset(held[:, j:j + 1], 0.0)
                    dve.tensor_tensor_reduce(out=ss[h], in0=bank[SB[j % 2]][:, 0:S],
                                             in1=ps[:, b, h, :], scale=1.0, scalar=3.0e38, op0=ALU.add,
                                             op1=ALU.min, accum_out=smin[:, j:j + 1]).then_inc(ss_ready.sem, 1)
                for s, at_ in enumerate(T_AT):
                    h = k - at_
                    if 0 <= h < NH:
                        n = s * NH + h
                        dve.wait_ge(*pt_ready(i, n + 1))
                        if n >= 2:
                            dve.wait_ge(*ctx_ready(i, n - 1))
                        dve.tensor_copy(ptc[n % 2][:, :, :], bank[TB][:, :].rearrange("p (a t) -> p a t", a=2))\
                            .then_inc(ptc_ready.sem, 1)
                if k == END - 1:
                    dve.wait_ge(*p_ready(i, NU))
                    dve.reciprocal(rsum[:, :], ssum[:, :]).then_inc(att_v.sem, 1)
                if k == END:
                    dve.wait_ge(*att_v(i, "rsum"))
                    dve.wait_ge(*ctx_ready(i, GSEQ * NH))
                    for a in range(2):
                        last = dve.tensor_tensor(
                            cn[:, :, a, :].rearrange("p b (h n) -> p b h n", n=HD),
                            bank[CB][:, 0:TILES * D].rearrange("p (b h n) -> p b h n", h=NH, n=HD),
                            rsum[:, :].rearrange("p (b h) -> p b h", h=NH).unsqueeze(3)
                            .to_broadcast([P, TILES, NH, HD]), ALU.mult)
                    last.then_inc(att_v.sem, 1)
                if k == END + 1:
                    dve.wait_ge(*att_t(i, "out"))
                    dve.scalar_tensor_tensor(out=h3[:, :], in0=bank[6][:, :], scalar=bo_v[:, :], in1=h2[:, :],
                                             op0=ALU.add, op1=ALU.add).then_inc(att_v.sem, 1)

            def together(before, i, after):
                for k in range(-EARLY, END + 2):
                    if before is not None:
                        attention(before, k)
                    if i is not None and k + EARLY < NM:
                        scan(i, k + EARLY)
                    if before is not None and k in ADD_AT:
                        add_up(before, 0, ADD_AT.index(k) + 1)
                    if i is not None:
                        if k + EARLY == NSTATE - 1 + LAG:
                            gated(i, 0)
                        if k + EARLY == NM + LAG:
                            gated(i, 1)
                        if k == END - 2:
                            combine_fb(i)
                    if after is not None and k == END - 1:
                        normalise_x(after)
                    if i is not None and k == END:
                        combine_h(i)
                if before is not None:
                    normalise(before, 1)
                if i is not None:
                    normalise(i, 0)
                if before is not None:
                    ranks(before, 1)
                    gates(before, 1)
                if after is not None:
                    dve.wait_ge(*comb_v(i, "h1"))
                    residual_x(after)
                if i is not None:
                    ranks(i, 0)
                if after is not None:
                    prepare(after, 0)
                if after is not None:
                    prepare(after, 1)
                if i is not None:
                    gates(i, 0)
                if before is not None:
                    weigh(before, 1)
                    for step in range(4):
                        add_up(before, 1, step)
                if i is not None:
                    weigh(i, 0)

            normalise_x(0)
            residual_x(0)
            prepare(0, 0)
            prepare(0, 1)
            experts_setup()
            together(None, 0, 1)
            with dve.Fori(1, NG - 1) as i:
                together(i - 1, i, i + 1)
            together(NG - 2, NG - 1, None)
            together(NG - 1, None, None)

        @block.tensor
        def _(pe):
            def mm(out_, lhsT, rhs, start=True, stop=True):
                return pe.matmul(out_, lhsT, rhs, start=start, stop=stop)

            def rows(c):
                return slice(32 * c, 32 * c + FD)

            pe.wait_ge(loaded[1].sem, 16)
            pe.wait_ge(*tokv(0, "feat"))
            for c in range(NG):
                mm(bank[c][:, :], W("tok_w1", rows(c)), feat[rows(c), :]).then_inc(tokp.sem, 1)
            for c in range(NG):
                pe.wait_ge(*toks(0, f"relu{c}"))
                mm(bank[4 + c][:, :], W("tok_w2"), tok_h[:, c, :]).then_inc(tokp.sem, 1)
            for c in range(NG):
                pe.wait_ge(*toks(0, f"h2_{c}"))
                mm(bank[c][:, :], W("center"), tok_h[:, c, :]).then_inc(tokp.sem, 1)
            for c in range(NG):
                pe.wait_ge(*toks(0, f"sq{c}"))
                mm(bank[4 + c][:, :], W("mean"), tok_sq[:, c, :]).then_inc(tokp.sem, 1)
            for c in range(NG):
                pe.wait_ge(*toks(0, f"ln{c}"))
                mm(bank[4 + c][:, :], W("tok_wres", rows(c)), feat[rows(c), :]).then_inc(tokp.sem, 1)

            pe.wait_ge(loaded[2].sem, 16)
            pe.wait_ge(*tokv(0, f"xn{NG - 1}"))
            for q in range(4):
                last = pe.transpose(bank[0][:, q * P:(q + 1) * P], conv_s[:, q, :], W("ident"))
            last.then_inc(setp.sem, 1)
            for d in range(2):
                last = mm(bank[1][:, d * P:(d + 1) * P], W("xp_dt", slice(0, RANK))[:, d * P:(d + 1) * P],
                          W("dt_w", slice(0, RANK))[:, d * P:(d + 1) * P])
            last.then_inc(setp.sem, 1)
            lo = slice(0, D)

            def mamba_setup():
                pe.wait_ge(*setv(0, "outs"))
                mm(bank[1][:, 2 * P:3 * P], out_s[:, :], W("center2")).then_inc(setp.sem, 1)
                mm(bank[1][:, 3 * P:3 * P + 1], W("center2"), bn_t[:, :]).then_inc(setp.sem, 1)
                for c in range(2):
                    last = mm(bank[1][:, 3 * P + 1 + c:3 * P + 2 + c], W("ff_w1")[:, c * P:(c + 1) * P], W("ln_b"))
                last.then_inc(setp.sem, 1)

            def experts_setup():
                pe.wait_ge(loaded[4].sem, 16)
                pe.wait_ge(loaded[5].sem, 16)
                pe.wait_ge(*tokv(0, f"h{NG - 1}"))
                for c in range(NE * CH0):
                    last = mm(bank[4][:, c:c + 1], W("w1", lo)[:, c * P:(c + 1) * P],
                              W("e0_lb", lo)[:, c // CH0:c // CH0 + 1])
                last.then_inc(setp.sem, 1)
                mm(bank[6][:, 0:2 * S - 1], W("at_wp", lo), W("enc", lo)).then_inc(setp.sem, 1)
                mm(bank[7][:, 0:1], W("at_wo", lo), W("at_bv", lo)).then_inc(setp.sem, 1)

            def centred(t, src, b):
                mm(bank[b][:, :], W("center"), src[:, :]).then_inc(t.sem, 1)

            def variances(i, t, s, b, squares):
                pe.wait_ge(*s(i, "sq"))
                mm(bank[b][:, :], W("mean"), squares[:, :]).then_inc(t.sem, 1)

            def prepare_in(i):
                taps = ((0, 2), (TAPS - 1, TAPS + 1))
                pe.wait_ge(*x_v(i, "high"))
                pe.wait_ge(*x_s(i, "low"))
                for d in range(2):
                    o = bank[2 * d][:, :].rearrange("p (s t) -> p s t", s=GSEQ)
                    for q in range(2):
                        last = mm(o, conv_w[:, 2 * d + q, :], xpad[:, :, taps[d][q]:taps[d][q] + S],
                                  start=(q == 0), stop=(q == 1))
                    last.then_inc(prep_t.sem, 1)
                    mm(bank[2 * d + 1][:, :].rearrange("p (s t) -> p s t", s=GSEQ), W("inz")[:, d * P:(d + 1) * P],
                       xpad[:, :, TAPS - 1:TAPS - 1 + S]).then_inc(prep_t.sem, 1)

            def prepare_xp(i):
                for d in range(2):
                    pe.wait_ge(*prep_s(i, f"z{d}"))
                    mm(bank[2 * d][:, :], W("bc_w")[:, d * P:(d + 1) * P], u[d][:, :]).then_inc(prep_t.sem, 1)
                    mm(bank[2 * d + 1][:, :], delta_w[:, d, :], u[d][:, :]).then_inc(prep_t.sem, 1)

            def rows_out(i, m):
                d, n = divmod(m, NSTATE)
                if n == 0:
                    pe.wait_ge(*prep_v(i, f"low{d}"))
                if m == 0:
                    pe.wait_ge(*prep_v(i, "delta0"))
                if m == 1:
                    pe.wait_ge(*prep_v(i, "rest1"))
                    pe.wait_ge(*drive_ready(i, 1))
                if m >= 2:
                    pe.wait_ge(*drive_ready(i, m))
                    pe.wait_ge(*c_ready(i, m - 1))
                mm(bank[RB[2 * m % 3]][:, :], sel[:, n:n + 1].to_broadcast([P, P]), bc[d][:, :])
                mm(bank[RB[(2 * m + 1) % 3]][:, :], sel[:, NSTATE + n:NSTATE + n + 1].to_broadcast([P, P]),
                   bc[d][:, :]).then_inc(bc_ready.sem, 1)

            def summed(i, m, paired):
                d, n = divmod(m, NSTATE)
                if m == 0:
                    pe.wait_ge(*prep_s(i, "ln1"))
                if m == NSTATE:
                    pe.wait_ge(*y_ready(i, "y0"))
                paired = paired and m >= PAIRED
                if paired and m % 2 == 0:
                    return
                if paired:
                    pe.wait_ge(*pair_ready(i - 1, (m - PAIRED + 1) // 2))
                else:
                    pe.wait_ge(*hc_ready(i, m + 1))
                mm(bank[YSUM][:, :], W("ident"), hc[m % RING][:, :], start=(n == int(paired)), stop=False)\
                    .then_inc(sum_done.sem, 2 if paired else 1)
                if n == NSTATE - 1:
                    mm(bank[YSUM][:, :], skip_w[:, d, :], u[d][:, :], start=False).then_inc(y_sum.sem, 1)

            def combine_out(i):
                pe.wait_ge(*y_ready(i, "y1"))
                pe.wait_ge(*c_ready(i, NM))
                mm(bank[0][:, :].rearrange("p (s t) -> p s t", s=GSEQ), W("centerd"),
                   xpad[:, :, TAPS - 1:TAPS - 1 + S], stop=False)
                for d in range(2):
                    last = mm(bank[0][d * D:(d + 1) * D, :], out_w[:, d, :], y[d][:, :], start=False)
                last.then_inc(comb_t.sem, 1)

            def combine_var(i):
                pe.wait_ge(*comb_s(i, "sq"))
                mm(bank[1][:, :], W("mean2"), sqm[:, :]).then_inc(comb_t.sem, 1)

            def combine_f(i):
                pe.wait_ge(*comb_v(i, "fb"))
                for c in range(2):
                    mm(bank[1 + c][:, :], ff_w1[:, c * P:(c + 1) * P], fb[:, :]).then_inc(comb_t.sem, 1)

            def combine_ff(i):
                for c in range(2):
                    pe.wait_ge(*comb_s(i, f"g{c}"))
                    last = mm(bank[0][:, :], W("ff_w2")[:, c * P:(c + 1) * P], f1[c][:, :], start=(c == 0),
                              stop=(c == 1))
                last.then_inc(comb_t.sem, 1)

            def logits(i, m):
                t, v = mt[m], mv[m]
                pe.wait_ge(*v(i, "high"))
                wr = W("e0_wr", lo) if m == 0 else W("e1_wg", lo)
                for b in range(TILES):
                    last = mm(bank[LB[m]][:, b * NE:(b + 1) * NE], (xa, xn[1])[m][lo, b * P:(b + 1) * P], wr)
                last.then_inc(t.sem, 1)

            def experts(i, m, before=None):
                v, ch = mv[m], NC[m] // NE

                def up(c):
                    if c < len(UB) and before is not None:
                        pe.wait_ge(*gelu_ready[1](before, NE - len(UB) + c + 1))
                    if c == 1 and m == 1:
                        pe.wait_ge(*v(i, "logits"))
                    if c >= len(UB):
                        pe.wait_ge(*gelu_ready[m](i, c + 1 - len(UB)))
                    o, col = bank[UB[c % len(UB)]][:, :], slice((FIRST[m] + c) * P, (FIRST[m] + c + 1) * P)
                    if c == 0:
                        pe.wait_ge(*v(i, "high"))
                    mm(o, w1_a[:, col], x_hi[m][:, :], stop=False)
                    if c == 0:
                        pe.wait_ge(*x_parts[m](i, "mid"))
                    mm(o, w1_a[:, col], x_mid[m][:, :], start=False, stop=False)
                    if c == 0:
                        pe.wait_ge(*x_parts[m](i, "again"))
                    mm(o, w1_b[:, col], x_lo[m][:, :], start=False).then_inc(hid_ready[m].sem, 1)

                def down(e):
                    pe.wait_ge(*gelu_ready[m](i, (e + 1) * ch))
                    if e in (0, 2) and before is not None:
                        pe.wait_ge(*yg_ready[1](before, 3 + e // 2))
                    if e >= 4:
                        pe.wait_ge(*yg_ready[m](i, e // 2 - 1))
                    w2 = W("e0_w2") if m == 0 else W("e1_w2")
                    for b in range(TILES):
                        at_ = (e % 2) * TILES * D + b * D
                        for c in range(ch):
                            n = (e * ch + c) * D
                            last = mm(bank[YB[e // 2 % 2]][:, at_:at_ + D], hid[(e * ch + c) % RING][:, b * P:(b + 1) * P],
                                      w2[:, n:n + D], start=(c == 0), stop=(c == ch - 1))
                    last.then_inc(down_done[m].sem, 1)

                for e in range(NE + 1):
                    if e < NE:
                        for c in range(ch):
                            up(e * ch + c)
                    if e >= 1:
                        down(e - 1)
                    if e == 2 and before is not None:
                        sum_up(before, 1, h3)
            def turn_gates(i, m):
                t, v = mt[m], mv[m]
                pe.wait_ge(*v(i, "gate"))
                for b in range(TILES):
                    last = mm(bank[GB[m]][0:NE, b * P:(b + 1) * P], gate[m][:, b, :], W("ident"))
                last.then_inc(t.sem, 1)

            def gated_bias(i):
                pe.wait_ge(*ms[0](i, "gate_t"))
                mm(bank[OB[0]][:, :], W("e0_b2", slice(0, NE)), gate_t[:, :], stop=False)

            def sum_up(i, m, src):
                t, v = mt[m], mv[m]
                pe.wait_ge(*v(i, "add3"))
                if m == 0:
                    for b in range(TILES):
                        last = mm(bank[OB[0]][:, b * P:(b + 1) * P], acc2[:, b, :], W("ident"), start=False,
                                  stop=(b == TILES - 1))
                else:
                    for b in range(TILES):
                        o = bank[OB[1]][:, b * D:(b + 1) * D]
                        mm(o, gate_t[:, b * P:(b + 1) * P], W("e1_b2", slice(0, NE)), stop=False)
                        last = mm(o, src[lo, b * P:(b + 1) * P], W("ident", lo)[:, 0:D], start=False)
                last.then_inc(t.sem, 1)

            def weighted(i, n):
                s, h = divmod(n, NH)
                pe.wait_ge(*ptc_ready(i, n + 1))
                for q in range(2):
                    at_ = (2 * s + q) * D + h * HD
                    for a in range(2):
                        last = mm(bank[CB][:, at_:at_ + HD], ptc[n % 2][:, a, q * P:(q + 1) * P],
                                  vv[:, 2 * s + a, h * HD:(h + 1) * HD], start=(a == 0), stop=(a == 1))
                last.then_inc(ctx_ready.sem, 1)

            def attention(i, k):
                if k == -2:
                    pe.wait_ge(*mv[0](i, "h"))
                    centred(att_t, h2, 5)
                if k == 0:
                    variances(i, att_t, att_s, 6, sq)
                if k == Q_AT - 0:
                    pe.wait_ge(*att_s(i, "xg"))
                    mm(bank[5][:, :], W("at_wq"), xg[:, :]).then_inc(att_t.sem, 1)
                if k == Q_AT + 0:
                    mm(bank[6][:, :], W("at_wk"), xg[:, :]).then_inc(att_t.sem, 1)
                if k == Q_AT + 1:
                    for b in range(TILES):
                        last = mm(bank[7][:, b * D:(b + 1) * D], xg[lo, b * P:(b + 1) * P], W("at_wv", lo))
                    last.then_inc(att_t.sem, 1)
                j = k - E_AT
                if 0 <= j < NU:
                    b, h = divmod(j, NH)
                    if b == 0:
                        pe.wait_ge(*att_s(i, f"qv{h}"))
                    first = P if b % 2 == 0 else 0
                    if j == 1:
                        pe.wait_ge(*att_v(i, "v"))
                    if j == 8:
                        pe.wait_ge(*att_v(i, "k"))
                    if j >= 2:
                        pe.wait_ge(*es_ready(i, j - 1))
                    mm(rel_bank(j)[:, 0:SKEW], qv[h][:, b * P:(b + 1) * P], pos[:, first:first + SKEW])\
                        .then_inc(e_ready.sem, 1)
                j = k - S_AT
                if 0 <= j < NU:
                    b, h = divmod(j, NH)
                    if j == 0:
                        pe.wait_ge(*att_s(i, "qu"))
                    if j >= 2:
                        pe.wait_ge(*ss_ready(i, j - 1))
                    mm(bank[SB[j % 2]][:, 0:S], qu[:, b * P:(b + 1) * P],
                       kk[h][:, (b // 2) * S:(b // 2 + 1) * S]).then_inc(s_ready.sem, 1)
                for s, at_ in enumerate(T_AT):
                    h = k - at_
                    n = s * NH + h
                    if 0 < h <= NH:
                        weighted(i, n - 1)
                    if 0 <= h < NH:
                        pe.wait_ge(*p_ready(i, (2 * s + 1) * NH + h + 1))
                        if n == 0:
                            pe.wait_ge(*es_ready(i, NU))
                        for a in range(2):
                            for q in range(2):
                                last = pe.transpose(bank[TB][:, a * S + q * P:a * S + (q + 1) * P],
                                                    pb[:, q * NH + h, a * P:(a + 1) * P], W("ident"))
                        last.then_inc(pt_ready.sem, 1)
                if k == END:
                    pe.wait_ge(*att_v(i, "cn"))
                    for b in range(TILES):
                        last = mm(bank[5][:, b * P:(b + 1) * P], cn[:, b, :, :].rearrange("p a n -> p (a n)"), W("ident"))
                    last.then_inc(att_t.sem, 1)
                if k == END + 1:
                    pe.wait_ge(*att_s(i, "ctx_t"))
                    mm(bank[6][:, :], W("at_wo"), ct[:, :]).then_inc(att_t.sem, 1)

            def centred_x(i):
                pe.wait_ge(*x_s(i, "h0"))
                centred(x_t, h0, 3)

            def together(before, i, after):
                for k in range(-EARLY, END + 2):
                    if i is not None and k + EARLY < NM:
                        rows_out(i, k + EARLY)
                    if before is not None:
                        if k == TURN_AT:
                            turn_gates(before, 0)
                        if k == BIAS_AT:
                            gated_bias(before)
                        if k == SUM_AT:
                            sum_up(before, 0, h1)
                        if k >= 0:
                            attention(before, k)
                    if i is not None:
                        if LAG <= k + EARLY < NM + LAG:
                            summed(i, k + EARLY - LAG, before is not None)
                    if before is not None and k < 0:
                        attention(before, k)
                    if i is not None:
                        if k + EARLY == NM + LAG:
                            combine_out(i)
                        if k == END - 4:
                            combine_var(i)
                    if after is not None and k == END - 4:
                        centred_x(after)
                    if after is not None and k == END - 3:
                        variances(after, x_t, x_s, 2, sqx)
                    if i is not None and k == END - 2:
                        if after is not None:
                            pe.wait_ge(*x_s(after, "ln"))
                        combine_f(i)
                    if i is not None and k == END - 1:
                        combine_ff(i)
                if before is not None:
                    pe.wait_ge(*att_v(before, "h"))
                    centred(mt[1], h3, XB[1])
                if i is not None:
                    pe.wait_ge(*comb_v(i, "h1"))
                    centred(mt[0], h1, XB[0])
                if before is not None:
                    variances(before, mt[1], ms[1], VB[1], sq1)
                if i is not None:
                    if before is None:
                        pe.wait_ge(*setv(0, "bo"))
                        pe.wait_ge(*setg(0, "low"))
                    variances(i, mt[0], ms[0], VB[0], sq)
                if after is not None:
                    prepare_in(after)
                if before is not None:
                    logits(before, 1)
                if i is not None:
                    logits(i, 0)
                if after is not None:
                    prepare_xp(after)
                if before is not None:
                    if i is not None:
                        pe.wait_ge(*mv[0](i, "logits"))
                    experts(before, 1)
                    turn_gates(before, 1)
                if i is not None:
                    experts(i, 0, before)
                elif before is not None:
                    sum_up(before, 1, h3)

            centred_x(0)
            mamba_setup()
            variances(0, x_t, x_s, 2, sqx)
            pe.wait_ge(*setv(0, "ffb"))
            prepare_in(0)
            prepare_xp(0)
            experts_setup()
            pe.wait_ge(loaded[3].sem, 16)
            together(None, 0, 1)
            with pe.Fori(1, NG - 1) as i:
                together(i - 1, i, i + 1)
            together(NG - 2, NG - 1, None)
            together(NG - 1, None, None)


def host_arrays(a):
    f = np.float32
    part = {}

    def put(name, rows, value):
        k, at, n = places()[name]
        value = np.asarray(value, f)
        part.setdefault(k, np.zeros((P, WIDTHS[k]), f))[rows, at:at + n] = value.reshape(value.shape[0], n)

    def col(v, times=1):
        return np.tile(np.asarray(v, f).reshape(-1), times)[:, None]

    every, lo, hi = slice(0, P), slice(0, D), slice(D, P)
    for c in range(NG):
        r = slice(32 * c, 32 * c + FD)
        per, harm, kind = np.meshgrid(np.arange(4), np.arange(HARM), np.arange(2), indexing="ij")
        put("invp", r, col(1.0 / np.array(PERIODS)[per]))
        put("harm", r, col(harm + 1.0))
        put("phase", r, col(a["L0_tok_ph"][per, harm]))
        put("amp", r, col(a["L0_tok_hw"][per, harm]))
        put("quarter", r, col(0.25 * kind))
        put("halfpi", r, col(0.5 * math.pi * kind))
        put("tok_w1", r, a["L0_tok_W1"])
        put("tok_wres", r, np.tile(a["L0_tok_Wres"], (1, 2)))
    put("tok_b1", every, col(a["L0_tok_b1"]))
    put("tok_b2", every, col(a["L0_tok_b2"], 2))
    put("tok_g", every, col(a["L0_tok_gamma"], 2))
    put("tok_b", every, col(a["L0_tok_beta"], 2))
    put("tok_bres", every, col(a["L0_tok_bres"], 2))
    put("tok_w2", every, np.tile(a["L0_tok_W2"], (1, 2)))
    cen = np.eye(D) - 1.0 / D
    zero = np.zeros((D, D))
    put("center", every, np.eye(P) - 1.0 / P * np.ones((P, P)))
    put("mean", every, np.full((P, P), 1.0 / P))
    put("ident", every, np.eye(P))
    put("mean2", every, np.kron(np.eye(2), np.full((D, D), 1.0 / D)))
    put("center2", every, np.block([[cen, zero], [zero, cen]]))
    put("centerd", lo, np.tile(cen, (1, 2)))

    m = {k[len("L0_attn_mamba_"):]: v for k, v in a.items() if k.startswith("L0_attn_mamba_")}
    both = lambda fn: np.concatenate([fn(d) for d in range(2)], axis=1)
    inner = 2 * D
    put("inx", every, both(lambda d: m["in_w"][d, :inner]))
    put("conv_w", every, both(lambda d: m["conv_w"][d]))
    put("conv_b", every, m["conv_b"].T)
    put("inz", lo, both(lambda d: m["in_w"][d, inner:].T))
    put("bc_w", every, both(lambda d: np.tile(m["xproj_w"][d, RANK:].T, (1, 4))))
    put("xp_dt", slice(0, RANK), both(lambda d: m["xproj_w"][d, :RANK]))
    put("dt_w", slice(0, RANK), both(lambda d: m["dt_w"][d].T))
    put("dt_b", every, m["dt_b"].T)
    put("alog", every, both(lambda d: m["Alog"][d]))
    put("dskip", every, m["D"].T)
    put("out_w", every, m["out_w"].reshape(P, P))
    for name, key in (("g", "gamma"), ("b", "beta"), ("m", "mean"), ("v", "var")):
        v = a["L0_attn_bn_" + key]
        put("bn_" + name, every, col(v[:2]))
        put("bn2_" + name, every, col(v[2], 2))
    put("ln_g", every, col(a["L0_attn_ln_gamma"][:2]))
    put("ln_b", every, col(a["L0_attn_ln_beta"][:2]))
    put("ff_w1", every, np.tile(a["L0_attn_ff_w1"].T, (2, 1)))
    put("ff_b1", every, a["L0_attn_ff_b1"].reshape(2, P).T)
    put("ff_w2", every, np.concatenate([np.tile(a["L0_attn_ff_w2"].T[c * P:(c + 1) * P], (1, 2)) for c in range(2)], 1))
    put("ff_b2", every, col(a["L0_attn_ff_b2"], 2))

    put("tri", every, np.tile(np.tril(np.ones((NE, NE)), -1).reshape(1, -1), (P, 1)))
    e = {k[len("L0_ffn_"):]: v for k, v in a.items() if k.startswith("L0_ffn_")}
    w1 = [a[f"L{n}_ffn_W1"].transpose(1, 0, 2).reshape(D, -1) for n in range(2)]
    put("w1", every, np.tile(np.concatenate(w1, axis=1), (2, 1)))
    put("w1_g", every, np.tile(np.concatenate([np.repeat(e["ln_g"].T, CH0, axis=1), np.ones((D, NE))], axis=1), (2, 1)))
    put("e0_lb", lo, e["ln_b"].T)
    put("e0_b1", every, e["b1"].reshape(NE * CH0, P).T)
    put("e0_w2", every, e["W2"].reshape(NE * CH0, P, D).transpose(1, 0, 2))
    put("e0_b2", slice(0, NE), np.tile(e["b2"], (1, 2)))
    put("e0_wr", lo, e["Wr"])
    put("e0_br", every, np.tile(e["br"], (P, 1)))

    t = {k[len("L1_attn_"):]: v for k, v in a.items() if k.startswith("L1_attn_")}

    def padded(v):
        v = np.asarray(v, f).reshape(NH, HD, -1)
        return np.concatenate([v, np.zeros_like(v)], axis=1).reshape(P, -1)

    put("at_g", every, col(t["ln_gamma"], 2))
    put("at_b", every, col(t["ln_beta"], 2))
    for name, key in (("wq", "Wq"), ("wk", "Wk"), ("wp", "Wpos")):
        put("at_" + name, lo, padded(t[key]).T)
    for name, key in (("bq", "bq"), ("bk", "bk"), ("bp", "bpos"), ("u", "u_bias"), ("v", "v_bias")):
        put("at_" + name, every, padded(t[key]))
    heads = np.kron(np.eye(NH), np.ones((P // NH, 1)))
    put("heads", every, heads)
    put("heads_q", every, -HD ** -0.5 * heads)
    put("at_wv", lo, t["Wv"].T)
    put("at_wo", lo, np.tile(t["Wo"].T, (1, 2)))
    put("at_bv", lo, col(t["bv"]))
    put("at_bo", every, col(t["bo"], 2))
    dist = np.clip(np.arange(2 * S - 1) - (S - 1), -MAXREL, MAXREL) + MAXREL
    div = np.exp(np.arange(0, D, 2, dtype=f) * f(-math.log(10000.0) / D)).astype(f)
    ang = dist.astype(f)[:, None] * div
    put("enc", lo, np.stack([np.sin(ang), np.cos(ang)], axis=-1).reshape(-1, D).T)

    g = {k[len("L1_ffn_"):]: v for k, v in a.items() if k.startswith("L1_ffn_")}
    put("e1_b1", every, g["b1"].T)
    put("e1_w2", every, g["W2"].transpose(1, 0, 2))
    put("e1_b2", slice(0, NE), g["b2"])
    put("e1_wg", lo, g["Wg"])
    put("e1_bg", every, np.tile(g["bg"], (P, 1)))

    tokens = np.stack([a["x"], a["itok_BS_0_23"], a["itok_BS_0_11"], a["itok_BS_0_30"]]).reshape(4, NG, T)
    idx = np.zeros((NG, 32, T), np.int32)
    idx[:, :FD] = np.repeat(tokens.transpose(1, 0, 2), FD // 4, axis=1)
    sel = np.eye(P, 2 * NSTATE) + np.eye(P, 2 * NSTATE, -64) + np.eye(P, 2 * NSTATE, -96)
    return idx.reshape(P, T), part[0], part[1], part[2], part[3], sel


def kernel(**inputs):
    import ml_dtypes
    import concourse.bacc as bacc
    from concourse.bass_utils import run_bass_kernel_spmd

    a = {k: np.asarray(v) for k, v in inputs.items()}
    idx, w0, w1, w2, w3, sel = host_arrays(a)
    arrays = {"idx_dram": idx, "w0_dram": w0, "w1_dram": w1, "w2_dram": w2, "w3_dram": w3,
              "sel_dram": sel.astype(ml_dtypes.bfloat16)}
    nc = bacc.Bacc("TRN2", target_bir_lowering=False, num_devices=1)
    ins = [nc.dram_tensor(n, v.shape, mybir.dt.from_np(v.dtype), kind="ExternalInput").ap() for n, v in arrays.items()]
    out = nc.dram_tensor("out_dram", (NG, P, TILES, D), F32, kind="ExternalOutput").ap()
    tower(nc, *ins, out)
    r = run_bass_kernel_spmd(nc, [arrays], core_ids=[0])
    got = np.asarray(r.results[0]["out_dram"])
    return got.transpose(0, 2, 1, 3).reshape(NSEQ, S, D)
```
